# Optimizing a Trainium2 kernel written in Bass

```python
import numpy as np
import jax
import jax.numpy as jnp

def _softmax(x, axis=-1):
    return jax.nn.softmax(x, axis=axis)

def _gelu(x):
    return jax.nn.gelu(x, approximate=True)

def _silu(x):
    return jax.nn.silu(x)

def _sigmoid(x):
    return jax.nn.sigmoid(x)

def _layernorm(x, axis=-1, eps=1e-05):
    m = jnp.mean(x, axis=axis, keepdims=True)
    v = jnp.var(x, axis=axis, keepdims=True)
    return (x - m) / jnp.sqrt(v + eps)

def _scatter_add(tgt, idx, src, axis=0):
    return tgt.at[idx].add(src)

def _segment_sum(src, seg, n):
    return jax.ops.segment_sum(src, seg, n)
kernel_name = 'mk_early_fusion_d2_tok_img768_r4_771a0e'

def setup_inputs(seed: int=0):
    np.random.seed(seed)
    _w = jnp.asarray

    def _rec_inputs():
        import jax
        import jax.numpy as jnp
        _rk = jax.random.key(seed)
        x = -0.000356955 + 1 * jax.random.normal(jax.random.fold_in(_rk, 1), (16, 3, 128, 128), jnp.float32)
        txt = 5.00692e-11 + 0.999999 * jax.random.normal(jax.random.fold_in(_rk, 2), (16, 77, 192), jnp.float32)
        return (x, txt)
    x, txt = _rec_inputs()

    def _L0_tok_setup():
        import jax, jax.numpy as jnp
        import numpy as np
        PATCH = 16
        EPS = 1e-06

        def _layernorm(x, gamma, beta, eps=EPS):
            mu = jnp.mean(x, axis=-1, keepdims=True)
            var = jnp.var(x, axis=-1, keepdims=True)
            return (x - mu) * jax.lax.rsqrt(var + eps) * gamma + beta
        key = jax.random.key(seed)
        k_x, k_w = jax.random.split(key)
        B, C, H, W = (128, 3, 224, 224)
        patch_dim = C * PATCH * PATCH
        embed_dim = 192
        x = jax.random.normal(k_x, (B, C, H, W), dtype=jnp.float32)
        W_proj = jax.random.normal(k_w, (patch_dim, embed_dim), dtype=jnp.float32) * (1.0 / np.sqrt(patch_dim))
        ln1_g = jnp.ones((patch_dim,), jnp.float32)
        ln1_b = jnp.zeros((patch_dim,), jnp.float32)
        ln2_g = jnp.ones((embed_dim,), jnp.float32)
        ln2_b = jnp.zeros((embed_dim,), jnp.float32)
        return {'x': x, 'W_proj': W_proj, 'ln1_g': ln1_g, 'ln1_b': ln1_b, 'ln2_g': ln2_g, 'ln2_b': ln2_b}
    _L0_tok_all = _L0_tok_setup()
    _L0_tok_in = {k: v for k, v in _L0_tok_all.items() if k in ('W_proj', 'ln1_g', 'ln1_b', 'ln2_g', 'ln2_b')}
    del _L0_tok_all

    def _L0_attn_setup():
        import jax, jax.numpy as jnp
        import numpy as np
        DIM = 192
        GP_NUM = 49
        key = jax.random.key(seed)
        ks = jax.random.split(key, 7)
        b, n, d = (16, 256, DIM)
        s = d ** (-0.5)
        x = jax.random.normal(ks[0], (b, n, d), dtype=jnp.float32)
        W_qkv = jax.random.normal(ks[1], (d, 3 * d), dtype=jnp.float32) * s
        b_qkv = jnp.zeros((3 * d,), dtype=jnp.float32)
        W_proj = jax.random.normal(ks[2], (d, d), dtype=jnp.float32) * s
        b_proj = jnp.zeros((d,), dtype=jnp.float32)
        W_gp = jax.random.normal(ks[3], (d, GP_NUM), dtype=jnp.float32) * s
        alpha = jnp.zeros((1,), dtype=jnp.float32)
        return {'x': x, 'W_qkv': W_qkv, 'b_qkv': b_qkv, 'W_proj': W_proj, 'b_proj': b_proj, 'W_gp': W_gp, 'alpha': alpha}
    _L0_attn_all = _L0_attn_setup()
    _L0_attn_in = {k: v for k, v in _L0_attn_all.items() if k in ('W_qkv', 'b_qkv', 'W_proj', 'b_proj', 'W_gp', 'alpha')}
    del _L0_attn_all

    def _L0_ffn_setup():
        import jax, jax.numpy as jnp
        import numpy as np
        H = 12
        ALPHA = (1, 2, 3)
        DEPTH = 5
        BLOCK_DEPTH = 3
        TOTAL_DEPTH_M1 = 14 - 1
        SMALL_ACTIVE = BLOCK_DEPTH <= DEPTH <= TOTAL_DEPTH_M1 - BLOCK_DEPTH

        def _ln(x, g, b, eps=1e-05):
            m = jnp.mean(x, axis=-1, keepdims=True)
            v = jnp.mean((x - m) ** 2, axis=-1, keepdims=True)
            return (x - m) * jax.lax.rsqrt(v + eps) * g + b

        def _attn_branch(xp, w_qkv, w_proj, b_proj, keep_heads, keep_ch):
            B2, N, C = xp.shape
            hd = C // H
            scale = hd ** (-0.5)
            qkv = (xp @ w_qkv).reshape(B2, N, 3, H, hd).transpose(2, 0, 3, 1, 4)
            hmask = (jnp.arange(H) < keep_heads).astype(xp.dtype)[None, :, None, None]
            q, k, v = (qkv[0] * hmask, qkv[1] * hmask, qkv[2] * hmask)
            a = jax.nn.softmax(jnp.einsum('bhnd,bhmd->bhnm', q, k) * scale, axis=-1)
            o = jnp.einsum('bhnm,bhmd->bhnd', a, v).transpose(0, 2, 1, 3).reshape(B2, N, C)
            o = o @ w_proj + b_proj
            cmask = (jnp.arange(C) < keep_ch).astype(xp.dtype)
            return o * cmask

        def _mlp_branch(xp, w1, b1, w2, b2, keep_ch):
            C = xp.shape[-1]
            cmask = (jnp.arange(C) < keep_ch).astype(xp.dtype)
            h = jax.nn.gelu(xp * cmask @ w1 + b1, approximate=False)
            return (h @ w2 + b2) * cmask
        key = jax.random.key(seed)
        ks = jax.random.split(key, 8)
        B, N, C = (64, 257, 192)
        HID = 4 * C

        def w(k, shape):
            return jax.random.normal(k, shape, jnp.float32) * 0.02
        return {'x': jax.random.normal(ks[0], (B, N, C), jnp.float32), 'gumbel_weights': jax.random.uniform(ks[1], (3,), jnp.float32), 'n1l_g': jnp.ones((C,), jnp.float32), 'n1l_b': jnp.zeros((C,), jnp.float32), 'n1s_g': jnp.ones((C,), jnp.float32), 'n1s_b': jnp.zeros((C,), jnp.float32), 'w_qkv': w(ks[2], (C, 3 * C)), 'w_proj': w(ks[3], (C, C)), 'b_proj': jnp.zeros((C,), jnp.float32), 'n2l_g': jnp.ones((C,), jnp.float32), 'n2l_b': jnp.zeros((C,), jnp.float32), 'n2s_g': jnp.ones((C,), jnp.float32), 'n2s_b': jnp.zeros((C,), jnp.float32), 'w_fc1': w(ks[4], (C, HID)), 'b_fc1': jnp.zeros((HID,), jnp.float32), 'w_fc2': w(ks[5], (HID, C)), 'b_fc2': jnp.zeros((C,), jnp.float32)}
    _L0_ffn_all = _L0_ffn_setup()
    _L0_ffn_in = {k: v for k, v in _L0_ffn_all.items() if k in ('gumbel_weights', 'n1l_g', 'n1l_b', 'n1s_g', 'n1s_b', 'w_qkv', 'w_proj', 'b_proj', 'n2l_g', 'n2l_b', 'n2s_g', 'n2s_b', 'w_fc1', 'b_fc1', 'w_fc2', 'b_fc2')}
    del _L0_ffn_all

    def _L1_attn_setup():
        import jax, jax.numpy as jnp
        import numpy as np
        B, S, H = (2, 512, 192)
        E, NH, WIN = (4, 12, 64)
        HD = H // NH
        NEG = -1e+30

        def _sliding_mask(seq_len, window):
            i = jnp.arange(seq_len)
            d = i[:, None] - i[None, :]
            return (d >= 0) & (d < window)
        key = jax.random.key(seed)
        ks = jax.random.split(key, 7)
        s = 0.02
        return {'x': jax.random.normal(ks[0], (B, S, H), jnp.float32), 'wq': jax.random.normal(ks[1], (E, H, H), jnp.float32) * s, 'wk': jax.random.normal(ks[2], (E, H, H), jnp.float32) * s, 'wv': jax.random.normal(ks[3], (E, H, H), jnp.float32) * s, 'wo': jax.random.normal(ks[4], (E, H, H), jnp.float32) * s, 'w_gate': jax.random.normal(ks[5], (H, E * H), jnp.float32) * s, 'w_up': jax.random.normal(ks[6], (E, H, H), jnp.float32).reshape(H, E * H) * 0 + jax.random.normal(jax.random.fold_in(key, 7), (H, E * H), jnp.float32) * s}
    _L1_attn_all = _L1_attn_setup()
    _L1_attn_in = {k: v for k, v in _L1_attn_all.items() if k in ('wq', 'wk', 'wv', 'wo', 'w_gate', 'w_up')}
    del _L1_attn_all

    def _L1_ffn_setup():
        import jax, jax.numpy as jnp
        import numpy as np
        B, S, D_IN, D_HID, D_OUT = (32, 128, 192, 768, 192)
        key = jax.random.key(seed)
        k1, k2, k3, k4 = jax.random.split(key, 4)
        init_k = float(np.sqrt(1.0 / D_IN))
        init_k2 = float(np.sqrt(1.0 / D_HID))
        x = jax.random.normal(k1, (B, S, D_IN), dtype=jnp.float32)
        in_weight = jax.random.uniform(k2, (D_HID, D_IN), dtype=jnp.float32, minval=-init_k, maxval=init_k)
        in_bias = jax.random.uniform(k3, (D_HID,), dtype=jnp.float32, minval=-init_k, maxval=init_k)
        out_weight = jax.random.uniform(k4, (D_HID, D_OUT), dtype=jnp.float32, minval=-init_k2, maxval=init_k2)
        return {'x': x, 'in_weight': in_weight, 'in_bias': in_bias, 'out_weight': out_weight}
    _L1_ffn_all = _L1_ffn_setup()
    _L1_ffn_in = {k: v for k, v in _L1_ffn_all.items() if k in ('in_weight', 'in_bias', 'out_weight')}
    del _L1_ffn_all
    return {'x': x, 'txt': txt, 'L0_tok_W_proj': _L0_tok_in['W_proj'], 'L0_tok_ln1_g': _L0_tok_in['ln1_g'], 'L0_tok_ln1_b': _L0_tok_in['ln1_b'], 'L0_tok_ln2_g': _L0_tok_in['ln2_g'], 'L0_tok_ln2_b': _L0_tok_in['ln2_b'], 'L0_attn_W_qkv': _L0_attn_in['W_qkv'], 'L0_attn_b_qkv': _L0_attn_in['b_qkv'], 'L0_attn_W_proj': _L0_attn_in['W_proj'], 'L0_attn_b_proj': _L0_attn_in['b_proj'], 'L0_attn_W_gp': _L0_attn_in['W_gp'], 'L0_attn_alpha': _L0_attn_in['alpha'], 'L0_ffn_gumbel_weights': _L0_ffn_in['gumbel_weights'], 'L0_ffn_n1l_g': _L0_ffn_in['n1l_g'], 'L0_ffn_n1l_b': _L0_ffn_in['n1l_b'], 'L0_ffn_n1s_g': _L0_ffn_in['n1s_g'], 'L0_ffn_n1s_b': _L0_ffn_in['n1s_b'], 'L0_ffn_w_qkv': _L0_ffn_in['w_qkv'], 'L0_ffn_w_proj': _L0_ffn_in['w_proj'], 'L0_ffn_b_proj': _L0_ffn_in['b_proj'], 'L0_ffn_n2l_g': _L0_ffn_in['n2l_g'], 'L0_ffn_n2l_b': _L0_ffn_in['n2l_b'], 'L0_ffn_n2s_g': _L0_ffn_in['n2s_g'], 'L0_ffn_n2s_b': _L0_ffn_in['n2s_b'], 'L0_ffn_w_fc1': _L0_ffn_in['w_fc1'], 'L0_ffn_b_fc1': _L0_ffn_in['b_fc1'], 'L0_ffn_w_fc2': _L0_ffn_in['w_fc2'], 'L0_ffn_b_fc2': _L0_ffn_in['b_fc2'], 'L1_attn_wq': _L1_attn_in['wq'], 'L1_attn_wk': _L1_attn_in['wk'], 'L1_attn_wv': _L1_attn_in['wv'], 'L1_attn_wo': _L1_attn_in['wo'], 'L1_attn_w_gate': _L1_attn_in['w_gate'], 'L1_attn_w_up': _L1_attn_in['w_up'], 'L1_ffn_in_weight': _L1_ffn_in['in_weight'], 'L1_ffn_in_bias': _L1_ffn_in['in_bias'], 'L1_ffn_out_weight': _L1_ffn_in['out_weight']}

def reference(x, txt, L0_tok_W_proj, L0_tok_ln1_g, L0_tok_ln1_b, L0_tok_ln2_g, L0_tok_ln2_b, L0_attn_W_qkv, L0_attn_b_qkv, L0_attn_W_proj, L0_attn_b_proj, L0_attn_W_gp, L0_attn_alpha, L0_ffn_gumbel_weights, L0_ffn_n1l_g, L0_ffn_n1l_b, L0_ffn_n1s_g, L0_ffn_n1s_b, L0_ffn_w_qkv, L0_ffn_w_proj, L0_ffn_b_proj, L0_ffn_n2l_g, L0_ffn_n2l_b, L0_ffn_n2s_g, L0_ffn_n2s_b, L0_ffn_w_fc1, L0_ffn_b_fc1, L0_ffn_w_fc2, L0_ffn_b_fc2, L1_attn_wq, L1_attn_wk, L1_attn_wv, L1_attn_wo, L1_attn_w_gate, L1_attn_w_up, L1_ffn_in_weight, L1_ffn_in_bias, L1_ffn_out_weight):
    import jax
    import jax.numpy as jnp

    def _L0_tok_ref(x, W_proj, ln1_g, ln1_b, ln2_g, ln2_b):
        import jax, jax.numpy as jnp
        import numpy as np
        PATCH = 16
        EPS = 1e-06

        def _layernorm(x, gamma, beta, eps=EPS):
            mu = jnp.mean(x, axis=-1, keepdims=True)
            var = jnp.var(x, axis=-1, keepdims=True)
            return (x - mu) * jax.lax.rsqrt(var + eps) * gamma + beta
        B, C, H, W = x.shape
        h, w = (H // PATCH, W // PATCH)
        p = x.reshape(B, C, h, PATCH, w, PATCH)
        p = p.transpose(0, 2, 4, 3, 5, 1)
        p = p.reshape(B, h * w, PATCH * PATCH * C)
        p = _layernorm(p, ln1_g, ln1_b)
        y = jnp.einsum('bnd,de->bne', p, W_proj)
        return _layernorm(y, ln2_g, ln2_b)

    def _L0_attn_ref(x, W_qkv, b_qkv, W_proj, b_proj, W_gp, alpha):
        import jax, jax.numpy as jnp
        import numpy as np
        DIM = 192
        GP_NUM = 49
        d = x.shape[-1]
        scale = d ** (-0.5)
        qkv = x @ W_qkv + b_qkv
        q, k, v = jnp.split(qkv, 3, axis=-1)
        scores = jnp.einsum('bnd,bmd->bnm', q, k) * scale
        attn = jax.nn.softmax(scores, axis=-1)
        gw = jax.nn.softmax(q @ W_gp, axis=-1)
        group = jnp.einsum('bng,bmg->bnm', gw, gw)
        a = jax.nn.sigmoid(alpha)
        weights = attn * (a + (1.0 - a) * group)
        out = jnp.einsum('bnm,bmd->bnd', weights, v)
        return out @ W_proj + b_proj

    def _L0_ffn_ref(x, gumbel_weights, n1l_g, n1l_b, n1s_g, n1s_b, w_qkv, w_proj, b_proj, n2l_g, n2l_b, n2s_g, n2s_b, w_fc1, b_fc1, w_fc2, b_fc2):
        import jax, jax.numpy as jnp
        import numpy as np
        H = 12
        ALPHA = (1, 2, 3)
        DEPTH = 5
        BLOCK_DEPTH = 3
        TOTAL_DEPTH_M1 = 14 - 1
        SMALL_ACTIVE = BLOCK_DEPTH <= DEPTH <= TOTAL_DEPTH_M1 - BLOCK_DEPTH

        def _ln(x, g, b, eps=1e-05):
            m = jnp.mean(x, axis=-1, keepdims=True)
            v = jnp.mean((x - m) ** 2, axis=-1, keepdims=True)
            return (x - m) * jax.lax.rsqrt(v + eps) * g + b

        def _attn_branch(xp, w_qkv, w_proj, b_proj, keep_heads, keep_ch):
            B2, N, C = xp.shape
            hd = C // H
            scale = hd ** (-0.5)
            qkv = (xp @ w_qkv).reshape(B2, N, 3, H, hd).transpose(2, 0, 3, 1, 4)
            hmask = (jnp.arange(H) < keep_heads).astype(xp.dtype)[None, :, None, None]
            q, k, v = (qkv[0] * hmask, qkv[1] * hmask, qkv[2] * hmask)
            a = jax.nn.softmax(jnp.einsum('bhnd,bhmd->bhnm', q, k) * scale, axis=-1)
            o = jnp.einsum('bhnm,bhmd->bhnd', a, v).transpose(0, 2, 1, 3).reshape(B2, N, C)
            o = o @ w_proj + b_proj
            cmask = (jnp.arange(C) < keep_ch).astype(xp.dtype)
            return o * cmask

        def _mlp_branch(xp, w1, b1, w2, b2, keep_ch):
            C = xp.shape[-1]
            cmask = (jnp.arange(C) < keep_ch).astype(xp.dtype)
            h = jax.nn.gelu(xp * cmask @ w1 + b1, approximate=False)
            return (h @ w2 + b2) * cmask
        B, N, C = x.shape
        B2 = B // 2
        nl = _ln(x[:B2], n1l_g, n1l_b)
        ns = _ln(x[B2:], n1s_g, n1s_b)
        a_large = _attn_branch(nl, w_qkv, w_proj, b_proj, H, C)
        if SMALL_ACTIVE:
            a_small = sum((gumbel_weights[i] * _attn_branch(ns, w_qkv, w_proj, b_proj, H // ALPHA[i], C // ALPHA[i]) for i in range(3)))
            attn_out = jnp.concatenate([a_large, a_small], axis=0)
        else:
            attn_out = jnp.concatenate([a_large, a_large], axis=0)
        x = x + attn_out
        nl2 = _ln(x[:B2], n2l_g, n2l_b)
        ns2 = _ln(x[B2:], n2s_g, n2s_b)
        m_large = _mlp_branch(nl2, w_fc1, b_fc1, w_fc2, b_fc2, C)
        if SMALL_ACTIVE:
            m_small = sum((gumbel_weights[i] * _mlp_branch(ns2, w_fc1, b_fc1, w_fc2, b_fc2, C // ALPHA[i]) for i in range(3)))
            mlp_out = jnp.concatenate([m_large, m_small], axis=0)
        else:
            mlp_out = jnp.concatenate([m_large, m_large], axis=0)
        return x + mlp_out

    def _L1_attn_ref(x, wq, wk, wv, wo, w_gate, w_up):
        import jax, jax.numpy as jnp
        import numpy as np
        B, S, H = (2, 512, 192)
        E, NH, WIN = (4, 12, 64)
        HD = H // NH
        NEG = -1e+30

        def _sliding_mask(seq_len, window):
            i = jnp.arange(seq_len)
            d = i[:, None] - i[None, :]
            return (d >= 0) & (d < window)
        b, s, h = x.shape
        nh, hd = (NH, h // NH)
        mask = _sliding_mask(s, WIN)
        scale = jnp.float32(1.0 / np.sqrt(hd))
        outs = []
        for e in range(wq.shape[0]):
            q = (x @ wq[e].T).reshape(b, s, nh, hd).transpose(0, 2, 1, 3)
            k = (x @ wk[e].T).reshape(b, s, nh, hd).transpose(0, 2, 1, 3)
            v = (x @ wv[e].T).reshape(b, s, nh, hd).transpose(0, 2, 1, 3)
            scores = jnp.einsum('bhqd,bhkd->bhqk', q, k) * scale
            scores = jnp.where(mask, scores, NEG)
            attn = jax.nn.softmax(scores, axis=-1)
            o = jnp.einsum('bhqk,bhkd->bhqd', attn, v)
            o = o.transpose(0, 2, 1, 3).reshape(b, s, h)
            outs.append(o @ wo[e].T)
        fused = jnp.concatenate(outs, axis=-1)
        gate = jax.nn.silu(fused @ w_gate.T)
        value = fused @ w_up.T
        return gate * value

    def _L1_ffn_ref(x, in_weight, in_bias, out_weight):
        import jax, jax.numpy as jnp
        import numpy as np
        B, S, D_IN, D_HID, D_OUT = (32, 128, 192, 768, 192)
        lead = x.shape[:-1]
        xt = x.reshape(-1, in_weight.shape[1])
        h = jax.nn.gelu(jnp.einsum('td,hd->th', xt, in_weight) + in_bias, approximate=False)
        out = jnp.einsum('th,ho->to', h, out_weight)
        return out.reshape(*lead, out_weight.shape[1])
    h = _L0_tok_ref(x, L0_tok_W_proj, L0_tok_ln1_g, L0_tok_ln1_b, L0_tok_ln2_g, L0_tok_ln2_b)
    h = jnp.concatenate([h, txt], axis=1)
    h = h + _L0_attn_ref(_layernorm(h, axis=-1), L0_attn_W_qkv, L0_attn_b_qkv, L0_attn_W_proj, L0_attn_b_proj, L0_attn_W_gp, L0_attn_alpha)
    h = h + _L0_ffn_ref(_layernorm(h, axis=-1), L0_ffn_gumbel_weights, L0_ffn_n1l_g, L0_ffn_n1l_b, L0_ffn_n1s_g, L0_ffn_n1s_b, L0_ffn_w_qkv, L0_ffn_w_proj, L0_ffn_b_proj, L0_ffn_n2l_g, L0_ffn_n2l_b, L0_ffn_n2s_g, L0_ffn_n2s_b, L0_ffn_w_fc1, L0_ffn_b_fc1, L0_ffn_w_fc2, L0_ffn_b_fc2)
    h = h + _L1_attn_ref(_layernorm(h, axis=-1), L1_attn_wq, L1_attn_wk, L1_attn_wv, L1_attn_wo, L1_attn_w_gate, L1_attn_w_up)
    h = h + _L1_ffn_ref(_layernorm(h, axis=-1), L1_ffn_in_weight, L1_ffn_in_bias, L1_ffn_out_weight)
    return h

_drawn_inputs = setup_inputs


def setup_inputs(seed=0):
    import zlib

    import numpy as np

    out = dict(_drawn_inputs(seed))
    spreads = {'L0_tok_ln1_g': (1.0, 0.2),
     'L0_tok_ln1_b': (0.0, 0.1),
     'L0_tok_ln2_g': (1.0, 0.2),
     'L0_tok_ln2_b': (0.0, 0.1),
     'L0_attn_b_qkv': (0.0, 0.1),
     'L0_attn_b_proj': (0.0, 0.1),
     'L0_ffn_n1l_g': (1.0, 0.6),
     'L0_ffn_n1l_b': (0.0, 0.8),
     'L0_ffn_n1s_g': (1.0, 0.6),
     'L0_ffn_n1s_b': (0.0, 0.8),
     'L0_ffn_b_proj': (0.0, 0.1),
     'L0_ffn_n2l_g': (1.0, 0.6),
     'L0_ffn_n2l_b': (0.0, 2.0),
     'L0_ffn_n2s_g': (1.0, 0.6),
     'L0_ffn_n2s_b': (0.0, 2.0),
     'L0_ffn_b_fc1': (0.0, 0.767),
     'L0_ffn_b_fc2': (0.0, 0.1)}
    factors = {'L0_attn_W_gp': 8.0,
     'L0_ffn_gumbel_weights': 6.356,
     'L0_ffn_w_qkv': 8.0,
     'L0_ffn_w_proj': 8.0,
     'L1_attn_wq': 8.0,
     'L1_attn_wk': 8.0,
     'L1_attn_wv': 8.0,
     'L1_attn_wo': 8.0,
     'L1_attn_w_gate': 8.0,
     'L1_attn_w_up': 8.0,
     'L1_ffn_in_bias': 57.456,
     'L1_ffn_in_weight': 8.0,
     'L1_ffn_out_weight': 8.0}
    for name, (base, spread) in spreads.items():
        noise = np.random.default_rng([zlib.crc32(name.encode()), seed]).standard_normal(out[name].shape)
        drawn = base * np.exp(spread * noise) if base else spread * noise
        out[name] = jnp.asarray(drawn.astype(out[name].dtype))
    for name, factor in factors.items():
        out[name] = (out[name] * factor).astype(out[name].dtype)
    return out
```

```python
from contextlib import ExitStack

import concourse.bass as bass
from concourse import mybir

F32 = mybir.dt.float32
BF16 = mybir.dt.bfloat16
ALU = mybir.AluOpType
ACT = mybir.ActivationFunctionType
AX = mybir.AxisListType

P = 128
C = 192
C1 = C - P
B, SEQ, NPATCH = 16, 141, 64
SLOT = 144
NTOK = B * SLOT
TILES = NTOK // P
HALF = TILES // 2
PD = 768
PK = PD // P
PT_TILES = B * NPATCH // P
HID = 768
HM = HID // P
NH, HD, HP = 12, 16, 32
HB = NH // 4
EXPERTS = 4
WIN = 64
GP = 49
CH = ((0, P), (1, C1))
QA_SEGS = ((0, 71), (71, 70))
NEG = -1e30


def ds(a, n):
    return bass.ds(a, n)


def fusion_kernel(nc: bass.Bass, d: dict, out: bass.AP, stop: int = 99):
    hd = nc.dram_tensor("h_staging", (NTOK, C), F32, kind="Internal").ap()
    with ExitStack() as ctx:
        def sb(name, shape, dt=F32):
            return ctx.enter_context(nc.sbuf_tensor(name, shape, dt))

        def sem(name):
            return ctx.enter_context(nc.semaphore(name))

        bank = [ctx.enter_context(nc.psum_tensor(f"bank{i}", [P, 512], F32)) for i in range(8)]

        H = sb("H", [P, TILES, C])
        XN = sb("XN", [P, TILES, C])
        XT = sb("XT", [P, 2, NTOK])
        ident = sb("ident", [P, P])
        identb = sb("identb", [P, P], BF16)
        stats = sb("stats", [P, TILES, 6])
        mean = sb("mean", [P, TILES])
        rstd = sb("rstd", [P, TILES])
        rstd2 = sb("rstd2", [P, TILES])
        tmpa = sb("tmpa", [P, TILES])
        tmpb = sb("tmpb", [P, TILES])
        tmpc = sb("tmpc", [P, TILES])
        nhalf = sb("nhalf", [P, TILES])
        xn = [sb(f"xn{i}", [P, C]) for i in range(2)]
        back = [sb(f"back{i}", [P, 2, P]) for i in range(2)]
        vecs = sb("vecs", [P, 64])
        rows = sb("rows", [P, 5, C])
        LN2G, LN2B, BV0, B2L, B2S = range(5)
        V_LN1G, V_LN1B, V_BQ, V_BK, V_BP0, V_N1L, V_N1S, V_N2L, V_N2S, V_BPL, V_B1, V_FB, V_GUM, V_ALPHA, V_KONE, V_HEAD = \
            0, 6, 12, 14, 16, 18, 22, 26, 30, 34, 36, 42, 48, 51, 52, 53
        gs = sb("gs", [P, 3])
        bps = sb("bps", [P, 2])
        alo = sb("alo", [P, 4])

        XB = sb("XB", [P, 2, SEQ])
        AT = sb("AT", [P, 2, NTOK])

        ph_n = [0]

        open_sems = []

        def phase_sem(names):
            ph_n[0] += 1
            got = [nc.alloc_semaphore(name=f"{x}_{ph_n[0]}") for x in names]
            open_sems.extend(got)
            return got

        def end_phase():
            nc.clear_and_free_semaphores(list(open_sems))
            open_sems.clear()
            nc.all_engine_barrier()

        s_vec, s_const, s_zero, s_vstep = (sem(x) for x in ("vectors_loaded", "constants_ready", "zeroed", "vector_step"))
        with nc.Block() as block:
            @block.sync
            def _(sp):
                sp.dma_start(vecs[:, :], d["vecs"]).then_inc(s_vec, 16)
                sp.dma_start(rows[:, :, :], d["rows"]).then_inc(s_vec, 16)

            @block.gpsimd
            def _(pool):
                nc.gpsimd.memset(ident[:, :], 0.0).then_inc(s_zero, 1)
                pool.wait_ge(s_zero, 1)
                nc.gpsimd.affine_select(out=ident[:, :], in_=ident[:, :], compare_op=ALU.not_equal, fill=1.0,
                                        base=0, pattern=[[-1, P]], channel_multiplier=1).then_inc(s_const, 1)

            @block.vector
            def _(dve):
                nc.vector.memset(XT[C1:P, 1, :], 0.0)
                nc.vector.memset(nhalf[:, :], -0.5)
                dve.wait_ge(s_const, 1)
                nc.vector.tensor_copy(identb[:, :], ident[:, :])
                dve.wait_ge(s_vec, 32)
                nc.vector.tensor_copy(gs[:, 0:1], vecs[:, V_GUM:V_GUM + 1]).then_inc(s_vstep, 1)
                nc.vector.tensor_tensor(gs[:, 1:2], vecs[:, V_GUM:V_GUM + 1], vecs[:, V_GUM + 1:V_GUM + 2],
                                        ALU.add).then_inc(s_vstep, 1)
                dve.wait_ge(s_vstep, 2)
                nc.vector.tensor_tensor(gs[:, 2:3], gs[:, 1:2], vecs[:, V_GUM + 2:V_GUM + 3],
                                        ALU.add).then_inc(s_vstep, 1)
                dve.wait_ge(s_vstep, 3)
                for a, b, k in ((0, 64, 2), (64, 96, 1), (96, 128, 0)):
                    nc.vector.tensor_tensor(bps[a:b, 0:1], vecs[a:b, V_BPL:V_BPL + 1], gs[a:b, k:k + 1], ALU.mult)
                nc.vector.tensor_tensor(bps[0:C1, 1:2], vecs[0:C1, V_BPL + 1:V_BPL + 2], gs[0:C1, 0:1], ALU.mult)
                for a, b, k in ((0, 64, 2), (64, 96, 1), (96, C, 0)):
                    nc.vector.tensor_scalar(rows[:, B2S, a:b], rows[:, B2L, a:b], gs[:, k:k + 1], None, ALU.mult)

            @block.scalar
            def _(act):
                act.wait_ge(s_vec, 32)
                nc.scalar.activation(alo[:, 0:1], vecs[:, V_ALPHA:V_ALPHA + 1], ACT.Exp, scale=-1.0)

        with nc.Block() as block:
            s_a, = phase_sem(["sigmoid_step"])

            @block.vector
            def _(dve):
                nc.vector.tensor_scalar(alo[:, 1:2], alo[:, 0:1], 1.0, None, ALU.add).then_inc(s_a, 1)
                dve.wait_ge(s_a, 1)
                nc.vector.reciprocal(alo[:, 2:3], alo[:, 1:2]).then_inc(s_a, 1)
                dve.wait_ge(s_a, 2)
                nc.vector.tensor_scalar(alo[:, 3:4], alo[:, 2:3], -1.0, 1.0, ALU.mult, ALU.add)

        with ExitStack() as ph:
            def psb(name, shape, dt=F32):
                return ph.enter_context(nc.sbuf_tensor(name, shape, dt))

            xp = psb("xp", [P, PT_TILES, PD])
            tokw = psb("tokw", [P, PK, C])
            tokws = psb("tokws", [P, PK, C])
            bnp = psb("bnp", [P, PT_TILES, 12])
            mvp = psb("mvp", [P, PT_TILES, 2])
            rp = psb("rp", [P, PT_TILES])
            ve = psb("ve", [P, PT_TILES])
            xpt = [psb(f"xpt{i}", [P, PK, P]) for i in range(2)]
            xpn = [psb(f"xpn{i}", [P, PD]) for i in range(2)]
            brow = psb("brow", [1, C])
            one1 = psb("one1", [1, P])
            Y = psb("Y", [P, PT_TILES, C])
            (s_w, s_p, s_st, s_bn, s_mv, s_rs, s_fold, s_fm, s_bd, s_bc, s_nrm, s_tr, s_ev, s_mm, s_y, s_ybn, s_yr,
             s_yn, s_yg, s_yo, s_hd, s_hl, s_one) = phase_sem([
                "tok_weights", "patches_loaded", "staged", "patch_stats", "patch_meanvar", "patch_rstd", "tok_folded",
                "tok_scaled", "bias_product", "bias_row", "patch_normed", "patch_transposed", "patch_evacuated",
                "embedded", "embed_copied", "embed_stats", "embed_rstd", "embed_normed", "embed_scaled", "embed_done",
                "embed_stored", "h_loaded", "tok_ones"])
            with nc.Block() as block:
                @block.sync
                def _(sp):
                    sp.dma_start(hd, d["h0"]).then_inc(s_st, 16)
                    sp.dma_start(xp[:, :, :], d["patches"].rearrange("(t p) n -> p t n", p=P)).then_inc(s_p, 16)
                    sp.dma_start(tokw[:, :, :], d["tok_w"].rearrange("(k p) n -> p k n", p=P)).then_inc(s_w, 16)
                    sp.wait_ge(s_st, 16)
                    with sp.Fori(0, PT_TILES) as t:
                        sp.wait_ge(s_yo, t + 1)
                        for k in range(2):
                            sp.dma_start(hd[ds(t * (2 * SLOT) + k * SLOT, NPATCH), :],
                                         Y[k * NPATCH:(k + 1) * NPATCH, ds(t, 1), :].rearrange("p t n -> p (t n)")
                                         ).then_inc(s_hd, 16)
                    sp.wait_ge(s_hd, 32 * PT_TILES)
                    sp.dma_start(H[:, :, :], hd.rearrange("(t p) n -> p t n", p=P)).then_inc(s_hl, 16)
                    sp.wait_ge(s_hl, 16)

                @block.vector
                def _(dve):
                    nc.vector.memset(one1[:, :], 1.0).then_inc(s_one, 1)
                    dve.wait_ge(s_p, 16)
                    with dve.Fori(0, PT_TILES) as t:
                        for k in range(2):
                            nc.vector.bn_stats(bnp[:, ds(t, 1), 6 * k:6 * k + 6],
                                               xp[:, ds(t, 1), k * 384:(k + 1) * 384]).then_inc(s_bn, 1)
                    dve.wait_ge(s_bn, 2 * PT_TILES)
                    for t in range(PT_TILES):
                        nc.vector.bn_aggr(mvp[:, t, :], bnp[:, t, :]).then_inc(s_mv, 1)
                    dve.wait_ge(s_mv, PT_TILES)
                    nc.vector.tensor_scalar(ve[:, :], mvp[:, :, 1], 1e-6, None, ALU.add).then_inc(s_mv, 1)
                    dve.wait_ge(s_w, 16)
                    for k in range(PK):
                        nc.vector.tensor_scalar(tokws[:, k, :], tokw[:, k, :], vecs[:, V_LN1G + k:V_LN1G + k + 1],
                                                None, ALU.mult).then_inc(s_fm, 1)
                    dve.wait_ge(s_rs, 1)
                    with dve.Fori(0, PT_TILES // 2) as t2:
                        t = t2 * 2
                        for k in range(2):
                            dve.wait_ge(s_ev, 2 * t + 2 * (k + 1))
                            nc.vector.tensor_scalar(xpn[k][:, :], xp[:, ds(t + k, 1), :].rearrange("p t n -> p (t n)"),
                                                    mvp[:, ds(t + k, 1), 0:1].rearrange("p t n -> p (t n)"),
                                                    rp[:, ds(t + k, 1)], ALU.subtract, ALU.mult).then_inc(s_nrm, 1)
                    dve.wait_ge(s_y, PT_TILES)
                    with dve.Fori(0, PT_TILES) as t:
                        nc.vector.bn_stats(bnp[:, ds(t, 1), 0:6], Y[:, ds(t, 1), :]).then_inc(s_ybn, 1)
                    dve.wait_ge(s_ybn, PT_TILES)
                    for t in range(PT_TILES):
                        nc.vector.bn_aggr(mvp[:, t, :], bnp[:, t, 0:6]).then_inc(s_ybn, 1)
                    dve.wait_ge(s_ybn, 2 * PT_TILES)
                    nc.vector.tensor_scalar(ve[:, :], mvp[:, :, 1], 1e-6, None, ALU.add).then_inc(s_ybn, 1)
                    dve.wait_ge(s_yr, 1)
                    with dve.Fori(0, PT_TILES) as t:
                        y = Y[:, ds(t, 1), :].rearrange("p t n -> p (t n)")
                        nc.vector.tensor_scalar(y, y, mvp[:, ds(t, 1), 0:1].rearrange("p t n -> p (t n)"),
                                                rp[:, ds(t, 1)], ALU.subtract, ALU.mult).then_inc(s_yn, 1)
                        dve.wait_ge(s_yn, t + 1)
                        nc.vector.tensor_tensor(y, y, rows[:, LN2G, :], ALU.mult).then_inc(s_yg, 1)
                        dve.wait_ge(s_yg, t + 1)
                        nc.vector.tensor_tensor(y, y, rows[:, LN2B, :], ALU.add).then_inc(s_yo, 1)

                @block.gpsimd
                def _(pool):
                    pool.wait_ge(s_mv, PT_TILES + 1)
                    nc.gpsimd.tensor_tensor(rp[:, :], ve[:, :], nhalf[:, 0:PT_TILES], ALU.pow).then_inc(s_rs, 1)
                    pool.wait_ge(s_ybn, 2 * PT_TILES + 1)
                    nc.gpsimd.tensor_tensor(rp[:, :], ve[:, :], nhalf[:, 0:PT_TILES], ALU.pow).then_inc(s_yr, 1)

                @block.tensor
                def _(pe):
                    pe.wait_ge(s_w, 16)
                    for k in range(PK):
                        mm = nc.tensor.matmul(bank[7][0:1, 0:C], vecs[:, V_LN1B + k:V_LN1B + k + 1], tokw[:, k, :],
                                              start=(k == 0), stop=(k == PK - 1))
                    mm.then_inc(s_bd, 1)
                    pe.wait_ge(s_fm, PK)
                    pe.wait_ge(s_bc, 1)
                    pe.wait_ge(s_one, 1)
                    with pe.Fori(0, PT_TILES // 2) as t2:
                        t = t2 * 2
                        for k in range(2):
                            pe.wait_ge(s_nrm, t + (k + 1))
                            for j in range(PK):
                                tr = nc.tensor.transpose(bank[2 * k + j // 4][:, (j % 4) * P:(j % 4 + 1) * P],
                                                         xpn[k][:, j * P:(j + 1) * P], ident[:, :])
                            tr.then_inc(s_tr, 1)
                            pe.wait_ge(s_ev, 2 * t + 2 * (k + 3))
                            for j in range(PK):
                                nc.tensor.matmul(bank[4 + k][:, 0:C], xpt[k][:, j, :], tokws[:, j, :],
                                                 start=(j == 0), stop=False)
                            nc.tensor.matmul(bank[4 + k][:, 0:C], one1[:, :], brow[:, :], start=False,
                                             stop=True).then_inc(s_mm, 1)

                @block.scalar
                def _(act):
                    act.sem_inc(s_ev, 4)
                    act.wait_ge(s_bd, 1)
                    nc.scalar.copy(brow[:, :], bank[7][0:1, 0:C]).then_inc(s_bc, 1)
                    with act.Fori(0, PT_TILES // 2) as t2:
                        t = t2 * 2
                        for k in range(2):
                            act.wait_ge(s_tr, t + (k + 1))
                            nc.scalar.copy(xpt[k][:, 0:4, :], bank[2 * k][:, 0:512]).then_inc(s_ev, 1)
                            nc.scalar.copy(xpt[k][:, 4:6, :], bank[2 * k + 1][:, 0:256]).then_inc(s_ev, 1)
                            act.wait_ge(s_mm, t + (k + 1))
                            nc.scalar.copy(Y[:, ds(t + k, 1), :], bank[4 + k][:, 0:C]).then_inc(s_y, 1)

        end_phase()
        if stop == 0:
            return H

        def residual_norm(src, add_from, save, twice, affine):
            (s_c, s_t, s_r, s_bn, s_x, s_pw, s_n, s_tr, s_e) = phase_sem([
                "back_copied", "back_transposed", "residual_added", "norm_stats", "norm_step", "norm_pow", "normed",
                "norm_transposed", "norm_evacuated"])
            with nc.Block() as block:
                @block.vector
                def _(dve):
                    if add_from:
                        with dve.Fori(0, TILES // 2) as i2:
                            i = i2 * 2
                            for k in range(2):
                                dve.wait_ge(s_t, i + (k + 1))
                                add_from[1](i + k, bank[k][:, 0:C], dve, s_r)
                                dve.wait_ge(s_r, i + (k + 3))
                                nc.vector.bn_stats(stats[:, ds(i + k, 1), :], src[:, ds(i + k, 1), :]
                                                   ).then_inc(s_bn, 1)
                    else:
                        with dve.Fori(0, TILES) as i:
                            nc.vector.bn_stats(stats[:, ds(i, 1), :], src[:, ds(i, 1), :]).then_inc(s_bn, 1)
                    dve.wait_ge(s_bn, TILES)
                    n = [0]

                    def step(ins):
                        n[0] += 1
                        ins.then_inc(s_x, 1)
                        dve.wait_ge(s_x, n[0])

                    step(nc.vector.tensor_tensor(tmpa[:, :], stats[:, :, 1], stats[:, :, 4], ALU.add))
                    step(nc.vector.tensor_scalar(mean[:, :], tmpa[:, :], 0.5, None, ALU.mult))
                    step(nc.vector.tensor_tensor(tmpa[:, :], stats[:, :, 1], stats[:, :, 4], ALU.subtract))
                    step(nc.vector.scalar_tensor_tensor(tmpb[:, :], tmpa[:, :], 0.25, tmpa[:, :], ALU.mult, ALU.mult))
                    step(nc.vector.tensor_tensor(tmpa[:, :], stats[:, :, 2], stats[:, :, 5], ALU.add))
                    step(nc.vector.scalar_tensor_tensor(tmpa[:, :], tmpa[:, :], 1.0 / C, tmpb[:, :], ALU.mult, ALU.add))
                    step(nc.vector.tensor_scalar(tmpc[:, :], tmpa[:, :], 1e-5, None, ALU.add))
                    dve.wait_ge(s_pw, 1)
                    if twice:
                        step(nc.vector.tensor_tensor(tmpb[:, :], tmpa[:, :], rstd[:, :], ALU.mult))
                        step(nc.vector.tensor_tensor(tmpb[:, :], tmpb[:, :], rstd[:, :], ALU.mult))
                        step(nc.vector.tensor_scalar(tmpc[:, :], tmpb[:, :], 1e-5, None, ALU.add))
                        dve.wait_ge(s_pw, 2)
                        step(nc.vector.tensor_tensor(rstd2[:, :], tmpb[:, :], rstd[:, :], ALU.mult))
                    r = rstd2 if twice else rstd
                    with dve.Fori(0, TILES // 2) as i2:
                        i = i2 * 2
                        for k in range(2):
                            t = src[:, ds(i + k, 1), :].rearrange("p t n -> p (t n)")
                            dve.wait_ge(s_e, i + (k + 1))
                            if save:
                                nc.vector.tensor_scalar(XN[:, ds(i + k, 1), :].rearrange("p t n -> p (t n)"), t,
                                                        mean[:, ds(i + k, 1)], rstd[:, ds(i + k, 1)],
                                                        ALU.subtract, ALU.mult)
                            nc.vector.tensor_scalar(xn[k][:, :], t, mean[:, ds(i + k, 1)], r[:, ds(i + k, 1)],
                                                    ALU.subtract, ALU.mult).then_inc(s_n, 1)

                @block.gpsimd
                def _(pool):
                    pool.wait_ge(s_x, 7)
                    nc.gpsimd.tensor_tensor(rstd[:, :], tmpc[:, :], nhalf[:, :], ALU.pow).then_inc(s_pw, 1)
                    if twice:
                        pool.wait_ge(s_x, 10)
                        nc.gpsimd.tensor_tensor(tmpb[:, :], tmpc[:, :], nhalf[:, :], ALU.pow).then_inc(s_pw, 1)

                @block.tensor
                def _(pe):
                    if add_from:
                        with pe.Fori(0, TILES // 2) as i2:
                            i = i2 * 2
                            for k in range(2):
                                pe.wait_ge(s_c, 2 * i + 2 * (k + 1))
                                nc.tensor.transpose(bank[k][:, 0:P], back[k][:, 0, :], ident[:, :])
                                nc.tensor.transpose(bank[k][:, P:C], back[k][0:C1, 1, :], ident[0:C1, 0:C1]
                                                    ).then_inc(s_t, 1)
                    with pe.Fori(0, TILES // 2) as i2:
                        i = i2 * 2
                        for k in range(2):
                            pe.wait_ge(s_n, i + (k + 1))
                            nc.tensor.transpose(bank[2 + k][:, 0:P], xn[k][:, 0:P], ident[:, :])
                            nc.tensor.transpose(bank[2 + k][0:C1, P:2 * P], xn[k][:, P:C], ident[:, :]
                                                ).then_inc(s_tr, 1)

                @block.scalar
                def _(act):
                    act.sem_inc(s_e, 2)
                    if add_from:
                        act.sem_inc(s_r, 2)
                        with act.Fori(0, TILES // 2) as i2:
                            i = i2 * 2
                            for k in range(2):
                                act.wait_ge(s_r, i + (k + 1))
                                nc.scalar.copy(back[k][:, 0, :], add_from[0][:, 0, ds((i + k) * P, P)]
                                               ).then_inc(s_c, 1)
                                nc.scalar.copy(back[k][0:C1, 1, :], add_from[0][0:C1, 1, ds((i + k) * P, P)]
                                               ).then_inc(s_c, 1)
                    halves = ((0, HALF, 0), (HALF, TILES, 1)) if affine else ((0, TILES, 0),)
                    for a, b, w in halves:
                        def evac(i, k):
                            act.wait_ge(s_tr, i + 1)
                            for c, n in CH:
                                src_ps = bank[2 + k][0:n, c * P:(c + 1) * P]
                                dst = XT[0:n, c, ds(i * P, P)]
                                if affine:
                                    g = affine[w] + c
                                    ins = nc.scalar.activation(dst, src_ps, ACT.Identity, scale=vecs[0:n, g:g + 1],
                                                               bias=vecs[0:n, g + 2:g + 3])
                                else:
                                    ins = nc.scalar.copy(dst, src_ps)
                            ins.then_inc(s_e, 1)
                        if a % 2:
                            evac(a, a % 2)
                        lo, hi = a + a % 2, b - b % 2
                        with act.Fori(0, (hi - lo) // 2) as i2:
                            i = i2 * 2 + lo
                            evac(i, 0)
                            evac(i + 1, 1)
                        if b % 2:
                            evac(b - 1, (b - 1) % 2)
            end_phase()

        def load_samples(sp, s_xb, s_used, first, count):
            sp.dma_start(XB[:, :, :], XT[:, :, first * SLOT:first * SLOT + SEQ]).then_inc(s_xb, 16)
            with sp.Fori(0, count - 1) as n:
                sp.wait_ge(s_used, n + 1)
                sp.dma_start(XB[:, :, :], XT[:, :, ds((n + 1 + first) * SLOT, SEQ)]).then_inc(s_xb, 16)

        residual_norm(H, None, False, False, None)
        with ExitStack() as ph:
            def psb(name, shape, dt=F32):
                return ph.enter_context(nc.sbuf_tensor(name, shape, dt))

            wqkv = psb("a0_wqkv", [P, 2, 3 * C])
            wproj = psb("a0_wproj", [P, 2, C])
            wgp = psb("a0_wgp", [P, 2, GP])
            QK = psb("a0_QK", [P, 2, 2, SEQ])
            V = psb("a0_V", [P, 2, C])
            gneg, gsum, gr, smax, sneg, ssum, sr = (psb(f"a0_{x}", [P, 2]) for x in
                                                    ("gneg", "gsum", "gr", "smax", "sneg", "ssum", "sr"))
            EG = psb("a0_EG", [P, 2, GP])
            GW = psb("a0_GW", [P, 2, P])
            GT = psb("a0_GT", [GP, SEQ])
            ES = psb("a0_ES", [P, 2, SEQ])
            TT = psb("a0_TT", [P, 2, SEQ])
            WW = psb("a0_WW", [P, 2, SEQ])
            WT = psb("a0_WT", [P, 2, SEQ])
            OT = psb("a0_OT", [P, 2, SEQ])
            scale = float(C) ** -0.5
            (s_w, s_xb, s_qkv, s_qk, s_v, s_lg, s_s, s_gm, s_sm0, s_sm, s_eg, s_es, s_rg, s_gw, s_rs, s_gt, s_gte,
             s_g, s_t, s_ww, s_wt, s_wte, s_o, s_ot, s_pr, s_at) = phase_sem([
                "weights", "sample_loaded", "projected", "qk_evacuated", "v_evacuated", "group_logits", "scores",
                "group_max", "score_max", "score_shift", "group_exp", "score_exp", "group_recip", "group_weights",
                "score_recip", "group_transposed", "group_evacuated", "group_product", "mix", "weighted",
                "weights_transposed", "weights_evacuated", "attended", "attended_evacuated", "out_projected",
                "out_evacuated"])
            with nc.Block() as block:
                @block.sync
                def _(sp):
                    sp.dma_start(wqkv[:, :, :], d["a0_qkv"]).then_inc(s_w, 16)
                    sp.dma_start(wproj[:, :, :], d["a0_proj"]).then_inc(s_w, 16)
                    sp.dma_start(wgp[:, :, :], d["a0_gp"]).then_inc(s_w, 16)
                    load_samples(sp, s_xb, s_qkv, 0, B)

                @block.tensor
                def _(pe):
                    def project(n):
                        pe.wait_ge(s_xb, 16 * n + 16)
                        for w in range(2):
                            for m, rows_m in CH:
                                for c, rows_c in CH:
                                    nc.tensor.matmul(bank[w][0:rows_m, m * SEQ:(m + 1) * SEQ],
                                                     wqkv[0:rows_c, c, w * C + m * P:w * C + m * P + rows_m],
                                                     XB[0:rows_c, c, :], start=(m == 0 and c == 0), stop=(c == 1),
                                                     skip_group_check=True)
                        for i, (t0, nt) in enumerate(QA_SEGS):
                            for c, rows_c in CH:
                                mm = nc.tensor.matmul(bank[2][0:nt, i * C:(i + 1) * C], XB[0:rows_c, c, t0:t0 + nt],
                                                      wqkv[0:rows_c, c, 2 * C:3 * C], start=(i == 0 and c == 0),
                                                      stop=(c == 1), skip_group_check=True)
                        mm.then_inc(s_qkv, 1)

                    def sample(n, last):
                        pe.wait_ge(s_qk, 4 * n + 4)
                        pe.wait_ge(s_at, 2 * n + 2)
                        for i, (t0, nt) in enumerate(QA_SEGS):
                            for c, rows_c in CH:
                                mm = nc.tensor.matmul(bank[3][0:nt, i * GP:(i + 1) * GP],
                                                      QK[0:rows_c, 0, c, t0:t0 + nt], wgp[0:rows_c, c, :],
                                                      start=(i == 0 and c == 0), stop=(c == 1), skip_group_check=True)
                        mm.then_inc(s_lg, 1)
                        for i, (t0, nt) in enumerate(QA_SEGS):
                            for c, rows_c in CH:
                                mm = nc.tensor.matmul(bank[4][0:nt, i * SEQ:(i + 1) * SEQ],
                                                      QK[0:rows_c, 0, c, t0:t0 + nt], QK[0:rows_c, 1, c, :],
                                                      start=(i == 0 and c == 0), stop=(c == 1), skip_group_check=True)
                        mm.then_inc(s_s, 1)
                        if not last:
                            pe.wait_ge(s_v, 2 * n + 2)
                            project(n + 1)
                        pe.wait_ge(s_gw, 2 * n + 2)
                        for i, (t0, nt) in enumerate(QA_SEGS):
                            tr = nc.tensor.transpose(bank[5][:, t0:t0 + nt], GW[0:nt, i, :], ident[0:nt, 0:nt])
                        tr.then_inc(s_gt, 1)
                        pe.wait_ge(s_gte, n + 1)
                        for i, (t0, nt) in enumerate(QA_SEGS):
                            mm = nc.tensor.matmul(bank[6][0:nt, i * SEQ:(i + 1) * SEQ], GT[:, t0:t0 + nt], GT[:, :],
                                                  start=(i == 0), stop=True, skip_group_check=True)
                        mm.then_inc(s_g, 1)
                        pe.wait_ge(s_ww, 2 * n + 2)
                        for i, (q0, nq) in enumerate(QA_SEGS):
                            for j, (k0, nk) in enumerate(QA_SEGS):
                                tr = nc.tensor.transpose(bank[7][0:nk, j * SEQ + q0:j * SEQ + q0 + nq],
                                                         WW[0:nq, i, k0:k0 + nk], ident[0:nq, 0:nq])
                        tr.then_inc(s_wt, 1)
                        pe.wait_ge(s_wte, 2 * n + 2)
                        pe.wait_ge(s_v, 2 * n + 2)
                        for m, rows_m in CH:
                            for j, (k0, nk) in enumerate(QA_SEGS):
                                mm = nc.tensor.matmul(bank[5][0:rows_m, m * SEQ:(m + 1) * SEQ],
                                                      V[0:nk, j, m * P:m * P + rows_m], WT[0:nk, j, :],
                                                      start=(m == 0 and j == 0), stop=(j == 1), skip_group_check=True)
                        mm.then_inc(s_o, 1)
                        pe.wait_ge(s_ot, 2 * n + 2)
                        for m, rows_m in CH:
                            for c, rows_c in CH:
                                mm = nc.tensor.matmul(bank[3][0:rows_m, m * SEQ:(m + 1) * SEQ],
                                                      wproj[0:rows_c, c, m * P:m * P + rows_m], OT[0:rows_c, c, :],
                                                      start=(m == 0 and c == 0), stop=(c == 1), skip_group_check=True)
                        mm.then_inc(s_pr, 1)

                    pe.wait_ge(s_w, 48)
                    project(0)
                    with pe.Fori(0, B - 1) as n:
                        sample(n, False)
                    sample(B - 1, True)

                @block.scalar
                def _(act):
                    def evacuate_qk(n):
                        act.wait_ge(s_qkv, n + 1)
                        for w, vb in ((0, V_BQ), (1, V_BK)):
                            for c, rows_c in CH:
                                nc.scalar.activation(QK[0:rows_c, w, c, :], bank[w][0:rows_c, c * SEQ:(c + 1) * SEQ],
                                                     ACT.Identity, bias=vecs[0:rows_c, vb + c:vb + c + 1]
                                                     ).then_inc(s_qk, 1)

                    def sample(n, last):
                        act.wait_ge(s_gm, 2 * n + 2)
                        for i, (t0, nt) in enumerate(QA_SEGS):
                            nc.scalar.activation(EG[0:nt, i, :], bank[3][0:nt, i * GP:(i + 1) * GP], ACT.Exp,
                                                 bias=gneg[0:nt, i:i + 1], accum_out=gsum[0:nt, i:i + 1]
                                                 ).then_inc(s_eg, 1)
                        act.wait_ge(s_sm, 2 * n + 2)
                        for i, (t0, nt) in enumerate(QA_SEGS):
                            nc.scalar.activation(ES[0:nt, i, :], bank[4][0:nt, i * SEQ:(i + 1) * SEQ], ACT.Exp,
                                                 bias=sneg[0:nt, i:i + 1], scale=scale, accum_out=ssum[0:nt, i:i + 1]
                                                 ).then_inc(s_es, 1)
                        if not last:
                            evacuate_qk(n + 1)
                        act.wait_ge(s_gt, n + 1)
                        nc.scalar.copy(GT[:, :], bank[5][0:GP, 0:SEQ]).then_inc(s_gte, 1)
                        act.wait_ge(s_wt, n + 1)
                        for j, (k0, nk) in enumerate(QA_SEGS):
                            nc.scalar.copy(WT[0:nk, j, :], bank[7][0:nk, j * SEQ:(j + 1) * SEQ]).then_inc(s_wte, 1)
                        act.wait_ge(s_o, n + 1)
                        for c, rows_c in CH:
                            nc.scalar.copy(OT[0:rows_c, c, :], bank[5][0:rows_c, c * SEQ:(c + 1) * SEQ]
                                           ).then_inc(s_ot, 1)

                    evacuate_qk(0)
                    with act.Fori(0, B - 1) as n:
                        sample(n, False)
                    sample(B - 1, True)

                @block.vector
                def _(dve):
                    def evacuate_v(n):
                        dve.wait_ge(s_qkv, n + 1)
                        for i, (t0, nt) in enumerate(QA_SEGS):
                            nc.vector.tensor_tensor(V[0:nt, i, :], bank[2][0:nt, i * C:(i + 1) * C],
                                                    rows[0:nt, BV0, :], ALU.add).then_inc(s_v, 1)

                    def sample(n, last):
                        dve.wait_ge(s_lg, n + 1)
                        for i, (t0, nt) in enumerate(QA_SEGS):
                            nc.vector.tensor_reduce(gneg[0:nt, i:i + 1], bank[3][0:nt, i * GP:(i + 1) * GP], AX.X,
                                                    ALU.max, negate=True).then_inc(s_gm, 1)
                        dve.wait_ge(s_s, n + 1)
                        for i, (t0, nt) in enumerate(QA_SEGS):
                            nc.vector.tensor_reduce(smax[0:nt, i:i + 1], bank[4][0:nt, i * SEQ:(i + 1) * SEQ], AX.X,
                                                    ALU.max).then_inc(s_sm0, 1)
                        dve.wait_ge(s_sm0, 2 * n + 2)
                        for i, (t0, nt) in enumerate(QA_SEGS):
                            nc.vector.tensor_scalar(sneg[0:nt, i:i + 1], smax[0:nt, i:i + 1], -scale, None, ALU.mult
                                                    ).then_inc(s_sm, 1)
                        dve.wait_ge(s_eg, 2 * n + 2)
                        for i, (t0, nt) in enumerate(QA_SEGS):
                            nc.vector.reciprocal(gr[0:nt, i:i + 1], gsum[0:nt, i:i + 1]).then_inc(s_rg, 1)
                        dve.wait_ge(s_rg, 2 * n + 2)
                        for i, (t0, nt) in enumerate(QA_SEGS):
                            nc.vector.tensor_scalar(GW[0:nt, i, 0:GP], EG[0:nt, i, :], gr[0:nt, i:i + 1], None, ALU.mult
                                                    ).then_inc(s_gw, 1)
                        dve.wait_ge(s_es, 2 * n + 2)
                        for i, (t0, nt) in enumerate(QA_SEGS):
                            nc.vector.reciprocal(sr[0:nt, i:i + 1], ssum[0:nt, i:i + 1]).then_inc(s_rs, 1)
                        dve.wait_ge(s_g, n + 1)
                        for i, (t0, nt) in enumerate(QA_SEGS):
                            nc.vector.tensor_scalar(TT[0:nt, i, :], bank[6][0:nt, i * SEQ:(i + 1) * SEQ],
                                                    alo[0:nt, 3:4], alo[0:nt, 2:3], ALU.mult, ALU.add
                                                    ).then_inc(s_t, 1)
                        dve.wait_ge(s_rs, 2 * n + 2)
                        dve.wait_ge(s_t, 2 * n + 2)
                        for i, (t0, nt) in enumerate(QA_SEGS):
                            nc.vector.scalar_tensor_tensor(WW[0:nt, i, :], ES[0:nt, i, :], sr[0:nt, i:i + 1],
                                                           TT[0:nt, i, :], ALU.mult, ALU.mult).then_inc(s_ww, 1)
                        if not last:
                            dve.wait_ge(s_o, n + 1)
                            evacuate_v(n + 1)
                        dve.wait_ge(s_pr, n + 1)
                        for c, rows_c in CH:
                            nc.vector.tensor_scalar(AT[0:rows_c, c, ds(n * SLOT, SEQ)],
                                                    bank[3][0:rows_c, c * SEQ:(c + 1) * SEQ],
                                                    vecs[0:rows_c, V_BP0 + c:V_BP0 + c + 1], None, ALU.add
                                                    ).then_inc(s_at, 1)

                    dve.sem_inc(s_at, 2)
                    nc.vector.memset(AT[:, :, :], 0.0)
                    nc.vector.memset(GW[:, :, :], 0.0)
                    evacuate_v(0)
                    with dve.Fori(0, B - 1) as n:
                        sample(n, False)
                    sample(B - 1, True)

        end_phase()

        def add_to_h(i, psum, dve, s):
            h = H[:, ds(i, 1), :]
            nc.vector.tensor_tensor(h, psum, h, ALU.add).then_inc(s, 1)

        residual_norm(H, (AT, add_to_h), True, True, (V_N1L, V_N1S))
        if stop == 2:
            return H

        def heads_attention(ph, cfg):
            def psb(name, shape, dt=F32):
                return ph.enter_context(nc.sbuf_tensor(f"{cfg['name']}_{name}", shape, dt))

            K, Q, QF, O, S, R, ON = (psb(x, [P, HB, SEQ]) for x in ("K", "Q", "QF", "O", "S", "R", "ON"))
            KH, QM = (psb(x, [P, 4, HB, SEQ]) for x in ("KH", "QM"))
            V = psb("V", [P, 2, NH, HP])
            ones = psb("ones", [P, HP])
            MX = psb("MX", [P, 2, HB * P])
            PT = psb("PT", [P, cfg["pt_rows"], HB, 4, SEQ])
            kv = cfg["kv"]
            sunits = [(b, *u) for u in cfg["sunits"] for b in range(HB)]
            tunits = [(b, *u) for u in cfg["tunits"] for b in range(HB)]
            scale = float(HD) ** -0.5
            N, outer, masks = cfg["count"], cfg["outer"], cfg.get("masks")
            ns, ne = len(sunits), len(tunits)
            ng = cfg["finish_ops"]
            t_banks = [7, 1, 2, 3, 0]
            out_bank = bank[t_banks[ne % 5]]
            pv_banks = (3, 0)
            (free_bank,) = {1, 2} - {t_banks[ne % 5]}
            s_banks = [7, 4, 5, free_bank, t_banks[ne % 5], pv_banks[0]]
            (s_set, s_w0, s_w1, s_xb, s_qkp, s_qkv, s_qk, s_v, s_sc, s_mx, s_mt, s_qf, s_qm, s_st, s_ex, s_pv, s_os,
             s_rc, s_on, s_out, s_fin) = phase_sem([
                "buffers_set", "weights0_loaded", "weights1_loaded", "sample_loaded", "qk_projected", "projected",
                "qk_evacuated", "v_evacuated", "scores", "maxima", "maxima_transposed", "queries_shifted",
                "queries_split", "scores_transposed", "exponentials", "attended", "sums_evacuated", "reciprocals",
                "normalised", "out_projected", "out_finished"])

            def runs(eng, body):
                if outer == 1:
                    for k in range(2):
                        body(k, k)
                else:
                    with eng.Fori(0, outer) as o:
                        for k in range(2):
                            body(o * 2 + k, k)

            def pipelined(eng, run, sample):
                sample(run * N, 0, True, False)
                with eng.Fori(0, N - 2) as j:
                    sample(run * N + 1 + j, j + 1, False, False)
                sample(run * N + (N - 1), N - 1, False, True)

            with nc.Block() as block:
                @block.gpsimd
                def _(pool):
                    cfg["load"](pool, (s_w0, s_w1), runs)

                @block.sync
                def _(sp):
                    sp.sem_inc(s_qkv, 1)

                    def run_loads(run, k):
                        with sp.Fori(0, N) as n:
                            sp.wait_ge(s_qkv, run * N + n + 1)
                            sp.dma_start(XB[:, :, :], XT[:, :, ds(cfg["sample"](n, k) * SLOT, SEQ)]
                                         ).then_inc(s_xb, 16)

                    runs(sp, run_loads)

                @block.tensor
                def _(pe):
                    def project(g, k):
                        pe.wait_ge(s_xb, g * 16 + 16)
                        for w in range(2):
                            for m in range(HB):
                                for c, n in CH:
                                    mm = nc.tensor.matmul(bank[4 + w][:, m * SEQ:(m + 1) * SEQ],
                                                          cfg["w"][k][w][0:n, c, m * P:(m + 1) * P], XB[0:n, c, :],
                                                          start=(m == 0 and c == 0), stop=(c == 1),
                                                          skip_group_check=True)
                        mm.then_inc(s_qkp, 1)
                        order = sorted(range(2), key=lambda i: -kv[i][1])
                        for x, i in enumerate(order):
                            t0, n_t = kv[i]
                            for c, n in CH:
                                mm = nc.tensor.matmul(bank[6][0:n_t, i * C:(i + 1) * C], XB[0:n, c, t0:t0 + n_t],
                                                      cfg["w"][k][2][0:n, c, :], start=(x == 0 and c == 0),
                                                      stop=(c == 1), skip_group_check=True)
                        mm.then_inc(s_qkv, 1)

                    def out_project(k):
                        for x, (col, m0, rows_m) in enumerate(cfg["out_tiles"]):
                            for b in range(HB):
                                mm = nc.tensor.matmul(out_bank[0:rows_m, col:col + SEQ],
                                                      cfg["w"][k][3][:, b, m0:m0 + rows_m], ON[:, b, :],
                                                      start=(x == 0 and b == 0), stop=(b == HB - 1),
                                                      skip_group_check=True)
                        mm.then_inc(s_out, 1)

                    def sample(g, n, first, last, k):
                        pe.wait_ge(s_qk, g * 6 + 6)
                        for u, (b, s, q0, nq, k0, nk, r0, nr) in enumerate(sunits):
                            if u == 4:
                                pe.wait_ge(s_fin, (g + 1 if first else g) * ng)
                            if u == 5:
                                pe.wait_ge(s_os, g * 2 + 2)
                            if u >= 6:
                                pe.wait_ge(s_mx, g * ns + (u - 5))
                            dst = bank[s_banks[u % 6]][0:nq, 0:nr * nk]
                            if masks:
                                nc.tensor.matmul(dst, identb[0:nq, 0:nq],
                                                 masks[s][0:nq, 0:nk].unsqueeze(1).broadcast_to([nq, nr, nk]),
                                                 start=True, stop=False, skip_group_check=True)
                            nc.tensor.matmul(dst, Q[:, b, q0:q0 + nq], KH[:, r0:r0 + nr, b, k0:k0 + nk],
                                             start=not masks, stop=True, skip_group_check=True).then_inc(s_sc, 1)
                        pe.wait_ge(s_mx, g * ns + ns)
                        for b in range(HB):
                            for s, (q0, nq) in enumerate(cfg["queries"]):
                                tr = nc.tensor.transpose(bank[7][:, b * SEQ + q0:b * SEQ + q0 + nq],
                                                         MX[0:nq, s, b * P:(b + 1) * P], ident[0:nq, 0:nq])
                        tr.then_inc(s_mt, 1)
                        if not last:
                            pe.wait_ge(s_v, g * 2 + 2)
                            project(g + 1, k)
                        pe.wait_ge(s_qm, g * 4 + 4)
                        for u, (b, row, k0, nk, q0, nq, r0, nr) in enumerate(tunits):
                            if u >= 5:
                                pe.wait_ge(s_ex, g * ne + (u - 4))
                            dst = bank[t_banks[u % 5]][0:nk, 0:nr * nq]
                            if masks:
                                nc.tensor.matmul(dst, identb[0:nk, 0:nk],
                                                 masks[2 + (k0 > 0)][0:nk, 0:nq].unsqueeze(1).broadcast_to([nk, nr, nq]),
                                                 start=True, stop=False, skip_group_check=True)
                            nc.tensor.matmul(dst, K[:, b, k0:k0 + nk], QM[:, r0:r0 + nr, b, q0:q0 + nq],
                                             start=not masks, stop=True, skip_group_check=True).then_inc(s_st, 1)
                        if not first:
                            pe.wait_ge(s_ex, g * ne + (ne - 4))
                            pe.wait_ge(s_on, g)
                            out_project(k)
                        pe.wait_ge(s_ex, (g + 1) * ne)
                        pe.wait_ge(s_v, g * 2 + 2)
                        for b in range(HB):
                            for y, (k0, nk, q0, nq, row) in enumerate(cfg["ksegs"]):
                                for dst in range(2):
                                    for r in range(4):
                                        vals = V[0:nk, kv.index((k0, nk)), 4 * b + r, :] if dst == 0 else ones[0:nk, :]
                                        mm = nc.tensor.matmul(
                                            bank[pv_banks[dst]][HP * r:HP * r + HP, b * SEQ + q0:b * SEQ + q0 + nq],
                                            vals, PT[0:nk, row, b, r, q0:q0 + nq],
                                            start=(b == 0 and y == 0), stop=(y == len(cfg["ksegs"]) - 1),
                                            tile_position=(0, HP * r), skip_group_check=True)
                        mm.then_inc(s_pv, 1)
                        if last:
                            pe.wait_ge(s_fin, g * ng)
                            pe.wait_ge(s_on, g + 1)
                            out_project(k)

                    pe.wait_ge(s_set, 3)
                    if "also" in cfg:
                        pe.wait_ge(*cfg["also"])

                    def run_samples(run, k):
                        pe.wait_ge((s_w0, s_w1)[cfg["which"](k)], cfg["loads"](run, k))
                        project(run * N, k)
                        pipelined(pe, run, lambda g, n, f, l: sample(g, n, f, l, k))

                    runs(pe, run_samples)

                @block.scalar
                def _(act):
                    def evacuate_qk(g):
                        act.wait_ge(s_qkp, g + 1)
                        nc.scalar.copy(Q[:, :, :], bank[4][:, 0:HB * SEQ]).then_inc(s_qk, 1)
                        for r in range(4):
                            nc.scalar.activation(KH[:, r, :, :], bank[5][:, 0:HB * SEQ], ACT.Identity,
                                                 scale=vecs[:, V_HEAD + r:V_HEAD + r + 1]).then_inc(s_qk, 1)

                    def evacuate_k(g):
                        nc.scalar.activation(K[:, :, :], bank[5][:, 0:HB * SEQ], ACT.Identity,
                                             bias=vecs[:, V_KONE:V_KONE + 1]).then_inc(s_qk, 1)

                    def evacuate_v(g):
                        act.wait_ge(s_qkv, g + 2)
                        for i, (t0, n_t) in enumerate(kv):
                            nc.scalar.copy(V[0:n_t, i, :, 0:HD],
                                           bank[6][0:n_t, i * C:(i + 1) * C].rearrange("p (h d) -> p h d", h=NH)
                                           ).then_inc(s_v, 1)

                    def sample(g, n, first, last):
                        if not last:
                            act.wait_ge(s_qf, g + 1)
                            evacuate_qk(g + 1)
                        for u, (b, row, k0, nk, q0, nq, r0, nr) in enumerate(tunits):
                            act.wait_ge(s_st, g * ne + u + 1)
                            nc.scalar.activation(PT[0:nk, row, b, r0:r0 + nr, q0:q0 + nq],
                                                 bank[t_banks[u % 5]][0:nk, 0:nr * nq].rearrange(
                                                     "p (r q) -> p r q", r=nr), ACT.Exp, scale=scale).then_inc(s_ex, 1)
                        if not last:
                            evacuate_k(g + 1)
                        act.wait_ge(s_pv, g + 1)
                        for dst, src in ((O, pv_banks[0]), (S, pv_banks[1])):
                            nc.scalar.copy(dst[:, :, :], bank[src][:, 0:HB * SEQ]).then_inc(s_os, 1)
                        if not last:
                            evacuate_v(g + 1)

                    act.sem_inc(s_os, 2)
                    act.wait_ge(s_set, 3)

                    def run_samples(run, k):
                        evacuate_qk(run * N)
                        evacuate_k(run * N)
                        evacuate_v(run * N)
                        pipelined(act, run, sample)

                    runs(act, run_samples)

                @block.vector
                def _(dve):
                    nc.vector.memset(V[:, :, :, :], 0.0).then_inc(s_set, 1)
                    nc.vector.memset(ones[:, :], 1.0).then_inc(s_set, 1)
                    nc.vector.memset(MX[:, :, :], 0.0).then_inc(s_set, 1)
                    dve.sem_inc(s_fin, ng)

                    def normalise(g):
                        dve.wait_ge(s_os, g * 2 + 4)
                        nc.vector.reciprocal(R[:, :, :], S[:, :, :]).then_inc(s_rc, 1)
                        dve.wait_ge(s_rc, g + 1)
                        nc.vector.tensor_tensor(ON[:, :, :], O[:, :, :], R[:, :, :], ALU.mult).then_inc(s_on, 1)

                    def sample(g, n, first, last, k):
                        for u, (b, s, q0, nq, k0, nk, r0, nr) in enumerate(sunits):
                            dve.wait_ge(s_sc, g * ns + u + 1)
                            c0 = b * P + HP * r0
                            dst = MX[0:nq, s, c0:c0 + HP * nr].rearrange("p (r c) -> p r c", r=nr)[:, :, HD]
                            nc.vector.tensor_reduce(
                                dst, bank[s_banks[u % 6]][0:nq, 0:nr * nk].rearrange("p (r k) -> p r k", r=nr),
                                AX.X, ALU.max).then_inc(s_mx, 1)
                        dve.wait_ge(s_mt, g + 1)
                        nc.vector.scalar_tensor_tensor(QF[:, :, :], bank[7][:, 0:HB * SEQ], -1.0, Q[:, :, :],
                                                       ALU.mult, ALU.add).then_inc(s_qf, 1)
                        dve.wait_ge(s_qf, g + 1)
                        for r in range(4):
                            nc.vector.tensor_scalar(QM[:, r, :, :], QF[:, :, :], vecs[:, V_HEAD + r:V_HEAD + r + 1],
                                                    None, ALU.mult).then_inc(s_qm, 1)
                        if not first:
                            normalise(g - 1)
                            dve.wait_ge(s_out, g)
                            cfg["finish"](n - 1, k, out_bank, s_fin)
                        if last:
                            normalise(g)
                            dve.wait_ge(s_out, g + 1)
                            cfg["finish"](n, k, out_bank, s_fin)

                    runs(dve, lambda run, k: pipelined(dve, run, lambda g, n, f, l: sample(g, n, f, l, k)))

        with ExitStack() as ph:
            def psb(name, shape, dt=F32):
                return ph.enter_context(nc.sbuf_tensor(name, shape, dt))

            fq, fk = psb("f_wq", [P, 2, HB * P]), psb("f_wk", [P, 2, HB * P])
            fv, fp = psb("f_wv", [P, 2, C]), psb("f_wp", [P, HB, C])
            fps = psb("f_wps", [P, HB, C])

            s_fs, = phase_sem(["elastic_weights"])

            def load_f(pool, s_ws, runs):
                s_w = s_ws[0]
                for dst, src in ((fq, "f_q"), (fk, "f_k"), (fv, "f_v"), (fp, "f_proj")):
                    pool.dma_start(dst[:, :, :], d[src]).then_inc(s_w, 16)
                pool.wait_ge(s_w, 64)
                n = 0
                for b, lo, hi, parts in ((0, 0, P, ((0, 64, 2), (64, 96, 1), (96, C, 0))),
                                         (1, 0, 64, ((0, 96, 1), (96, C, 0))), (1, 64, P, ((0, C, 0),)),
                                         (2, 0, P, ((0, C, 0),))):
                    for c0, c1, k in parts:
                        n += 1
                        nc.gpsimd.tensor_scalar(fps[lo:hi, b, c0:c1], fp[lo:hi, b, c0:c1], gs[lo:hi, k:k + 1], None,
                                                ALU.mult).then_inc(s_fs, 1)
                        pool.wait_ge(s_fs, n)

            def finish_f(n, k, psum, s_fin):
                for c, rows_c in CH:
                    bias = vecs[0:rows_c, V_BPL + c:V_BPL + c + 1] if k == 0 else bps[0:rows_c, c:c + 1]
                    nc.vector.tensor_scalar(AT[0:rows_c, c, ds((n + k * (B // 2)) * SLOT, SEQ)],
                                            psum[0:rows_c, c * SEQ:(c + 1) * SEQ], bias, None, ALU.add
                                            ).then_inc(s_fin, 1)

            heads_attention(ph, {
                "name": "f", "outer": 1, "count": B // 2, "w": [(fq, fk, fv, fp), (fq, fk, fv, fps)],
                "load": load_f, "loads": lambda run, k: 64, "which": lambda k: 0, "also": (s_fs, 7), "sample": lambda n, k: n + k * (B // 2),
                "finish": finish_f, "finish_ops": 2, "out_tiles": ((0, 0, P), (SEQ, P, C1)),
                "queries": QA_SEGS, "kv": list(QA_SEGS), "pt_rows": 2,
                "sunits": [(s, q0, nq, 0, SEQ, r0, 2) for s, (q0, nq) in enumerate(QA_SEGS) for r0 in (0, 2)],
                "tunits": [(s, k0, nk, 0, SEQ, r0, 2) for s, (k0, nk) in enumerate(QA_SEGS) for r0 in (0, 2)],
                "ksegs": [(k0, nk, 0, SEQ, s) for s, (k0, nk) in enumerate(QA_SEGS)],
            })

        end_phase()

        def add_to_xn(i, psum, dve, s):
            x = XN[:, ds(i, 1), :]
            nc.vector.tensor_tensor(x, psum, x, ALU.add).then_inc(s, 1)

        residual_norm(XN, (AT, add_to_xn), False, False, (V_N2L, V_N2S))
        if stop == 3:
            return H

        GT_ = 3 * P

        def feed_forward(tag, w1, w2s, hid, s_w, n_w, b1, groups, k_rows, finish, fin_ops, store=None):
            nv = len(k_rows)
            units = nv * HM
            g0, g1 = groups
            (s_up, s_gl, s_dn, s_fn, s_x, s_store) = phase_sem([
                f"{tag}_hidden", f"{tag}_gelu", f"{tag}_down", f"{tag}_finished", f"{tag}_partial", f"{tag}_stored"])
            with nc.Block() as block:
                @block.tensor
                def _(pe):
                    pe.wait_ge(s_w, n_w)
                    with pe.Fori(0, g1 - g0) as g:
                        for m in range(HM):
                            for v, rows_k in enumerate(k_rows):
                                u = m * nv + v
                                if v == 0:
                                    pe.wait_ge(s_gl, g * units + u + nv)
                                chunks = [(c, min(P, rows_k - c * P)) for c in range(2) if rows_k > c * P]
                                for x, (c, n) in enumerate(chunks):
                                    mm = nc.tensor.matmul(bank[u % 6][:, 0:GT_], w1[0:n, c, m * P:(m + 1) * P],
                                                          XT[0:n, c, ds((g + g0) * GT_, GT_)], start=(x == 0),
                                                          stop=(x == len(chunks) - 1))
                                mm.then_inc(s_up, 1)
                        pe.wait_ge(s_gl, (g + 1) * units + 6)
                        for j in range(3):
                            pe.wait_ge(s_fn, g * 3 + (1 if j < 2 else 2))
                            for m in range(HM):
                                for v, w in enumerate(w2s):
                                    n = w.shape[2]
                                    mm = nc.tensor.matmul(bank[6 + j % 2][:, 0:n], hid[:, m * nv + v, j * P:(j + 1) * P],
                                                          w[:, m, :], start=(m == 0 and v == 0),
                                                          stop=(m == HM - 1), skip_group_check=True)
                            mm.then_inc(s_dn, 1)

                @block.scalar
                def _(act):
                    act.sem_inc(s_gl, 6)
                    with act.Fori(0, g1 - g0) as g:
                        for m in range(HM):
                            for v in range(nv):
                                u = m * nv + v
                                act.wait_ge(s_up, g * units + u + 1)
                                nc.scalar.activation(hid[:, u, :], bank[u % 6][:, 0:GT_], ACT.Gelu,
                                                     bias=vecs[:, b1 + m:b1 + m + 1]).then_inc(s_gl, 1)

                @block.vector
                def _(dve):
                    dve.sem_inc(s_fn, 1)
                    with dve.Fori(0, g1 - g0) as g:
                        for j in range(3):
                            dve.wait_ge(s_dn, g * 3 + j + 1)
                            finish(dve, (g + g0) * 3 + j, g * 3 + j, bank[6 + j % 2][:, 0:C], s_x, s_fn)

                if store:
                    @block.sync
                    def _(sp):
                        with sp.Fori(0, g1 - g0) as g:
                            sp.wait_ge(s_fn, g * 3 + 4)
                            sp.dma_start(out.rearrange("(t p) n -> p t n", p=P)[:, ds((g + g0) * 3, 3), :],
                                         H[:, ds((g + g0) * 3, 3), :]).then_inc(s_store, 16)
                        sp.wait_ge(s_store, 16 * (g1 - g0))

        with ExitStack() as ph:
            def psb(name, shape, dt=F32):
                return ph.enter_context(nc.sbuf_tensor(name, shape, dt))

            w1 = psb("m_w1", [P, 2, HID])
            w2 = psb("m_w2", [P, HM, C])
            w2a, w2b, w2c = psb("m_w2a", [P, HM, C]), psb("m_w2b", [P, HM, 96]), psb("m_w2c", [P, HM, 64])
            hid = psb("m_hid", [P, 3 * HM, GT_])
            part = psb("m_part", [P, C])
            s_w, s_wm = phase_sem(["mlp_weights", "mlp_elastic_weights"])
            with nc.Block() as block:
                @block.sync
                def _(sp):
                    sp.dma_start(w1[:, :, :], d["f_w1"]).then_inc(s_w, 16)
                    sp.dma_start(w2[:, :, :], d["f_w2"]).then_inc(s_w, 16)

                @block.vector
                def _(dve):
                    dve.wait_ge(s_w, 32)
                    for k, (w, n) in enumerate(((w2a, C), (w2b, 96), (w2c, 64))):
                        nc.vector.tensor_scalar(w[:, :, :], w2[:, :, 0:n], vecs[:, V_GUM + k:V_GUM + k + 1], None,
                                                ALU.mult).then_inc(s_wm, 1)

            def finish_m(row):
                def finish(dve, tile, count, psum, s_x, s_fn):
                    h = H[:, ds(tile, 1), :].rearrange("p t n -> p (t n)")
                    x = XN[:, ds(tile, 1), :].rearrange("p t n -> p (t n)")
                    nc.vector.tensor_tensor(part[:, :], psum, x, ALU.add).then_inc(s_x, 1)
                    dve.wait_ge(s_x, count * 3 + 1)
                    nc.vector.tensor_tensor(part[:, :], part[:, :], rows[:, row, :], ALU.add).then_inc(s_x, 1)
                    dve.wait_ge(s_x, count * 3 + 2)
                    nc.vector.tensor_tensor(h, part[:, :], h, ALU.add).then_inc(s_x, 1)
                    dve.wait_ge(s_x, count * 3 + 3)
                    dve.sem_inc(s_fn, 1)
                return finish

            feed_forward("wide", w1, (w2,), hid, s_w, 32, V_B1, (0, 3), (C,), finish_m(B2L), 3)
            feed_forward("elastic", w1, (w2a, w2b, w2c), hid, s_w, 32, V_B1, (3, 6), (C, 96, 64), finish_m(B2S), 3)

        end_phase()
        residual_norm(H, None, False, False, None)
        if stop == 4:
            return H

        with ExitStack() as ph:
            def psb(name, shape, dt=F32):
                return ph.enter_context(nc.sbuf_tensor(name, shape, dt))

            GU = psb("e_GU", [P, HB, NTOK])
            gu_w = psb("e_guw", [P, EXPERTS, HB * HB * P])
            with ExitStack() as ph2:
                eo = ph2.enter_context(nc.sbuf_tensor("e_o", [P, EXPERTS, 2 * HB * P], F32))
                eg = ph2.enter_context(nc.sbuf_tensor("e_g", [P, EXPERTS, 2 * 2 * C], F32))
                s_l, s_f, s_c = phase_sem(["fold_loaded", "folded", "fold_evacuated"])
                with nc.Block() as block:
                    @block.sync
                    def _(sp):
                        sp.dma_start(eo[:, :, :], d["e_o"].rearrange("e p c n -> p e (c n)")).then_inc(s_l, 16)
                        sp.dma_start(eg[:, :, :], d["e_gu"].rearrange("e p c n -> p e (c n)")).then_inc(s_l, 16)

                    @block.vector
                    def _(dve):
                        nc.vector.memset(GU[:, :, :], 0.0)

                    @block.tensor
                    def _(pe):
                        pe.wait_ge(s_l, 32)
                        for e in range(EXPERTS):
                            for b in range(HB):
                                u = e * HB + b
                                if u >= 8:
                                    pe.wait_ge(s_c, u - 7)
                                for c, n in CH:
                                    mm = nc.tensor.matmul(bank[u % 8][:, 0:2 * C],
                                                          eo[0:n, e, c * HB * P + b * P:c * HB * P + (b + 1) * P],
                                                          eg[0:n, e, c * 2 * C:(c + 1) * 2 * C],
                                                          start=(c == 0), stop=(c == 1))
                                mm.then_inc(s_f, 1)

                    @block.scalar
                    def _(act):
                        for u in range(EXPERTS * HB):
                            act.wait_ge(s_f, u + 1)
                            nc.scalar.copy(gu_w[:, u // HB, (u % HB) * 2 * C:(u % HB + 1) * 2 * C],
                                           bank[u % 8][:, 0:2 * C]).then_inc(s_c, 1)

            ew = [(psb(f"e_wq{k}", [P, 2, HB * P]), psb(f"e_wk{k}", [P, 2, HB * P]), psb(f"e_wv{k}", [P, 2, C]),
                   psb(f"e_wg{k}", [P, HB, 2 * C])) for k in range(2)]
            mka, mkb = psb("e_mka", [P, 76], BF16), psb("e_mkb", [P, 128], BF16)
            mkta, mktb = psb("e_mkta", [P, 76], BF16), psb("e_mktb", [P, 65], BF16)
            s_m, = phase_sem(["masks"])
            with nc.Block() as block:
                @block.gpsimd
                def _(pool):
                    n = 0
                    for mk, (np_, nf), base, cm in ((mka, (76, 76), 0, 1), (mkb, (65, 128), 63, 1),
                                                    (mkta, (76, 76), 0, -1), (mktb, (128, 65), 63, -1)):
                        n += 1
                        nc.gpsimd.memset(mk[:, :], 0.0).then_inc(s_m, 1)
                        for b_, c_ in ((base, cm), (WIN - 1 - base, -cm)):
                            pool.wait_ge(s_m, n)
                            n += 1
                            nc.gpsimd.affine_select(out=mk[0:np_, :], in_=mk[0:np_, :], compare_op=ALU.is_ge,
                                                    fill=NEG, base=b_, pattern=[[-c_, nf]], channel_multiplier=c_
                                                    ).then_inc(s_m, 1)
                        pool.wait_ge(s_m, n)

            def load_e(pool, s_ws, runs):
                def load(run, k):
                    pool.wait_ge(s_free, run * 1 + 1)
                    s_w = s_ws[k]
                    for dst, src in zip(ew[k][:3], ("e_q", "e_k", "e_v")):
                        pool.dma_start(dst[:, :, :], d[src][ds(run, 1)].rearrange("e p c n -> p (e c) n")
                                       ).then_inc(s_w, 16)
                    pool.dma_start(ew[k][3][:, :, :], gu_w[:, ds(run, 1), :].rearrange("p e (b n) -> p (e b) n", b=HB)
                                   ).then_inc(s_w, 16)
                pool.sem_inc(s_free, 2)
                runs(pool, load)

            s_free, = phase_sem(["run_through"])

            def finish_e(n, k, psum, s_fin):
                gu = GU[:, :, ds(n * SLOT, SEQ)]
                ins = nc.vector.tensor_tensor(gu, psum[:, 0:HB * SEQ].rearrange("p (b q) -> p b q", b=HB), gu, ALU.add)
                ins.then_inc(s_fin, 1)
                if isinstance(n, int) and n == B - 1:
                    nc.vector.sem_inc(s_free, 1)

            heads_attention(ph, {
                "name": "e", "outer": EXPERTS // 2, "count": B, "w": ew, "load": load_e,
                "loads": lambda run, k: (run - k) * 32 + 64, "which": lambda k: k, "sample": lambda n, k: n,
                "finish": finish_e, "finish_ops": 1, "out_tiles": tuple((b * SEQ, b * P, P) for b in range(HB)),
                "queries": [(0, 76), (76, 65)], "kv": [(0, 76), (13, 128)], "masks": (mka, mkb, mkta, mktb), "pt_rows": 1,
                "sunits": [(0, 0, 76, 0, 76, 0, 4), (1, 76, 65, 13, 128, 0, 4)],
                "tunits": [(0, 0, 76, 0, 76, 0, 4), (0, 13, 128, 76, 65, 0, 4)],
                "ksegs": [(0, 76, 0, 76, 0), (13, 128, 76, 65, 0)],
            })

            sg = psb("e_sg", [P, 2, GT_])
            s_sl, s_gm = phase_sem(["silu", "gated"])
            with nc.Block() as block:
                @block.scalar
                def _(act):
                    act.sem_inc(s_gm, 2)
                    with act.Fori(0, NTOK // GT_) as g:
                        act.wait_ge(s_gm, g * 2 + 2)
                        cols = ds(g * GT_, GT_)
                        nc.scalar.activation(sg[:, 0, :], GU[:, 0, cols], ACT.Silu).then_inc(s_sl, 1)
                        nc.scalar.activation(sg[C1:P, 1, :], GU[0:C1, 1, cols], ACT.Silu).then_inc(s_sl, 1)

                @block.vector
                def _(dve):
                    with dve.Fori(0, NTOK // GT_) as g:
                        dve.wait_ge(s_sl, g * 2 + 2)
                        cols = ds(g * GT_, GT_)
                        nc.vector.tensor_tensor(AT[:, 0, cols], sg[:, 0, :], GU[:, 2, cols], ALU.mult).then_inc(s_gm, 1)
                        nc.vector.tensor_tensor(AT[0:C1, 1, cols], sg[C1:P, 1, :], GU[C1:P, 1, cols], ALU.mult
                                                ).then_inc(s_gm, 1)

        end_phase()
        residual_norm(H, (AT, add_to_h), False, False, None)
        if stop == 5:
            return H

        with ExitStack() as ph:
            def psb(name, shape, dt=F32):
                return ph.enter_context(nc.sbuf_tensor(name, shape, dt))

            w1 = psb("l_w1", [P, 2, HID])
            w2 = psb("l_w2", [P, HM, C])
            hid = psb("l_hid", [P, HM, GT_])
            s_w, = phase_sem(["last_weights"])
            with nc.Block() as block:
                @block.sync
                def _(sp):
                    sp.dma_start(w1[:, :, :], d["g_w1"]).then_inc(s_w, 16)
                    sp.dma_start(w2[:, :, :], d["g_w2"]).then_inc(s_w, 16)

            def finish_l(dve, tile, count, psum, s_x, s_fn):
                h = H[:, ds(tile, 1), :].rearrange("p t n -> p (t n)")
                nc.vector.tensor_tensor(h, psum, h, ALU.add).then_inc(s_fn, 1)

            feed_forward("last", w1, (w2,), hid, s_w, 32, V_FB, (0, 6), (C,), finish_l, 1, store=True)
        end_phase()
        return H


def kernel(**inputs):
    import numpy as np
    import concourse.bacc as bacc
    from concourse.bass_utils import run_bass_kernel_spmd

    arrays = lay_out(**inputs)
    nc = bacc.Bacc("TRN2", target_bir_lowering=False, num_devices=1)
    d = {n: nc.dram_tensor(f"in_{n}_dram", a.shape, mybir.dt.from_np(a.dtype), kind="ExternalInput").ap()
         for n, a in arrays.items()}
    out = nc.dram_tensor("out_0_dram", (NTOK, C), F32, kind="ExternalOutput").ap()
    fusion_kernel(nc, d, out)
    r = run_bass_kernel_spmd(nc, [{f"in_{n}_dram": a for n, a in arrays.items()}], core_ids=[0])
    got = np.asarray(r.results[0]["out_0_dram"])
    return np.ascontiguousarray(got.reshape(B, SLOT, C)[:, :SEQ])


def lay_out(**inputs):
    import numpy as np

    a = {k: np.asarray(v) for k, v in inputs.items()}

    def chunks(w):
        o = np.zeros((2, P, w.shape[1]), np.float32)
        o[0], o[1, :C1] = w[:P], w[P:]
        return np.ascontiguousarray(o.transpose(1, 0, 2))

    def heads_out(w):
        o = np.zeros((w.shape[0], NH, HP), np.float32)
        o[:, :, :HD] = w.reshape(-1, NH, HD)
        return o.reshape(-1, NH * HP)

    def heads_in(w):
        return np.ascontiguousarray(heads_out(w.T).T.reshape(HB, P, -1).transpose(1, 0, 2))

    def blocks(w):
        return np.ascontiguousarray(w.reshape(-1, P, w.shape[1]).transpose(1, 0, 2))

    def cols(v):
        o = np.zeros(-(-v.size // P) * P, np.float32)
        o[:v.size] = v.ravel()
        return o.reshape(-1, P).T

    x = a["x"].reshape(B, 3, 8, 16, 8, 16).transpose(0, 2, 4, 3, 5, 1).reshape(B * NPATCH, PD)
    h0 = np.zeros((B, SLOT, C), np.float32)
    h0[:, NPATCH:SEQ] = a["txt"]
    bqkv = a["L0_attn_b_qkv"]
    kone = np.zeros(P, np.float32)
    kone[HD::HP] = 1.0
    head = (np.arange(P)[:, None] // HP == np.arange(4)).astype(np.float32)
    f = "L0_ffn_"
    vecs = [cols(a["L0_tok_ln1_g"]), cols(a["L0_tok_ln1_b"]), cols(bqkv[:C]), cols(bqkv[C:2 * C]),
            cols(a["L0_attn_b_proj"])]
    for n in ("n1l", "n1s", "n2l", "n2s"):
        vecs += [cols(a[f + n + "_g"]), cols(a[f + n + "_b"])]
    vecs += [cols(a[f + "b_proj"]), cols(a[f + "b_fc1"]), cols(a["L1_ffn_in_bias"]),
             np.repeat(a[f + "gumbel_weights"][None], P, 0), np.repeat(a["L0_attn_alpha"][None], P, 0), kone[:, None],
             head]
    vecs = np.concatenate(vecs, 1)
    vecs = np.concatenate([vecs, np.zeros((P, 64 - vecs.shape[1]), np.float32)], 1)
    rows = np.stack([a["L0_tok_ln2_g"], a["L0_tok_ln2_b"], bqkv[2 * C:], a[f + "b_fc2"], a[f + "b_fc2"]])
    r = {
        "patches": x, "h0": h0.reshape(NTOK, C), "tok_w": a["L0_tok_W_proj"], "vecs": vecs,
        "rows": np.repeat(rows[None], P, 0),
        "a0_qkv": chunks(a["L0_attn_W_qkv"]), "a0_proj": chunks(a["L0_attn_W_proj"]), "a0_gp": chunks(a["L0_attn_W_gp"]),
        "f_q": chunks(heads_out(a[f + "w_qkv"][:, :C])), "f_k": chunks(heads_out(a[f + "w_qkv"][:, C:2 * C])),
        "f_v": chunks(a[f + "w_qkv"][:, 2 * C:]), "f_proj": heads_in(a[f + "w_proj"]),
        "f_w1": chunks(a[f + "w_fc1"]), "f_w2": blocks(a[f + "w_fc2"]),
        "g_w1": chunks(a["L1_ffn_in_weight"].T), "g_w2": blocks(a["L1_ffn_out_weight"]),
        "e_q": np.stack([chunks(heads_out(w.T)) for w in a["L1_attn_wq"]]),
        "e_k": np.stack([chunks(heads_out(w.T)) for w in a["L1_attn_wk"]]),
        "e_v": np.stack([chunks(w.T) for w in a["L1_attn_wv"]]),
        "e_o": np.stack([chunks(heads_out(w)) for w in a["L1_attn_wo"]]),
        "e_gu": np.stack([chunks(np.concatenate([a["L1_attn_w_gate"][:, cols_e], a["L1_attn_w_up"][P:, cols_e],
                                                 a["L1_attn_w_up"][:P, cols_e]], 0).T)
                          for cols_e in (slice(e * C, (e + 1) * C) for e in range(EXPERTS))]),
    }
    return {k: np.ascontiguousarray(v) for k, v in r.items()}
```

```python
from contextlib import ExitStack

import concourse.bass as bass
from concourse import mybir

F32 = mybir.dt.float32
BF16 = mybir.dt.bfloat16
ALU = mybir.AluOpType
ACT = mybir.ActivationFunctionType
AX = mybir.AxisListType

P = 128
C = 192
C1 = C - P
B, SEQ, NPATCH = 16, 141, 64
SLOT = 144
NTOK = B * SLOT
TILES = NTOK // P
HALF = TILES // 2
PD = 768
PK = PD // P
PT_TILES = B * NPATCH // P
HID = 768
HM = HID // P
NH, HD, HP = 12, 16, 32
HB = NH // 4
EXPERTS = 4
WIN = 64
GP = 49
NR, HC = 6, 96
CH = ((0, P), (1, C1))
QA_SEGS = ((0, 71), (71, 70))
NEG = -1e30


def ds(a, n):
    return bass.ds(a, n)


def fusion_kernel(nc: bass.Bass, d: dict, out: bass.AP, stop: int = 99):
    hd = nc.dram_tensor("h_staging", (NTOK, C), F32, kind="Internal").ap()
    with ExitStack() as ctx:
        def sb(name, shape, dt=F32):
            return ctx.enter_context(nc.sbuf_tensor(name, shape, dt))

        def sem(name):
            return ctx.enter_context(nc.semaphore(name))

        bank = [ctx.enter_context(nc.psum_tensor(f"bank{i}", [P, 512], F32)) for i in range(8)]

        H = sb("H", [P, TILES, C])
        XN = sb("XN", [P, TILES, C])
        XT = sb("XT", [P, 2, NTOK])
        ident = sb("ident", [P, P])
        identb = sb("identb", [P, P], BF16)
        stats = sb("stats", [P, TILES, 6])
        mean = sb("mean", [P, TILES])
        rstd = sb("rstd", [P, TILES])
        rstd2 = sb("rstd2", [P, TILES])
        tmpa = sb("tmpa", [P, TILES])
        tmpb = sb("tmpb", [P, TILES])
        tmpc = sb("tmpc", [P, TILES])
        nhalf = sb("nhalf", [P, TILES])
        vecs = sb("vecs", [P, 64])
        rows = sb("rows", [P, 5, C])
        LN2G, LN2B, BV0, B2L, B2S = range(5)
        V_LN1G, V_LN1B, V_BQ, V_BK, V_BP0, V_N1L, V_N1S, V_N2L, V_N2S, V_BPL, V_B1, V_FB, V_GUM, V_ALPHA, V_HEAD = \
            0, 6, 12, 14, 16, 18, 22, 26, 30, 34, 36, 42, 48, 51, 52
        gs = sb("gs", [P, 3])
        bps = sb("bps", [P, 2])
        alo = sb("alo", [P, 4])

        XB = sb("XB", [P, 2, SEQ])
        AT = sb("AT", [P, 2, NTOK])

        ph_n = [0]

        open_sems = []

        def phase_sem(names):
            ph_n[0] += 1
            got = [nc.alloc_semaphore(name=f"{x}_{ph_n[0]}") for x in names]
            open_sems.extend(got)
            return got

        def end_phase():
            nc.clear_and_free_semaphores(list(open_sems))
            open_sems.clear()
            nc.all_engine_barrier()

        s_vec, s_const, s_zero, s_vstep = (sem(x) for x in ("vectors_loaded", "constants_ready", "zeroed", "vector_step"))
        with nc.Block() as block:
            @block.sync
            def _(sp):
                sp.dma_start(vecs[:, :], d["vecs"]).then_inc(s_vec, 16)
                sp.dma_start(rows[:, :, :], d["rows"]).then_inc(s_vec, 16)

            @block.gpsimd
            def _(pool):
                nc.gpsimd.memset(ident[:, :], 0.0).then_inc(s_zero, 1)
                pool.wait_ge(s_zero, 1)
                nc.gpsimd.affine_select(out=ident[:, :], in_=ident[:, :], compare_op=ALU.not_equal, fill=1.0,
                                        base=0, pattern=[[-1, P]], channel_multiplier=1).then_inc(s_const, 1)

            @block.vector
            def _(dve):
                nc.vector.memset(XT[C1:P, 1, :], 0.0)
                nc.vector.memset(nhalf[:, :], -0.5)
                dve.wait_ge(s_const, 1)
                nc.vector.tensor_copy(identb[:, :], ident[:, :])
                dve.wait_ge(s_vec, 32)
                nc.vector.tensor_copy(gs[:, 0:1], vecs[:, V_GUM:V_GUM + 1]).then_inc(s_vstep, 1)
                nc.vector.tensor_tensor(gs[:, 1:2], vecs[:, V_GUM:V_GUM + 1], vecs[:, V_GUM + 1:V_GUM + 2],
                                        ALU.add).then_inc(s_vstep, 1)
                dve.wait_ge(s_vstep, 2)
                nc.vector.tensor_tensor(gs[:, 2:3], gs[:, 1:2], vecs[:, V_GUM + 2:V_GUM + 3],
                                        ALU.add).then_inc(s_vstep, 1)
                dve.wait_ge(s_vstep, 3)
                for a, b, k in ((0, 64, 2), (64, 96, 1), (96, 128, 0)):
                    nc.vector.tensor_tensor(bps[a:b, 0:1], vecs[a:b, V_BPL:V_BPL + 1], gs[a:b, k:k + 1], ALU.mult)
                nc.vector.tensor_tensor(bps[0:C1, 1:2], vecs[0:C1, V_BPL + 1:V_BPL + 2], gs[0:C1, 0:1], ALU.mult)
                for a, b, k in ((0, 64, 2), (64, 96, 1), (96, C, 0)):
                    nc.vector.tensor_scalar(rows[:, B2S, a:b], rows[:, B2L, a:b], gs[:, k:k + 1], None, ALU.mult)

            @block.scalar
            def _(act):
                act.wait_ge(s_vec, 32)
                nc.scalar.activation(alo[:, 0:1], vecs[:, V_ALPHA:V_ALPHA + 1], ACT.Exp, scale=-1.0)

        with nc.Block() as block:
            s_a, = phase_sem(["sigmoid_step"])

            @block.vector
            def _(dve):
                nc.vector.tensor_scalar(alo[:, 1:2], alo[:, 0:1], 1.0, None, ALU.add).then_inc(s_a, 1)
                dve.wait_ge(s_a, 1)
                nc.vector.reciprocal(alo[:, 2:3], alo[:, 1:2]).then_inc(s_a, 1)
                dve.wait_ge(s_a, 2)
                nc.vector.tensor_scalar(alo[:, 3:4], alo[:, 2:3], -1.0, 1.0, ALU.mult, ALU.add)

        with ExitStack() as ph:
            def psb(name, shape, dt=F32):
                return ph.enter_context(nc.sbuf_tensor(name, shape, dt))

            xp = psb("xp", [P, PT_TILES, PD])
            tokw = psb("tokw", [P, PK, C])
            tokws = psb("tokws", [P, PK, C])
            bnp = psb("bnp", [P, PT_TILES, 12])
            mvp = psb("mvp", [P, PT_TILES, 2])
            rp = psb("rp", [P, PT_TILES])
            ve = psb("ve", [P, PT_TILES])
            xpt = [psb(f"xpt{i}", [P, PK, P]) for i in range(2)]
            xpn = [psb(f"xpn{i}", [P, PD]) for i in range(2)]
            brow = psb("brow", [1, C])
            one1 = psb("one1", [1, P])
            Y = psb("Y", [P, PT_TILES, C])
            (s_w, s_p, s_st, s_bn, s_mv, s_rs, s_fold, s_fm, s_bd, s_bc, s_nrm, s_tr, s_ev, s_mm, s_y, s_ybn, s_yr,
             s_yn, s_yg, s_yo, s_hd, s_hl, s_one) = phase_sem([
                "tok_weights", "patches_loaded", "staged", "patch_stats", "patch_meanvar", "patch_rstd", "tok_folded",
                "tok_scaled", "bias_product", "bias_row", "patch_normed", "patch_transposed", "patch_evacuated",
                "embedded", "embed_copied", "embed_stats", "embed_rstd", "embed_normed", "embed_scaled", "embed_done",
                "embed_stored", "h_loaded", "tok_ones"])
            with nc.Block() as block:
                @block.sync
                def _(sp):
                    sp.dma_start(hd, d["h0"]).then_inc(s_st, 16)
                    sp.dma_start(xp[:, :, :], d["patches"].rearrange("(t p) n -> p t n", p=P)).then_inc(s_p, 16)
                    sp.dma_start(tokw[:, :, :], d["tok_w"].rearrange("(k p) n -> p k n", p=P)).then_inc(s_w, 16)
                    sp.wait_ge(s_st, 16)
                    with sp.Fori(0, PT_TILES) as t:
                        sp.wait_ge(s_yo, t + 1)
                        for k in range(2):
                            sp.dma_start(hd[ds(t * (2 * SLOT) + k * SLOT, NPATCH), :],
                                         Y[k * NPATCH:(k + 1) * NPATCH, ds(t, 1), :].rearrange("p t n -> p (t n)")
                                         ).then_inc(s_hd, 16)
                    sp.wait_ge(s_hd, 32 * PT_TILES)
                    sp.dma_start(H[:, :, :], hd.rearrange("(t p) n -> p t n", p=P)).then_inc(s_hl, 16)
                    sp.wait_ge(s_hl, 16)

                @block.vector
                def _(dve):
                    nc.vector.memset(one1[:, :], 1.0).then_inc(s_one, 1)
                    dve.wait_ge(s_p, 16)
                    with dve.Fori(0, PT_TILES) as t:
                        for k in range(2):
                            nc.vector.bn_stats(bnp[:, ds(t, 1), 6 * k:6 * k + 6],
                                               xp[:, ds(t, 1), k * 384:(k + 1) * 384]).then_inc(s_bn, 1)
                    dve.wait_ge(s_bn, 2 * PT_TILES)
                    for t in range(PT_TILES):
                        nc.vector.bn_aggr(mvp[:, t, :], bnp[:, t, :]).then_inc(s_mv, 1)
                    dve.wait_ge(s_mv, PT_TILES)
                    nc.vector.tensor_scalar(ve[:, :], mvp[:, :, 1], 1e-6, None, ALU.add).then_inc(s_mv, 1)
                    dve.wait_ge(s_w, 16)
                    for k in range(PK):
                        nc.vector.tensor_scalar(tokws[:, k, :], tokw[:, k, :], vecs[:, V_LN1G + k:V_LN1G + k + 1],
                                                None, ALU.mult).then_inc(s_fm, 1)
                    dve.wait_ge(s_rs, 1)
                    with dve.Fori(0, PT_TILES // 2) as t2:
                        t = t2 * 2
                        for k in range(2):
                            dve.wait_ge(s_ev, 2 * t + 2 * (k + 1))
                            nc.vector.tensor_scalar(xpn[k][:, :], xp[:, ds(t + k, 1), :].rearrange("p t n -> p (t n)"),
                                                    mvp[:, ds(t + k, 1), 0:1].rearrange("p t n -> p (t n)"),
                                                    rp[:, ds(t + k, 1)], ALU.subtract, ALU.mult).then_inc(s_nrm, 1)
                    dve.wait_ge(s_y, PT_TILES)
                    with dve.Fori(0, PT_TILES) as t:
                        nc.vector.bn_stats(bnp[:, ds(t, 1), 0:6], Y[:, ds(t, 1), :]).then_inc(s_ybn, 1)
                    dve.wait_ge(s_ybn, PT_TILES)
                    for t in range(PT_TILES):
                        nc.vector.bn_aggr(mvp[:, t, :], bnp[:, t, 0:6]).then_inc(s_ybn, 1)
                    dve.wait_ge(s_ybn, 2 * PT_TILES)
                    nc.vector.tensor_scalar(ve[:, :], mvp[:, :, 1], 1e-6, None, ALU.add).then_inc(s_ybn, 1)
                    dve.wait_ge(s_yr, 1)
                    with dve.Fori(0, PT_TILES) as t:
                        y = Y[:, ds(t, 1), :].rearrange("p t n -> p (t n)")
                        nc.vector.tensor_scalar(y, y, mvp[:, ds(t, 1), 0:1].rearrange("p t n -> p (t n)"),
                                                rp[:, ds(t, 1)], ALU.subtract, ALU.mult).then_inc(s_yn, 1)
                        dve.wait_ge(s_yn, t + 1)
                        nc.vector.tensor_tensor(y, y, rows[:, LN2G, :], ALU.mult).then_inc(s_yg, 1)
                        dve.wait_ge(s_yg, t + 1)
                        nc.vector.tensor_tensor(y, y, rows[:, LN2B, :], ALU.add).then_inc(s_yo, 1)

                @block.gpsimd
                def _(pool):
                    pool.wait_ge(s_mv, PT_TILES + 1)
                    nc.gpsimd.tensor_tensor(rp[:, :], ve[:, :], nhalf[:, 0:PT_TILES], ALU.pow).then_inc(s_rs, 1)
                    pool.wait_ge(s_ybn, 2 * PT_TILES + 1)
                    nc.gpsimd.tensor_tensor(rp[:, :], ve[:, :], nhalf[:, 0:PT_TILES], ALU.pow).then_inc(s_yr, 1)

                @block.tensor
                def _(pe):
                    pe.wait_ge(s_w, 16)
                    for k in range(PK):
                        mm = nc.tensor.matmul(bank[7][0:1, 0:C], vecs[:, V_LN1B + k:V_LN1B + k + 1], tokw[:, k, :],
                                              start=(k == 0), stop=(k == PK - 1))
                    mm.then_inc(s_bd, 1)
                    pe.wait_ge(s_fm, PK)
                    pe.wait_ge(s_bc, 1)
                    pe.wait_ge(s_one, 1)
                    with pe.Fori(0, PT_TILES // 2) as t2:
                        t = t2 * 2
                        for k in range(2):
                            pe.wait_ge(s_nrm, t + (k + 1))
                            for j in range(PK):
                                tr = nc.tensor.transpose(bank[2 * k + j // 4][:, (j % 4) * P:(j % 4 + 1) * P],
                                                         xpn[k][:, j * P:(j + 1) * P], ident[:, :])
                            tr.then_inc(s_tr, 1)
                            pe.wait_ge(s_ev, 2 * t + 2 * (k + 3))
                            for j in range(PK):
                                nc.tensor.matmul(bank[4 + k][:, 0:C], xpt[k][:, j, :], tokws[:, j, :],
                                                 start=(j == 0), stop=False)
                            nc.tensor.matmul(bank[4 + k][:, 0:C], one1[:, :], brow[:, :], start=False,
                                             stop=True).then_inc(s_mm, 1)

                @block.scalar
                def _(act):
                    act.sem_inc(s_ev, 4)
                    act.wait_ge(s_bd, 1)
                    nc.scalar.copy(brow[:, :], bank[7][0:1, 0:C]).then_inc(s_bc, 1)
                    with act.Fori(0, PT_TILES // 2) as t2:
                        t = t2 * 2
                        for k in range(2):
                            act.wait_ge(s_tr, t + (k + 1))
                            nc.scalar.copy(xpt[k][:, 0:4, :], bank[2 * k][:, 0:512]).then_inc(s_ev, 1)
                            nc.scalar.copy(xpt[k][:, 4:6, :], bank[2 * k + 1][:, 0:256]).then_inc(s_ev, 1)
                            act.wait_ge(s_mm, t + (k + 1))
                            nc.scalar.copy(Y[:, ds(t + k, 1), :], bank[4 + k][:, 0:C]).then_inc(s_y, 1)

        end_phase()
        if stop == 0:
            return H

        NG = 6

        def residual_norm(src, finish, save, twice, affine):
            (s_t, s_r, s_bn, s_x, s_ps, s_pw, s_n, s_tr, s_e) = phase_sem([
                "back_transposed", "residual_added", "norm_stats", "norm_step", "pow_step", "norm_pow", "normed",
                "norm_transposed", "norm_evacuated"])
            STEPS = 7
            with ExitStack() as ph:
                xn = [ph.enter_context(nc.sbuf_tensor(f"xn{i}_{ph_n[0]}", [P, C], F32)) for i in range(NG)]
                with nc.Block() as block:
                    @block.vector
                    def _(dve):
                        with dve.Fori(0, TILES // NG) as g:
                            for j in range(0, NG, 2):
                                if finish:
                                    for k in (j, j + 1):
                                        dve.wait_ge(s_t, g * NG + (k + 1))
                                        finish(g * NG + k, bank[k][:, 0:C], dve, s_r)
                                for k in (j, j + 1):
                                    if finish:
                                        dve.wait_ge(s_r, g * NG + (k + 1))
                                    nc.vector.bn_stats(stats[:, ds(g * NG + k, 1), :], src[:, ds(g * NG + k, 1), :]
                                                       ).then_inc(s_bn, 1)
                            dve.wait_ge(s_bn, g * NG + NG)
                            n = [0]

                            def step(ins):
                                n[0] += 1
                                ins.then_inc(s_x, 1)
                                if n[0] < STEPS:
                                    dve.wait_ge(s_x, g * STEPS + n[0])

                            st = stats[:, ds(g * NG, NG), :]
                            ta, tb, tc, tm = (x[:, ds(g * NG, NG)] for x in (tmpa, tmpb, tmpc, mean))
                            step(nc.vector.tensor_tensor(ta, st[:, :, 1], st[:, :, 4], ALU.add))
                            step(nc.vector.tensor_scalar(tm, ta, 0.5, None, ALU.mult))
                            step(nc.vector.tensor_tensor(ta, st[:, :, 1], st[:, :, 4], ALU.subtract))
                            step(nc.vector.scalar_tensor_tensor(tb, ta, 0.25, ta, ALU.mult, ALU.mult))
                            step(nc.vector.tensor_tensor(ta, st[:, :, 2], st[:, :, 5], ALU.add))
                            step(nc.vector.scalar_tensor_tensor(ta, ta, 1.0 / C, tb, ALU.mult, ALU.add))
                            step(nc.vector.tensor_scalar(tc, ta, 1e-5, None, ALU.add))
                        r = rstd2 if twice else rstd
                        with dve.Fori(0, TILES // NG) as g:
                            dve.wait_ge(s_pw, g + 1)
                            for k in range(NG):
                                i = g * NG + k
                                t = src[:, ds(i, 1), :].rearrange("p t n -> p (t n)")
                                if save:
                                    nc.vector.tensor_scalar(XN[:, ds(i, 1), :].rearrange("p t n -> p (t n)"), t,
                                                            mean[:, ds(i, 1)], rstd[:, ds(i, 1)],
                                                            ALU.subtract, ALU.mult)
                                dve.wait_ge(s_e, g * NG + (k + 1))
                                nc.vector.tensor_scalar(xn[k][:, :], t, mean[:, ds(i, 1)], r[:, ds(i, 1)],
                                                        ALU.subtract, ALU.mult).then_inc(s_n, 1)

                    @block.gpsimd
                    def _(pool):
                        n = [0]

                        def step(ins):
                            n[0] += 1
                            ins.then_inc(s_ps, 1)
                            pool.wait_ge(s_ps, n[0])

                        for g in range(TILES // NG):
                            r, r2, v, ve, t, ex = (x[:, g * NG:(g + 1) * NG]
                                                   for x in (rstd, rstd2, tmpa, tmpc, tmpb, nhalf))
                            pool.wait_ge(s_x, STEPS * (g + 1))
                            ins = nc.gpsimd.tensor_tensor(r, ve, ex, ALU.pow)
                            if twice:
                                step(ins)
                                step(nc.gpsimd.tensor_tensor(t, v, r, ALU.mult))
                                step(nc.gpsimd.tensor_tensor(t, t, r, ALU.mult))
                                step(nc.gpsimd.tensor_scalar(t, t, 1e-5, None, ALU.add))
                                step(nc.gpsimd.tensor_tensor(t, t, ex, ALU.pow))
                                ins = nc.gpsimd.tensor_tensor(r2, t, r, ALU.mult)
                            ins.then_inc(s_pw, 1)

                    @block.tensor
                    def _(pe):
                        if finish:
                            for i in range(TILES):
                                if i >= NG:
                                    pe.wait_ge(s_r, i - NG + 1)
                                nc.tensor.transpose(bank[i % NG][:, 0:P], AT[:, 0, i * P:(i + 1) * P], ident[:, :])
                                nc.tensor.transpose(bank[i % NG][:, P:C], AT[0:C1, 1, i * P:(i + 1) * P],
                                                    ident[0:C1, 0:C1]).then_inc(s_t, 1)
                        with pe.Fori(0, TILES // NG) as g:
                            for k in range(NG):
                                pe.wait_ge(s_n, g * NG + (k + 1))
                                nc.tensor.transpose(bank[k][:, 0:P], xn[k][:, 0:P], ident[:, :])
                                nc.tensor.transpose(bank[k][0:C1, P:2 * P], xn[k][:, P:C], ident[:, :]
                                                    ).then_inc(s_tr, 1)

                    @block.scalar
                    def _(act):
                        act.sem_inc(s_e, NG)
                        for i in range(TILES):
                            act.wait_ge(s_tr, i + 1)
                            for c, n in CH:
                                src_ps = bank[i % NG][0:n, c * P:(c + 1) * P]
                                dst = XT[0:n, c, i * P:(i + 1) * P]
                                if affine:
                                    v = affine[i // HALF] + c
                                    ins = nc.scalar.activation(dst, src_ps, ACT.Identity, scale=vecs[0:n, v:v + 1],
                                                               bias=vecs[0:n, v + 2:v + 3])
                                else:
                                    ins = nc.scalar.copy(dst, src_ps)
                            ins.then_inc(s_e, 1)
            end_phase()

        def load_samples(sp, s_xb, s_used, first, count):
            sp.dma_start(XB[:, :, :], XT[:, :, first * SLOT:first * SLOT + SEQ]).then_inc(s_xb, 16)
            with sp.Fori(0, count - 1) as n:
                sp.wait_ge(s_used, n + 1)
                sp.dma_start(XB[:, :, :], XT[:, :, ds((n + 1 + first) * SLOT, SEQ)]).then_inc(s_xb, 16)

        residual_norm(H, None, False, False, None)
        with ExitStack() as ph:
            def psb(name, shape, dt=F32):
                return ph.enter_context(nc.sbuf_tensor(name, shape, dt))

            wqkv = psb("a0_wqkv", [P, 2, 3 * C])
            wproj = psb("a0_wproj", [P, 2, C])
            wgp = psb("a0_wgp", [P, 2, GP])
            QK = psb("a0_QK", [P, 2, 2, SEQ])
            V = psb("a0_V", [P, 2, C])
            gneg, gsum, gr, smax, sneg, ssum, sr = (psb(f"a0_{x}", [P, 2]) for x in
                                                    ("gneg", "gsum", "gr", "smax", "sneg", "ssum", "sr"))
            EG = psb("a0_EG", [P, 2, GP])
            GW = psb("a0_GW", [P, 2, P])
            GT = psb("a0_GT", [GP, SEQ])
            ES = psb("a0_ES", [P, 2, SEQ])
            TT = psb("a0_TT", [P, 2, SEQ])
            WW = psb("a0_WW", [P, 2, SEQ])
            WT = psb("a0_WT", [P, 2, SEQ])
            OT = psb("a0_OT", [P, 2, SEQ])
            scale = float(C) ** -0.5
            (s_w, s_xb, s_qkp, s_qkv, s_qk, s_v, s_lg, s_s, s_gm, s_sm0, s_sm, s_eg, s_es, s_rg, s_gw, s_rs, s_gt, s_gte,
             s_g, s_t, s_ww, s_wt, s_wte, s_o, s_ot, s_pr, s_at) = phase_sem([
                "weights", "sample_loaded", "qk_projected", "projected", "qk_evacuated", "v_evacuated", "group_logits", "scores",
                "group_max", "score_max", "score_shift", "group_exp", "score_exp", "group_recip", "group_weights",
                "score_recip", "group_transposed", "group_evacuated", "group_product", "mix", "weighted",
                "weights_transposed", "weights_evacuated", "attended", "attended_evacuated", "out_projected",
                "out_evacuated"])
            with nc.Block() as block:
                @block.sync
                def _(sp):
                    sp.dma_start(wqkv[:, :, :], d["a0_qkv"]).then_inc(s_w, 16)
                    sp.dma_start(wproj[:, :, :], d["a0_proj"]).then_inc(s_w, 16)
                    sp.dma_start(wgp[:, :, :], d["a0_gp"]).then_inc(s_w, 16)
                    load_samples(sp, s_xb, s_qkv, 0, B)

                @block.tensor
                def _(pe):
                    def project_qk(n):
                        pe.wait_ge(s_xb, 16 * n + 16)
                        for w in range(2):
                            for m, rows_m in CH:
                                for c, rows_c in CH:
                                    mm = nc.tensor.matmul(bank[w][0:rows_m, m * SEQ:(m + 1) * SEQ],
                                                          wqkv[0:rows_c, c, w * C + m * P:w * C + m * P + rows_m],
                                                          XB[0:rows_c, c, :], start=(m == 0 and c == 0), stop=(c == 1),
                                                          skip_group_check=True)
                        mm.then_inc(s_qkp, 1)

                    def project_v(n):
                        for i, (t0, nt) in enumerate(QA_SEGS):
                            for c, rows_c in CH:
                                mm = nc.tensor.matmul(bank[2][0:nt, i * C:(i + 1) * C], XB[0:rows_c, c, t0:t0 + nt],
                                                      wqkv[0:rows_c, c, 2 * C:3 * C], start=(i == 0 and c == 0),
                                                      stop=(c == 1), skip_group_check=True)
                        mm.then_inc(s_qkv, 1)

                    def scores(n):
                        pe.wait_ge(s_qk, 4 * n + 4)
                        for i, (t0, nt) in enumerate(QA_SEGS):
                            for c, rows_c in CH:
                                mm = nc.tensor.matmul(bank[3][0:nt, i * GP:(i + 1) * GP],
                                                      QK[0:rows_c, 0, c, t0:t0 + nt], wgp[0:rows_c, c, :],
                                                      start=(i == 0 and c == 0), stop=(c == 1), skip_group_check=True)
                        mm.then_inc(s_lg, 1)
                        for i, (t0, nt) in enumerate(QA_SEGS):
                            for c, rows_c in CH:
                                mm = nc.tensor.matmul(bank[4][0:nt, i * SEQ:(i + 1) * SEQ],
                                                      QK[0:rows_c, 0, c, t0:t0 + nt], QK[0:rows_c, 1, c, :],
                                                      start=(i == 0 and c == 0), stop=(c == 1), skip_group_check=True)
                        mm.then_inc(s_s, 1)

                    def out_project(n):
                        pe.wait_ge(s_ot, 2 * n + 2)
                        for m, rows_m in CH:
                            for c, rows_c in CH:
                                mm = nc.tensor.matmul(bank[6][0:rows_m, m * SEQ:(m + 1) * SEQ],
                                                      wproj[0:rows_c, c, m * P:m * P + rows_m], OT[0:rows_c, c, :],
                                                      start=(m == 0 and c == 0), stop=(c == 1), skip_group_check=True)
                        mm.then_inc(s_pr, 1)

                    def sample(n, first, last):
                        pe.wait_ge(s_gw, 2 * n + 2)
                        for i, (t0, nt) in enumerate(QA_SEGS):
                            tr = nc.tensor.transpose(bank[7][:, 2 * SEQ + t0:2 * SEQ + t0 + nt], GW[0:nt, i, :],
                                                     ident[0:nt, 0:nt])
                        tr.then_inc(s_gt, 1)
                        if not first:
                            out_project(n - 1)
                        if not last:
                            project_qk(n + 1)
                        pe.wait_ge(s_gte, n + 1)
                        if not first:
                            pe.wait_ge(s_at, 2 * n)
                        for i, (t0, nt) in enumerate(QA_SEGS):
                            mm = nc.tensor.matmul(bank[6][0:nt, i * SEQ:(i + 1) * SEQ], GT[:, t0:t0 + nt], GT[:, :],
                                                  start=(i == 0), stop=True, skip_group_check=True)
                        mm.then_inc(s_g, 1)
                        if not last:
                            pe.wait_ge(s_v, 2 * n + 2)
                            project_v(n + 1)
                        pe.wait_ge(s_ww, 2 * n + 2)
                        for i, (q0, nq) in enumerate(QA_SEGS):
                            for j, (k0, nk) in enumerate(QA_SEGS):
                                tr = nc.tensor.transpose(bank[7][0:nk, j * SEQ + q0:j * SEQ + q0 + nq],
                                                         WW[0:nq, i, k0:k0 + nk], ident[0:nq, 0:nq])
                        tr.then_inc(s_wt, 1)
                        if not last:
                            scores(n + 1)
                        pe.wait_ge(s_wte, 2 * n + 2)
                        pe.wait_ge(s_v, 2 * n + 2)
                        for m, rows_m in CH:
                            for j, (k0, nk) in enumerate(QA_SEGS):
                                mm = nc.tensor.matmul(bank[5][0:rows_m, m * SEQ:(m + 1) * SEQ],
                                                      V[0:nk, j, m * P:m * P + rows_m], WT[0:nk, j, :],
                                                      start=(m == 0 and j == 0), stop=(j == 1), skip_group_check=True)
                        mm.then_inc(s_o, 1)

                    pe.wait_ge(s_w, 48)
                    project_qk(0)
                    project_v(0)
                    scores(0)
                    sample(0, True, False)
                    with pe.Fori(0, B - 2) as i:
                        sample(i + 1, False, False)
                    sample(B - 1, False, True)
                    out_project(B - 1)

                @block.scalar
                def _(act):
                    def evacuate_qk(n):
                        act.wait_ge(s_qkp, n + 1)
                        for w, vb in ((0, V_BQ), (1, V_BK)):
                            for c, rows_c in CH:
                                nc.scalar.activation(QK[0:rows_c, w, c, :], bank[w][0:rows_c, c * SEQ:(c + 1) * SEQ],
                                                     ACT.Identity, bias=vecs[0:rows_c, vb + c:vb + c + 1]
                                                     ).then_inc(s_qk, 1)

                    def exponentials(n):
                        act.wait_ge(s_gm, 2 * n + 2)
                        for i, (t0, nt) in enumerate(QA_SEGS):
                            nc.scalar.activation(EG[0:nt, i, :], bank[3][0:nt, i * GP:(i + 1) * GP], ACT.Exp,
                                                 bias=gneg[0:nt, i:i + 1], accum_out=gsum[0:nt, i:i + 1]
                                                 ).then_inc(s_eg, 1)
                        act.wait_ge(s_sm, 2 * n + 2)
                        for i, (t0, nt) in enumerate(QA_SEGS):
                            nc.scalar.activation(ES[0:nt, i, :], bank[4][0:nt, i * SEQ:(i + 1) * SEQ], ACT.Exp,
                                                 bias=sneg[0:nt, i:i + 1], scale=scale, accum_out=ssum[0:nt, i:i + 1]
                                                 ).then_inc(s_es, 1)

                    def sample(n, last):
                        act.wait_ge(s_gt, n + 1)
                        nc.scalar.copy(GT[:, :], bank[7][0:GP, 2 * SEQ:3 * SEQ]).then_inc(s_gte, 1)
                        if not last:
                            evacuate_qk(n + 1)
                        act.wait_ge(s_wt, n + 1)
                        for j, (k0, nk) in enumerate(QA_SEGS):
                            nc.scalar.copy(WT[0:nk, j, :], bank[7][0:nk, j * SEQ:(j + 1) * SEQ]).then_inc(s_wte, 1)
                        if not last:
                            exponentials(n + 1)
                        act.wait_ge(s_o, n + 1)
                        for c, rows_c in CH:
                            nc.scalar.copy(OT[0:rows_c, c, :], bank[5][0:rows_c, c * SEQ:(c + 1) * SEQ]
                                           ).then_inc(s_ot, 1)

                    evacuate_qk(0)
                    exponentials(0)
                    with act.Fori(0, B - 1) as n:
                        sample(n, False)
                    sample(B - 1, True)

                @block.vector
                def _(dve):
                    def evacuate_v(n):
                        dve.wait_ge(s_qkv, n + 1)
                        for i, (t0, nt) in enumerate(QA_SEGS):
                            nc.vector.tensor_tensor(V[0:nt, i, :], bank[2][0:nt, i * C:(i + 1) * C],
                                                    rows[0:nt, BV0, :], ALU.add).then_inc(s_v, 1)

                    def softmax(n):
                        dve.wait_ge(s_lg, n + 1)
                        for i, (t0, nt) in enumerate(QA_SEGS):
                            nc.vector.tensor_reduce(gneg[0:nt, i:i + 1], bank[3][0:nt, i * GP:(i + 1) * GP], AX.X,
                                                    ALU.max, negate=True).then_inc(s_gm, 1)
                        dve.wait_ge(s_s, n + 1)
                        for i, (t0, nt) in enumerate(QA_SEGS):
                            nc.vector.tensor_reduce(smax[0:nt, i:i + 1], bank[4][0:nt, i * SEQ:(i + 1) * SEQ], AX.X,
                                                    ALU.max).then_inc(s_sm0, 1)
                        dve.wait_ge(s_sm0, 2 * n + 2)
                        for i, (t0, nt) in enumerate(QA_SEGS):
                            nc.vector.tensor_scalar(sneg[0:nt, i:i + 1], smax[0:nt, i:i + 1], -scale, None, ALU.mult
                                                    ).then_inc(s_sm, 1)
                        dve.wait_ge(s_eg, 2 * n + 2)
                        for i, (t0, nt) in enumerate(QA_SEGS):
                            nc.vector.reciprocal(gr[0:nt, i:i + 1], gsum[0:nt, i:i + 1]).then_inc(s_rg, 1)
                        dve.wait_ge(s_rg, 2 * n + 2)
                        for i, (t0, nt) in enumerate(QA_SEGS):
                            nc.vector.tensor_scalar(GW[0:nt, i, 0:GP], EG[0:nt, i, :], gr[0:nt, i:i + 1], None, ALU.mult
                                                    ).then_inc(s_gw, 1)
                        dve.wait_ge(s_es, 2 * n + 2)
                        for i, (t0, nt) in enumerate(QA_SEGS):
                            nc.vector.reciprocal(sr[0:nt, i:i + 1], ssum[0:nt, i:i + 1]).then_inc(s_rs, 1)

                    def finish(n):
                        dve.wait_ge(s_pr, n + 1)
                        for c, rows_c in CH:
                            nc.vector.tensor_scalar(AT[0:rows_c, c, ds(n * SLOT, SEQ)],
                                                    bank[6][0:rows_c, c * SEQ:(c + 1) * SEQ],
                                                    vecs[0:rows_c, V_BP0 + c:V_BP0 + c + 1], None, ALU.add
                                                    ).then_inc(s_at, 1)

                    def sample(n, first, last):
                        if not first:
                            finish(n - 1)
                        dve.wait_ge(s_g, n + 1)
                        for i, (t0, nt) in enumerate(QA_SEGS):
                            nc.vector.tensor_scalar(TT[0:nt, i, :], bank[6][0:nt, i * SEQ:(i + 1) * SEQ],
                                                    alo[0:nt, 3:4], alo[0:nt, 2:3], ALU.mult, ALU.add
                                                    ).then_inc(s_t, 1)
                        dve.wait_ge(s_rs, 2 * n + 2)
                        dve.wait_ge(s_t, 2 * n + 2)
                        for i, (t0, nt) in enumerate(QA_SEGS):
                            nc.vector.scalar_tensor_tensor(WW[0:nt, i, :], ES[0:nt, i, :], sr[0:nt, i:i + 1],
                                                           TT[0:nt, i, :], ALU.mult, ALU.mult).then_inc(s_ww, 1)
                        if not last:
                            softmax(n + 1)
                            dve.wait_ge(s_o, n + 1)
                            evacuate_v(n + 1)

                    nc.vector.memset(AT[:, :, :], 0.0)
                    nc.vector.memset(GW[:, :, :], 0.0)
                    evacuate_v(0)
                    softmax(0)
                    sample(0, True, False)
                    with dve.Fori(0, B - 2) as i:
                        sample(i + 1, False, False)
                    sample(B - 1, False, True)
                    finish(B - 1)

        end_phase()

        def add_to_h(i, psum, dve, s):
            h = H[:, ds(i, 1), :]
            nc.vector.tensor_tensor(h, psum, h, ALU.add).then_inc(s, 1)

        residual_norm(H, add_to_h, True, True, (V_N1L, V_N1S))
        if stop == 2:
            return H

        def heads_attention(ph, cfg):
            def psb(name, shape, dt=F32):
                return ph.enter_context(nc.sbuf_tensor(f"{cfg['name']}_{name}", shape, dt))

            sunits, tunits, kv = cfg["sunits"], cfg["tunits"], cfg["kv"]
            ns, nt = len(sunits), len(tunits)
            width = max(u[5] * u[7] for u in sunits)
            groups = nt // 2
            per_group = ns // groups
            s_ring = (2, 3, 4, 5) if ns % 4 == 2 else (4, 5, 2, 3)
            Q = psb("Q", [HC, 2, SEQ])
            KH = psb("KH", [HC, NR, 2, SEQ])
            V = psb("V", [P, 2, NH, HP])
            W = psb("W", [P, ns, width])
            MX, SM, RS = (psb(x, [P, ns, NR]) for x in ("MX", "SM", "RS"))
            PT = psb("PT", [P, cfg["pt_rows"], NH, SEQ])
            O = psb("O", [P, HB, SEQ])
            scale = float(HD) ** -0.5
            N, RUNS, masks = cfg["count"], cfg["runs"], cfg.get("masks")
            ng, nqk = cfg["finish_ops"], 1 + NR
            (s_set, s_w0, s_w1, s_xb, s_qkp, s_vp, s_qk, s_v, s_sc, s_mx, s_sub, s_ex, s_sm, s_rc, s_nrm, s_tr, s_pt,
             s_pv, s_os, s_out, s_fin) = phase_sem([
                "buffers_set", "weights0_loaded", "weights1_loaded", "sample_loaded", "qk_projected", "v_projected",
                "qk_evacuated", "v_evacuated", "scores", "maxima", "shifted", "exponentials", "sums", "reciprocals",
                "normalised", "weights_transposed", "weights_evacuated", "attended", "attended_evacuated",
                "out_projected", "out_finished"])

            def unit(x, u):
                c, s, q0, nq, k0, nk, r0, nr = sunits[u]
                return x[0:nq, 0:nr * nk].rearrange("p (r k) -> p r k", r=nr)

            def per_query(x, u):
                c, s, q0, nq, k0, nk, r0, nr = sunits[u]
                return x[0:nq, u, 0:nr].unsqueeze(2).broadcast_to([nq, nr, nk])

            def pipelined(eng, sample):
                for run in range(RUNS):
                    sample(run * N, run - 1 if run else None, run, run)
                    with eng.Fori(0, N - 2) as j:
                        sample(j + (run * N + 1), run, run, run)
                    sample(run * N + (N - 1), run, run, run + 1 if run + 1 < RUNS else None)

            LAST = RUNS * N - 1
            with nc.Block() as block:
                @block.sync
                def _(sp):
                    sp.sem_inc(s_vp, 1)
                    for run in range(RUNS):
                        with sp.Fori(0, N) as n:
                            sp.wait_ge(s_vp, n + (run * N + 1))
                            sp.dma_start(XB[:, :, :], XT[:, :, ds((n + cfg["first"](run)) * SLOT, SEQ)]
                                         ).then_inc(s_xb, 16)

                @block.tensor
                def _(pe):
                    def project_qk(g, run):
                        pe.wait_ge(s_xb, g * 16 + 16)
                        for w in range(2):
                            for m in range(2):
                                for c, n in CH:
                                    mm = nc.tensor.matmul(bank[4 + w][0:HC, m * SEQ:(m + 1) * SEQ],
                                                          cfg["w"][run % 2][w][0:n, c, m * HC:(m + 1) * HC], XB[0:n, c, :],
                                                          start=(m == 0 and c == 0), stop=(c == 1),
                                                          skip_group_check=True)
                        mm.then_inc(s_qkp, 1)

                    def project_v(run):
                        order = sorted(range(2), key=lambda i: -kv[i][1])
                        for x, i in enumerate(order):
                            t0, n_t = kv[i]
                            for c, n in CH:
                                mm = nc.tensor.matmul(bank[6][0:n_t, i * C:(i + 1) * C], XB[0:n, c, t0:t0 + n_t],
                                                      cfg["w"][run % 2][2][0:n, c, :], start=(x == 0 and c == 0),
                                                      stop=(c == 1), skip_group_check=True)
                        mm.then_inc(s_vp, 1)

                    def weights_of(run):
                        pe.wait_ge((s_w0, s_w1)[cfg["which"](run)], cfg["loads"](run))

                    def transpose(g, group):
                        for i in (2 * group, 2 * group + 1):
                            h0, row, k0, nk, nr, q0, nq, parts = tunits[i]
                            if i >= 2:
                                pe.wait_ge(s_pt, g * nt + (i - 1))
                            pe.wait_ge(s_nrm, g * ns + (1 + max(p[0] for p in parts)))
                            for u, heads, w0, col, n_q in parts:
                                stride = sunits[u][5]
                                for x, r in enumerate(heads):
                                    tr = nc.tensor.transpose(bank[i % 2][0:nk, r * nq + col:r * nq + col + n_q],
                                                             W[0:n_q, u, x * stride + w0:x * stride + w0 + nk],
                                                             ident[0:n_q, 0:n_q])
                            tr.then_inc(s_tr, 1)

                    def scores(g, group):
                        for u in range(group * per_group, (group + 1) * per_group):
                            c, s, q0, nq, k0, nk, r0, nr = sunits[u]
                            if u >= 4:
                                pe.wait_ge(s_sub, g * ns + (u - 3))
                            dst = bank[s_ring[u % 4]][0:nq, 0:nr * nk]
                            if masks:
                                nc.tensor.matmul(dst, identb[0:nq, 0:nq],
                                                 masks[s][0:nq, 0:nk].unsqueeze(1).broadcast_to([nq, nr, nk]),
                                                 start=True, stop=False, skip_group_check=True)
                            nc.tensor.matmul(dst, Q[:, c, q0:q0 + nq], KH[:, r0:r0 + nr, c, k0:k0 + nk],
                                             start=not masks, stop=True, skip_group_check=True).then_inc(s_sc, 1)

                    def attend(g):
                        pe.wait_ge(s_pt, (g + 1) * nt)
                        pe.wait_ge(s_v, g * 2 + 2)
                        pe.wait_ge(s_fin, (g + 1) * ng)
                        for b in range(HB):
                            for y, (k0, nk, q0, nq, row) in enumerate(cfg["ksegs"]):
                                for r in range(4):
                                    mm = nc.tensor.matmul(
                                        bank[7][HP * r:HP * r + HP, b * SEQ + q0:b * SEQ + q0 + nq],
                                        V[0:nk, kv.index((k0, nk)), 4 * b + r, :], PT[0:nk, row, 4 * b + r, q0:q0 + nq],
                                        start=(b == 0 and y == 0), stop=(y == len(cfg["ksegs"]) - 1),
                                        tile_position=(0, HP * r), skip_group_check=True)
                        mm.then_inc(s_pv, 1)

                    def out_project(g, run):
                        pe.wait_ge(s_os, g + 1)
                        for x, (col, m0, rows_m) in enumerate(cfg["out_tiles"]):
                            for b in range(HB):
                                mm = nc.tensor.matmul(bank[7][0:rows_m, col:col + SEQ],
                                                      cfg["w"][run % 2][3][:, b, m0:m0 + rows_m], O[:, b, :],
                                                      start=(x == 0 and b == 0), stop=(b == HB - 1),
                                                      skip_group_check=True)
                        mm.then_inc(s_out, 1)

                    def sample(g, prev, k, following):
                        pe.wait_ge(s_qk, g * nqk + nqk)
                        if prev is not None:
                            pe.wait_ge(s_sub, g * ns)
                        for group in range(groups):
                            if prev is not None:
                                transpose(g - 1, group)
                            scores(g, group)
                        if prev is not None:
                            attend(g - 1)
                        if following is not None:
                            if following != k:
                                weights_of(following)
                            pe.wait_ge(s_sub, g * ns + (ns - 2))
                            project_qk(g + 1, following)
                            pe.wait_ge(s_v, g * 2 + 2)
                            project_v(following)
                        if prev is not None:
                            out_project(g - 1, prev)

                    pe.wait_ge(s_set, 2)
                    if "also" in cfg:
                        pe.wait_ge(*cfg["also"])
                    weights_of(0)
                    project_qk(0, 0)
                    project_v(0)
                    pipelined(pe, sample)
                    for group in range(groups):
                        transpose(LAST, group)
                    attend(LAST)
                    out_project(LAST, RUNS - 1)

                @block.scalar
                def _(act):
                    def evacuate_qk(g):
                        act.wait_ge(s_qkp, g + 1)
                        nc.scalar.copy(Q[:, :, :], bank[4][0:HC, 0:2 * SEQ]).then_inc(s_qk, 1)
                        for r in range(NR):
                            nc.scalar.activation(KH[:, r, :, :], bank[5][0:HC, 0:2 * SEQ], ACT.Identity,
                                                 scale=vecs[0:HC, V_HEAD + r:V_HEAD + r + 1]).then_inc(s_qk, 1)

                    def evacuate_v(g):
                        act.wait_ge(s_vp, g + 2)
                        for i, (t0, n_t) in enumerate(kv):
                            nc.scalar.copy(V[0:n_t, i, :, 0:HD],
                                           bank[6][0:n_t, i * C:(i + 1) * C].rearrange("p (h d) -> p h d", h=NH)
                                           ).then_inc(s_v, 1)

                    def evacuate_weights(g, group):
                        for i in (2 * group, 2 * group + 1):
                            h0, row, k0, nk, nr, q0, nq, parts = tunits[i]
                            act.wait_ge(s_tr, g * nt + (i + 1))
                            nc.scalar.copy(PT[0:nk, row, h0:h0 + nr, q0:q0 + nq],
                                           bank[i % 2][0:nk, 0:nr * nq].rearrange("p (r q) -> p r q", r=nr)
                                           ).then_inc(s_pt, 1)

                    def evacuate_attended(g):
                        act.wait_ge(s_pv, g + 1)
                        nc.scalar.copy(O[:, :, :], bank[7][:, 0:HB * SEQ]).then_inc(s_os, 1)

                    def sample(g, prev, k, following):
                        for group in range(groups + 1):
                            if prev is not None and group < groups:
                                evacuate_weights(g - 1, group)
                            if group == groups:
                                if prev is not None:
                                    evacuate_attended(g - 1)
                                evacuate_v(g)
                            if group:
                                for u in range((group - 1) * per_group, group * per_group):
                                    act.wait_ge(s_sub, g * ns + (u + 1))
                                    x = unit(W[:, u, :], u)
                                    nc.scalar.activation(x, x, ACT.Exp, scale=scale).then_inc(s_ex, 1)
                        if following is not None:
                            evacuate_qk(g + 1)

                    act.wait_ge(s_set, 2)
                    evacuate_qk(0)
                    pipelined(act, sample)
                    for group in range(groups):
                        evacuate_weights(LAST, group)
                    evacuate_attended(LAST)

                @block.vector
                def _(dve):
                    nc.vector.memset(V[:, :, :, :], 0.0).then_inc(s_set, 1)
                    dve.wait_ge(s_set, 1)
                    dve.sem_inc(s_set, 1)
                    dve.sem_inc(s_fin, ng)

                    def sample(g, prev, k, following):
                        def shift(u):
                            dve.wait_ge(s_mx, g * ns + (u + 1))
                            nc.vector.tensor_tensor(unit(W[:, u, :], u), unit(bank[s_ring[u % 4]], u), per_query(MX, u),
                                                    ALU.subtract).then_inc(s_sub, 1)

                        def reciprocal(u):
                            dve.wait_ge(s_sm, g * ns + (u + 1))
                            nq, nr = sunits[u][3], sunits[u][7]
                            nc.vector.reciprocal(RS[0:nq, u, 0:nr], SM[0:nq, u, 0:nr]).then_inc(s_rc, 1)

                        for u in range(ns):
                            nq, nr = sunits[u][3], sunits[u][7]
                            dve.wait_ge(s_sc, g * ns + (u + 1))
                            nc.vector.tensor_reduce(MX[0:nq, u, 0:nr], unit(bank[s_ring[u % 4]], u), AX.X, ALU.max
                                                    ).then_inc(s_mx, 1)
                            shift(u)
                        for u in range(ns):
                            nq, nr = sunits[u][3], sunits[u][7]
                            dve.wait_ge(s_ex, g * ns + (u + 1))
                            nc.vector.tensor_reduce(SM[0:nq, u, 0:nr], unit(W[:, u, :], u), AX.X, ALU.add
                                                    ).then_inc(s_sm, 1)
                            reciprocal(u)
                        if prev is not None:
                            dve.wait_ge(s_out, g)
                            cfg["finish"](g - 1, prev, bank[7], s_fin)

                    pipelined(dve, sample)
                    dve.wait_ge(s_out, LAST + 1)
                    cfg["finish"](LAST, RUNS - 1, bank[7], s_fin)

                @block.gpsimd
                def _(pool):
                    def sample(g, prev, k, following):
                        for u in range(ns):
                            pool.wait_ge(s_rc, g * ns + (u + 1))
                            x = unit(W[:, u, :], u)
                            nc.gpsimd.tensor_tensor(x, x, per_query(RS, u), ALU.mult).then_inc(s_nrm, 1)

                    for run in range(RUNS):
                        if run < 2:
                            cfg["load"](pool, (s_w0, s_w1)[run % 2], run)
                    for run in range(RUNS):
                        sample(run * N, None, run, run)
                        sample(run * N + 1, run, run, run)
                        if 1 <= run < RUNS - 1:
                            cfg["load"](pool, (s_w0, s_w1)[(run + 1) % 2], run + 1)
                        with pool.Fori(0, N - 2) as j:
                            sample(j + (run * N + 2), run, run, run)

        with ExitStack() as ph:
            def psb(name, shape, dt=F32):
                return ph.enter_context(nc.sbuf_tensor(name, shape, dt))

            fq, fk = psb("f_wq", [P, 2, C]), psb("f_wk", [P, 2, C])
            fv, fp = psb("f_wv", [P, 2, C]), psb("f_wp", [P, HB, C])
            fps = psb("f_wps", [P, HB, C])

            s_fs, = phase_sem(["elastic_weights"])

            def load_f(pool, s_w, run):
                if run:
                    return
                for dst, src in ((fq, "f_q"), (fk, "f_k"), (fv, "f_v"), (fp, "f_proj")):
                    pool.dma_start(dst[:, :, :], d[src]).then_inc(s_w, 16)
                pool.wait_ge(s_w, 64)
                n = 0
                for b, lo, hi, parts in ((0, 0, P, ((0, 64, 2), (64, 96, 1), (96, C, 0))),
                                         (1, 0, 64, ((0, 96, 1), (96, C, 0))), (1, 64, P, ((0, C, 0),)),
                                         (2, 0, P, ((0, C, 0),))):
                    for c0, c1, k in parts:
                        n += 1
                        nc.gpsimd.tensor_scalar(fps[lo:hi, b, c0:c1], fp[lo:hi, b, c0:c1], gs[lo:hi, k:k + 1], None,
                                                ALU.mult).then_inc(s_fs, 1)
                        pool.wait_ge(s_fs, n)

            def finish_f(g, run, psum, s_fin):
                for c, rows_c in CH:
                    bias = vecs[0:rows_c, V_BPL + c:V_BPL + c + 1] if run == 0 else bps[0:rows_c, c:c + 1]
                    nc.vector.tensor_scalar(AT[0:rows_c, c, ds(g * SLOT, SEQ)],
                                            psum[0:rows_c, c * SEQ:(c + 1) * SEQ], bias, None, ALU.add
                                            ).then_inc(s_fin, 1)

            heads_attention(ph, {
                "name": "f", "runs": 2, "count": B // 2, "w": [(fq, fk, fv, fp), (fq, fk, fv, fps)],
                "load": load_f, "loads": lambda run: 64, "which": lambda run: 0, "also": (s_fs, 7), "first": lambda run: run * (B // 2),
                "finish": finish_f, "finish_ops": 2, "out_tiles": ((0, 0, P), (SEQ, P, C1)),
                "kv": list(QA_SEGS), "pt_rows": 2,
                "sunits": [(c, s, q0, nq, 0, SEQ, r0, 3) for c in range(2) for r0 in (0, 3)
                           for s, (q0, nq) in enumerate(QA_SEGS)],
                "tunits": [(3 * j, row, k0, nk, 3, 0, SEQ,
                            [(2 * j + s, range(3), k0, q0, nq) for s, (q0, nq) in enumerate(QA_SEGS)])
                           for j in range(4) for row, (k0, nk) in enumerate(QA_SEGS)],
                "ksegs": [(k0, nk, 0, SEQ, s) for s, (k0, nk) in enumerate(QA_SEGS)],
            })

        end_phase()

        def add_to_xn(i, psum, dve, s):
            x = XN[:, ds(i, 1), :]
            nc.vector.tensor_tensor(x, psum, x, ALU.add).then_inc(s, 1)

        residual_norm(XN, add_to_xn, False, False, (V_N2L, V_N2S))
        if stop == 3:
            return H

        GT_ = 3 * P

        def feed_forward(tag, w1, w2s, hid, s_w, n_w, b1, groups, k_rows, finish, fin_ops, store=None):
            nv = len(k_rows)
            units = nv * HM
            g0, g1 = groups
            (s_up, s_gl, s_dn, s_fn, s_x, s_store) = phase_sem([
                f"{tag}_hidden", f"{tag}_gelu", f"{tag}_down", f"{tag}_finished", f"{tag}_partial", f"{tag}_stored"])
            with nc.Block() as block:
                @block.tensor
                def _(pe):
                    pe.wait_ge(s_w, n_w)
                    with pe.Fori(0, g1 - g0) as g:
                        for m in range(HM):
                            for v, rows_k in enumerate(k_rows):
                                u = m * nv + v
                                if v == 0:
                                    pe.wait_ge(s_gl, g * units + u + nv)
                                chunks = [(c, min(P, rows_k - c * P)) for c in range(2) if rows_k > c * P]
                                for x, (c, n) in enumerate(chunks):
                                    mm = nc.tensor.matmul(bank[u % 6][:, 0:GT_], w1[0:n, c, m * P:(m + 1) * P],
                                                          XT[0:n, c, ds((g + g0) * GT_, GT_)], start=(x == 0),
                                                          stop=(x == len(chunks) - 1))
                                mm.then_inc(s_up, 1)
                        pe.wait_ge(s_gl, (g + 1) * units + 6)
                        for j in range(3):
                            pe.wait_ge(s_fn, g * 3 + (1 if j < 2 else 2))
                            for m in range(HM):
                                for v, w in enumerate(w2s):
                                    n = w.shape[2]
                                    mm = nc.tensor.matmul(bank[6 + j % 2][:, 0:n], hid[:, m * nv + v, j * P:(j + 1) * P],
                                                          w[:, m, :], start=(m == 0 and v == 0),
                                                          stop=(m == HM - 1), skip_group_check=True)
                            mm.then_inc(s_dn, 1)

                @block.scalar
                def _(act):
                    act.sem_inc(s_gl, 6)
                    with act.Fori(0, g1 - g0) as g:
                        for m in range(HM):
                            for v in range(nv):
                                u = m * nv + v
                                act.wait_ge(s_up, g * units + u + 1)
                                nc.scalar.activation(hid[:, u, :], bank[u % 6][:, 0:GT_], ACT.Gelu,
                                                     bias=vecs[:, b1 + m:b1 + m + 1]).then_inc(s_gl, 1)

                @block.vector
                def _(dve):
                    dve.sem_inc(s_fn, 1)
                    with dve.Fori(0, g1 - g0) as g:
                        for j in range(3):
                            dve.wait_ge(s_dn, g * 3 + j + 1)
                            finish(dve, (g + g0) * 3 + j, g * 3 + j, bank[6 + j % 2][:, 0:C], s_x, s_fn)

                if store:
                    @block.sync
                    def _(sp):
                        with sp.Fori(0, g1 - g0) as g:
                            sp.wait_ge(s_fn, g * 3 + 4)
                            sp.dma_start(out.rearrange("(t p) n -> p t n", p=P)[:, ds((g + g0) * 3, 3), :],
                                         H[:, ds((g + g0) * 3, 3), :]).then_inc(s_store, 16)
                        sp.wait_ge(s_store, 16 * (g1 - g0))

        with ExitStack() as ph:
            def psb(name, shape, dt=F32):
                return ph.enter_context(nc.sbuf_tensor(name, shape, dt))

            w1 = psb("m_w1", [P, 2, HID])
            w2 = psb("m_w2", [P, HM, C])
            w2a, w2b, w2c = psb("m_w2a", [P, HM, C]), psb("m_w2b", [P, HM, 96]), psb("m_w2c", [P, HM, 64])
            hid = psb("m_hid", [P, 3 * HM, GT_])
            part = psb("m_part", [P, C])
            s_w, s_wm = phase_sem(["mlp_weights", "mlp_elastic_weights"])
            with nc.Block() as block:
                @block.sync
                def _(sp):
                    sp.dma_start(w1[:, :, :], d["f_w1"]).then_inc(s_w, 16)
                    sp.dma_start(w2[:, :, :], d["f_w2"]).then_inc(s_w, 16)

                @block.vector
                def _(dve):
                    dve.wait_ge(s_w, 32)
                    for k, (w, n) in enumerate(((w2a, C), (w2b, 96), (w2c, 64))):
                        nc.vector.tensor_scalar(w[:, :, :], w2[:, :, 0:n], vecs[:, V_GUM + k:V_GUM + k + 1], None,
                                                ALU.mult).then_inc(s_wm, 1)

            def finish_m(row):
                def finish(dve, tile, count, psum, s_x, s_fn):
                    h = H[:, ds(tile, 1), :].rearrange("p t n -> p (t n)")
                    x = XN[:, ds(tile, 1), :].rearrange("p t n -> p (t n)")
                    nc.vector.tensor_tensor(part[:, :], psum, x, ALU.add).then_inc(s_x, 1)
                    dve.wait_ge(s_x, count * 3 + 1)
                    nc.vector.tensor_tensor(part[:, :], part[:, :], rows[:, row, :], ALU.add).then_inc(s_x, 1)
                    dve.wait_ge(s_x, count * 3 + 2)
                    nc.vector.tensor_tensor(h, part[:, :], h, ALU.add).then_inc(s_x, 1)
                    dve.wait_ge(s_x, count * 3 + 3)
                    dve.sem_inc(s_fn, 1)
                return finish

            feed_forward("wide", w1, (w2,), hid, s_w, 32, V_B1, (0, 3), (C,), finish_m(B2L), 3)
            feed_forward("elastic", w1, (w2a, w2b, w2c), hid, s_w, 32, V_B1, (3, 6), (C, 96, 64), finish_m(B2S), 3)

        end_phase()
        residual_norm(H, None, False, False, None)
        if stop == 4:
            return H

        with ExitStack() as ph:
            def psb(name, shape, dt=F32):
                return ph.enter_context(nc.sbuf_tensor(name, shape, dt))

            GU = psb("e_GU", [P, HB, NTOK])
            gu_w = psb("e_guw", [P, EXPERTS, HB * HB * P])
            with ExitStack() as ph2:
                eo = ph2.enter_context(nc.sbuf_tensor("e_o", [P, EXPERTS, 2 * HB * P], F32))
                eg = ph2.enter_context(nc.sbuf_tensor("e_g", [P, EXPERTS, 2 * 2 * C], F32))
                s_l, s_f, s_c = phase_sem(["fold_loaded", "folded", "fold_evacuated"])
                with nc.Block() as block:
                    @block.sync
                    def _(sp):
                        sp.dma_start(eo[:, :, :], d["e_o"].rearrange("e p c n -> p e (c n)")).then_inc(s_l, 16)
                        sp.dma_start(eg[:, :, :], d["e_gu"].rearrange("e p c n -> p e (c n)")).then_inc(s_l, 16)

                    @block.vector
                    def _(dve):
                        nc.vector.memset(GU[:, :, :], 0.0)

                    @block.tensor
                    def _(pe):
                        pe.wait_ge(s_l, 32)
                        for e in range(EXPERTS):
                            for b in range(HB):
                                u = e * HB + b
                                if u >= 8:
                                    pe.wait_ge(s_c, u - 7)
                                for c, n in CH:
                                    mm = nc.tensor.matmul(bank[u % 8][:, 0:2 * C],
                                                          eo[0:n, e, c * HB * P + b * P:c * HB * P + (b + 1) * P],
                                                          eg[0:n, e, c * 2 * C:(c + 1) * 2 * C],
                                                          start=(c == 0), stop=(c == 1))
                                mm.then_inc(s_f, 1)

                    @block.scalar
                    def _(act):
                        for u in range(EXPERTS * HB):
                            act.wait_ge(s_f, u + 1)
                            nc.scalar.copy(gu_w[:, u // HB, (u % HB) * 2 * C:(u % HB + 1) * 2 * C],
                                           bank[u % 8][:, 0:2 * C]).then_inc(s_c, 1)

            ew = [(psb(f"e_wq{k}", [P, 2, C]), psb(f"e_wk{k}", [P, 2, C]), psb(f"e_wv{k}", [P, 2, C]),
                   psb(f"e_wg{k}", [P, HB, 2 * C])) for k in range(2)]
            mka, mkb = psb("e_mka", [P, 76], BF16), psb("e_mkb", [P, 128], BF16)
            s_m, = phase_sem(["masks"])
            with nc.Block() as block:
                @block.gpsimd
                def _(pool):
                    n = 0
                    for mk, (np_, nf), base, cm in ((mka, (76, 76), 0, 1), (mkb, (65, 128), 63, 1)):
                        n += 1
                        nc.gpsimd.memset(mk[:, :], 0.0).then_inc(s_m, 1)
                        for b_, c_ in ((base, cm), (WIN - 1 - base, -cm)):
                            pool.wait_ge(s_m, n)
                            n += 1
                            nc.gpsimd.affine_select(out=mk[0:np_, :], in_=mk[0:np_, :], compare_op=ALU.is_ge,
                                                    fill=NEG, base=b_, pattern=[[-c_, nf]], channel_multiplier=c_
                                                    ).then_inc(s_m, 1)
                        pool.wait_ge(s_m, n)

            s_free, = phase_sem(["run_through"])

            def load_e(pool, s_w, run):
                if run >= 2:
                    pool.wait_ge(s_free, run - 1)
                for dst, src in zip(ew[run % 2], (d["e_q"][run], d["e_k"][run], d["e_v"][run],
                                                  gu_w[:, run, :].rearrange("p (b n) -> p b n", b=HB))):
                    pool.dma_start(dst[:, :, :], src).then_inc(s_w, 16)

            def finish_e(g, run, psum, s_fin):
                gu = GU[:, :, ds((g - run * B) * SLOT, SEQ)]
                nc.vector.tensor_tensor(gu, psum[:, 0:HB * SEQ].rearrange("p (b q) -> p b q", b=HB), gu, ALU.add
                                        ).then_inc(s_fin, 1)
                if isinstance(g, int) and g == run * B + B - 1:
                    nc.vector.sem_inc(s_free, 1)

            heads_attention(ph, {
                "name": "e", "runs": EXPERTS, "count": B, "w": ew, "load": load_e,
                "loads": lambda run: run // 2 * 64 + 64, "which": lambda run: run % 2, "first": lambda run: 0,
                "finish": finish_e, "finish_ops": 1, "out_tiles": tuple((b * SEQ, b * P, P) for b in range(HB)),
                "kv": [(0, 76), (13, 128)], "masks": (mka, mkb), "pt_rows": 1,
                "sunits": [u for c in range(2) for u in ((c, 0, 0, 76, 0, 76, 0, 6), (c, 1, 76, 65, 13, 128, 0, 3),
                                                         (c, 1, 76, 65, 13, 128, 3, 3))],
                "tunits": [u for c in range(2) for u in (
                    (6 * c, 0, 0, 76, 6, 0, 76, [(3 * c, range(6), 0, 0, 76)]),
                    (6 * c, 0, 13, 128, 6, 76, 65, [(3 * c + 1, range(3), 0, 0, 65), (3 * c + 2, range(3, 6), 0, 0, 65)]))],
                "ksegs": [(0, 76, 0, 76, 0), (13, 128, 76, 65, 0)],
            })

            PARTS = 3
            part_n = NTOK // PARTS
            s_sl, = phase_sem(["silu"])
            with nc.Block() as block:
                @block.scalar
                def _(act):
                    for g in range(PARTS):
                        cols = slice(g * part_n, (g + 1) * part_n)
                        nc.scalar.activation(AT[:, 0, cols], GU[:, 0, cols], ACT.Silu).then_inc(s_sl, 1)
                        nc.scalar.activation(AT[C1:P, 1, cols], GU[0:C1, 1, cols], ACT.Silu).then_inc(s_sl, 1)

                @block.vector
                def _(dve):
                    for g in range(PARTS):
                        cols = slice(g * part_n, (g + 1) * part_n)
                        dve.wait_ge(s_sl, g * 2 + 1)
                        nc.vector.tensor_tensor(AT[:, 0, cols], AT[:, 0, cols], GU[:, 2, cols], ALU.mult)
                        dve.wait_ge(s_sl, g * 2 + 2)
                        nc.vector.tensor_tensor(AT[0:C1, 1, cols], AT[C1:P, 1, cols], GU[C1:P, 1, cols], ALU.mult)

        end_phase()
        residual_norm(H, add_to_h, False, False, None)
        if stop == 5:
            return H

        with ExitStack() as ph:
            def psb(name, shape, dt=F32):
                return ph.enter_context(nc.sbuf_tensor(name, shape, dt))

            w1 = psb("l_w1", [P, 2, HID])
            w2 = psb("l_w2", [P, HM, C])
            hid = psb("l_hid", [P, HM, GT_])
            s_w, = phase_sem(["last_weights"])
            with nc.Block() as block:
                @block.sync
                def _(sp):
                    sp.dma_start(w1[:, :, :], d["g_w1"]).then_inc(s_w, 16)
                    sp.dma_start(w2[:, :, :], d["g_w2"]).then_inc(s_w, 16)

            def finish_l(dve, tile, count, psum, s_x, s_fn):
                h = H[:, ds(tile, 1), :].rearrange("p t n -> p (t n)")
                nc.vector.tensor_tensor(h, psum, h, ALU.add).then_inc(s_fn, 1)

            feed_forward("last", w1, (w2,), hid, s_w, 32, V_FB, (0, 6), (C,), finish_l, 1, store=True)
        end_phase()
        return H


def kernel(**inputs):
    import numpy as np
    import concourse.bacc as bacc
    from concourse.bass_utils import run_bass_kernel_spmd

    arrays = lay_out(**inputs)
    nc = bacc.Bacc("TRN2", target_bir_lowering=False, num_devices=1)
    d = {n: nc.dram_tensor(f"in_{n}_dram", a.shape, mybir.dt.from_np(a.dtype), kind="ExternalInput").ap()
         for n, a in arrays.items()}
    out = nc.dram_tensor("out_0_dram", (NTOK, C), F32, kind="ExternalOutput").ap()
    fusion_kernel(nc, d, out)
    r = run_bass_kernel_spmd(nc, [{f"in_{n}_dram": a for n, a in arrays.items()}], core_ids=[0])
    got = np.asarray(r.results[0]["out_0_dram"])
    return np.ascontiguousarray(got.reshape(B, SLOT, C)[:, :SEQ])


def lay_out(**inputs):
    import numpy as np

    a = {k: np.asarray(v) for k, v in inputs.items()}

    def chunks(w):
        o = np.zeros((2, P, w.shape[1]), np.float32)
        o[0], o[1, :C1] = w[:P], w[P:]
        return np.ascontiguousarray(o.transpose(1, 0, 2))

    def heads_out(w):
        o = np.zeros((w.shape[0], NH, HP), np.float32)
        o[:, :, :HD] = w.reshape(-1, NH, HD)
        return o.reshape(-1, NH * HP)

    def heads_in(w):
        return np.ascontiguousarray(heads_out(w.T).T.reshape(HB, P, -1).transpose(1, 0, 2))

    def blocks(w):
        return np.ascontiguousarray(w.reshape(-1, P, w.shape[1]).transpose(1, 0, 2))

    def cols(v):
        o = np.zeros(-(-v.size // P) * P, np.float32)
        o[:v.size] = v.ravel()
        return o.reshape(-1, P).T

    x = a["x"].reshape(B, 3, 8, 16, 8, 16).transpose(0, 2, 4, 3, 5, 1).reshape(B * NPATCH, PD)
    h0 = np.zeros((B, SLOT, C), np.float32)
    h0[:, NPATCH:SEQ] = a["txt"]
    bqkv = a["L0_attn_b_qkv"]
    head = (np.arange(P)[:, None] // HD == np.arange(NR)).astype(np.float32)
    f = "L0_ffn_"
    vecs = [cols(a["L0_tok_ln1_g"]), cols(a["L0_tok_ln1_b"]), cols(bqkv[:C]), cols(bqkv[C:2 * C]),
            cols(a["L0_attn_b_proj"])]
    for n in ("n1l", "n1s", "n2l", "n2s"):
        vecs += [cols(a[f + n + "_g"]), cols(a[f + n + "_b"])]
    vecs += [cols(a[f + "b_proj"]), cols(a[f + "b_fc1"]), cols(a["L1_ffn_in_bias"]),
             np.repeat(a[f + "gumbel_weights"][None], P, 0), np.repeat(a["L0_attn_alpha"][None], P, 0),
             head]
    vecs = np.concatenate(vecs, 1)
    vecs = np.concatenate([vecs, np.zeros((P, 64 - vecs.shape[1]), np.float32)], 1)
    rows = np.stack([a["L0_tok_ln2_g"], a["L0_tok_ln2_b"], bqkv[2 * C:], a[f + "b_fc2"], a[f + "b_fc2"]])
    r = {
        "patches": x, "h0": h0.reshape(NTOK, C), "tok_w": a["L0_tok_W_proj"], "vecs": vecs,
        "rows": np.repeat(rows[None], P, 0),
        "a0_qkv": chunks(a["L0_attn_W_qkv"]), "a0_proj": chunks(a["L0_attn_W_proj"]), "a0_gp": chunks(a["L0_attn_W_gp"]),
        "f_q": chunks(a[f + "w_qkv"][:, :C]), "f_k": chunks(a[f + "w_qkv"][:, C:2 * C]),
        "f_v": chunks(a[f + "w_qkv"][:, 2 * C:]), "f_proj": heads_in(a[f + "w_proj"]),
        "f_w1": chunks(a[f + "w_fc1"]), "f_w2": blocks(a[f + "w_fc2"]),
        "g_w1": chunks(a["L1_ffn_in_weight"].T), "g_w2": blocks(a["L1_ffn_out_weight"]),
        "e_q": np.stack([chunks(w.T) for w in a["L1_attn_wq"]]),
        "e_k": np.stack([chunks(w.T) for w in a["L1_attn_wk"]]),
        "e_v": np.stack([chunks(w.T) for w in a["L1_attn_wv"]]),
        "e_o": np.stack([chunks(heads_out(w)) for w in a["L1_attn_wo"]]),
        "e_gu": np.stack([chunks(np.concatenate([a["L1_attn_w_gate"][:, cols_e], a["L1_attn_w_up"][P:, cols_e],
                                                 a["L1_attn_w_up"][:P, cols_e]], 0).T)
                          for cols_e in (slice(e * C, (e + 1) * C) for e in range(EXPERTS))]),
    }
    return {k: np.ascontiguousarray(v) for k, v in r.items()}
```

```python
from contextlib import ExitStack

import concourse.bass as bass
from concourse import mybir

F32 = mybir.dt.float32
BF16 = mybir.dt.bfloat16
ALU = mybir.AluOpType
ACT = mybir.ActivationFunctionType
AX = mybir.AxisListType

P = 128
C = 192
C1 = C - P
B, SEQ, NPATCH = 16, 141, 64
SLOT = 144
NTOK = B * SLOT
TILES = NTOK // P
HALF = TILES // 2
PD = 768
PK = PD // P
PT_TILES = B * NPATCH // P
HID = 768
HM = HID // P
NH, HD, HP = 12, 16, 32
HB = NH // 4
EXPERTS = 4
WIN = 64
GP = 49
NR, HC = 6, 96
UH = 3
UNITS = NH // UH + 1
TAIL = SEQ - HP
CH = ((0, P), (1, C1))
QA_SEGS = ((0, 71), (71, 70))
NEG = -1e30


def ds(a, n):
    return bass.ds(a, n)


def fusion_kernel(nc: bass.Bass, d: dict, out: bass.AP, stop: int = 99):
    with ExitStack() as ctx:
        def sb(name, shape, dt=F32):
            return ctx.enter_context(nc.sbuf_tensor(name, shape, dt))

        def sem(name):
            return ctx.enter_context(nc.semaphore(name))

        bank = [ctx.enter_context(nc.psum_tensor(f"bank{i}", [P, 512], F32)) for i in range(8)]

        H = sb("H", [P, TILES, C])
        XN = sb("XN", [P, TILES, C])
        XT = sb("XT", [P, 2, NTOK])
        ident = sb("ident", [P, P])
        identb = sb("identb", [P, P], BF16)
        stats = sb("stats", [P, TILES, 6])
        mean = sb("mean", [P, TILES])
        rstd = sb("rstd", [P, TILES])
        rstd2 = sb("rstd2", [P, TILES])
        tmpa = sb("tmpa", [P, TILES])
        tmpb = sb("tmpb", [P, TILES])
        tmpc = sb("tmpc", [P, TILES])
        nhalf = sb("nhalf", [P, TILES])
        vecs = sb("vecs", [P, 64])
        rows = sb("rows", [P, 5, C])
        LN2G, LN2B, BV0, B2L, B2S = range(5)
        V_LN1G, V_LN1B, V_BQ, V_BK, V_BP0, V_N1L, V_N1S, V_N2L, V_N2S, V_BPL, V_B1, V_FB, V_GUM, V_ALPHA, V_HEAD = \
            0, 6, 12, 14, 16, 18, 22, 26, 30, 34, 36, 42, 48, 51, 52
        gs = sb("gs", [P, 3])
        bps = sb("bps", [P, 2])
        alo = sb("alo", [P, 4])

        XB = sb("XB", [P, 2, SEQ])
        AT = sb("AT", [P, 2, NTOK])

        ph_n = [0]

        open_sems = []

        def phase_sem(names):
            ph_n[0] += 1
            got = [nc.alloc_semaphore(name=f"{x}_{ph_n[0]}") for x in names]
            open_sems.extend(got)
            return got

        def end_phase():
            nc.clear_and_free_semaphores(list(open_sems))
            open_sems.clear()
            nc.all_engine_barrier()

        s_vec, s_const, s_zero, s_vstep = (sem(x) for x in ("vectors_loaded", "constants_ready", "zeroed", "vector_step"))
        with nc.Block() as block:
            @block.sync
            def _(sp):
                sp.dma_start(vecs[:, :], d["vecs"]).then_inc(s_vec, 16)
                sp.dma_start(rows[:, :, :], d["rows"]).then_inc(s_vec, 16)

            @block.gpsimd
            def _(pool):
                nc.gpsimd.memset(ident[:, :], 0.0).then_inc(s_zero, 1)
                pool.wait_ge(s_zero, 1)
                nc.gpsimd.affine_select(out=ident[:, :], in_=ident[:, :], compare_op=ALU.not_equal, fill=1.0,
                                        base=0, pattern=[[-1, P]], channel_multiplier=1).then_inc(s_const, 1)

            @block.vector
            def _(dve):
                nc.vector.memset(XT[C1:P, 1, :], 0.0)
                nc.vector.memset(nhalf[:, :], -0.5)
                dve.wait_ge(s_const, 1)
                nc.vector.tensor_copy(identb[:, :], ident[:, :])
                dve.wait_ge(s_vec, 32)
                nc.vector.tensor_copy(gs[:, 0:1], vecs[:, V_GUM:V_GUM + 1]).then_inc(s_vstep, 1)
                nc.vector.tensor_tensor(gs[:, 1:2], vecs[:, V_GUM:V_GUM + 1], vecs[:, V_GUM + 1:V_GUM + 2],
                                        ALU.add).then_inc(s_vstep, 1)
                dve.wait_ge(s_vstep, 2)
                nc.vector.tensor_tensor(gs[:, 2:3], gs[:, 1:2], vecs[:, V_GUM + 2:V_GUM + 3],
                                        ALU.add).then_inc(s_vstep, 1)
                dve.wait_ge(s_vstep, 3)
                for a, b, k in ((0, 64, 2), (64, 96, 1), (96, 128, 0)):
                    nc.vector.tensor_tensor(bps[a:b, 0:1], vecs[a:b, V_BPL:V_BPL + 1], gs[a:b, k:k + 1], ALU.mult)
                nc.vector.tensor_tensor(bps[0:C1, 1:2], vecs[0:C1, V_BPL + 1:V_BPL + 2], gs[0:C1, 0:1], ALU.mult)
                for a, b, k in ((0, 64, 2), (64, 96, 1), (96, C, 0)):
                    nc.vector.tensor_scalar(rows[:, B2S, a:b], rows[:, B2L, a:b], gs[:, k:k + 1], None, ALU.mult)

            @block.scalar
            def _(act):
                act.wait_ge(s_vec, 32)
                nc.scalar.activation(alo[:, 0:1], vecs[:, V_ALPHA:V_ALPHA + 1], ACT.Exp, scale=-1.0)

        with nc.Block() as block:
            s_a, = phase_sem(["sigmoid_step"])

            @block.vector
            def _(dve):
                nc.vector.tensor_scalar(alo[:, 1:2], alo[:, 0:1], 1.0, None, ALU.add).then_inc(s_a, 1)
                dve.wait_ge(s_a, 1)
                nc.vector.reciprocal(alo[:, 2:3], alo[:, 1:2]).then_inc(s_a, 1)
                dve.wait_ge(s_a, 2)
                nc.vector.tensor_scalar(alo[:, 3:4], alo[:, 2:3], -1.0, 1.0, ALU.mult, ALU.add)

        w_early, w_ffn, w_fold, w_exp, w_last = (sem(f"weights_{x}") for x in ("attention", "ffn", "fold", "experts", "last"))
        early = ctx.enter_context(ExitStack())

        def esb(name, shape):
            return early.enter_context(nc.sbuf_tensor(name, shape, F32))

        a_wqkv, a_wproj, a_wgp = esb("a0_wqkv", [P, 2, 3 * C]), esb("a0_wproj", [P, 2, C]), esb("a0_wgp", [P, 2, GP])
        f_wq, f_wk, f_wv, f_wp = esb("f_wq", [P, 2, C]), esb("f_wk", [P, 2, C]), esb("f_wv", [P, 2, C]), esb("f_wp", [P, HB, C])

        with ExitStack() as ph:
            def psb(name, shape, dt=F32):
                return ph.enter_context(nc.sbuf_tensor(name, shape, dt))

            xp = psb("xp", [P, PT_TILES, PD])
            tokw = psb("tokw", [P, PK, C])
            tokws = psb("tokws", [P, PK, C])
            bnp = psb("bnp", [P, PT_TILES, 12])
            mvp = psb("mvp", [P, PT_TILES, 2])
            ve = psb("ve", [P, PT_TILES])
            rp = psb("rp", [P, PT_TILES])
            bny = psb("bny", [P, PT_TILES, 6])
            mvy = psb("mvy", [P, PT_TILES, 2])
            vy = psb("vy", [P, PT_TILES])
            ry = psb("ry", [P, PT_TILES])
            xpt = [psb(f"xpt{i}", [P, PK, P]) for i in range(2)]
            xpn = [psb(f"xpn{i}", [P, PD]) for i in range(4)]
            brow = psb("brow", [1, C])
            one1 = psb("one1", [1, P])
            Y = psb("Y", [P, PT_TILES, C])
            PAIRS = PT_TILES // 2
            s_p = phase_sem([f"patches_loaded{q}" for q in range(PAIRS)])
            (s_w, s_h, s_bn, s_mv, s_ve, s_rp, s_fm, s_bd, s_bc, s_nrm, s_tr, s_ev, s_mm, s_ybn, s_ymv, s_yve, s_ry,
             s_yg, s_yo, s_hd, s_one) = phase_sem([
                "tok_weights", "text_loaded", "patch_stats", "patch_meanvar", "patch_variance", "patch_rstd",
                "tok_scaled", "bias_product", "bias_row", "patch_normed", "patch_transposed", "patch_evacuated",
                "embedded", "embed_stats", "embed_meanvar", "embed_variance", "embed_rstd", "embed_scaled",
                "embed_done", "embed_placed", "tok_ones"])
            with nc.Block() as block:
                def patch_rows(eng, sample):
                    y0, row = sample % 2 * NPATCH, sample * SLOT
                    done, n = 0, 0
                    while done < NPATCH:
                        p0 = (row + done) % P
                        rows_n = min(NPATCH - done, P - p0)
                        eng.dma_start(H[p0:p0 + rows_n, (row + done) // P, :],
                                      Y[y0 + done:y0 + done + rows_n, sample // 2, :]).then_inc(s_hd, 16)
                        done += rows_n
                        n += 1
                    return n

                @block.sync
                def _(sp):
                    sp.dma_start(tokw[:, :, :], d["tok_w"].rearrange("(k p) n -> p k n", p=P)).then_inc(s_w, 16)
                    for q in range(PAIRS):
                        sp.dma_start(xp[:, 2 * q:2 * q + 2, :],
                                     d["patches"].rearrange("(t p) n -> p t n", p=P)[:, 2 * q:2 * q + 2, :]
                                     ).then_inc(s_p[q], 16)
                    sp.dma_start(H[:, :, :], d["h0"].rearrange("(t p) n -> p t n", p=P)).then_inc(s_h, 16)
                    for dst, src in ((a_wqkv, "a0_qkv"), (a_wproj, "a0_proj"), (a_wgp, "a0_gp"), (f_wq, "f_q"),
                                     (f_wk, "f_k"), (f_wv, "f_v"), (f_wp, "f_proj")):
                        sp.dma_start(dst[:, :, :], d[src]).then_inc(w_early, 16)
                    sp.wait_ge(s_h, 16)
                    n = 0
                    for t in range(PT_TILES):
                        sp.wait_ge(s_yo, t + 1)
                        for k in range(2):
                            n += patch_rows(sp, 2 * t + k)
                    sp.wait_ge(s_hd, 16 * n)

                @block.vector
                def _(dve):
                    def stats(q):
                        dve.wait_ge(s_p[q], 16)
                        for t in (2 * q, 2 * q + 1):
                            for k in range(2):
                                nc.vector.bn_stats(bnp[:, t, 6 * k:6 * k + 6], xp[:, t, k * 384:(k + 1) * 384]
                                                   ).then_inc(s_bn, 1)
                        dve.wait_ge(s_bn, 4 * q + 4)
                        for t in (2 * q, 2 * q + 1):
                            nc.vector.bn_aggr(mvp[:, t, :], bnp[:, t, :]).then_inc(s_mv, 1)
                        dve.wait_ge(s_mv, 2 * q + 2)
                        nc.vector.tensor_scalar(ve[:, 2 * q:2 * q + 2], mvp[:, 2 * q:2 * q + 2, 1], 1e-6, None, ALU.add
                                                ).then_inc(s_ve, 1)

                    def norm(q):
                        dve.wait_ge(s_rp, q + 1)
                        for t in (2 * q, 2 * q + 1):
                            if t >= 4:
                                dve.wait_ge(s_tr, t - 3)
                            nc.vector.tensor_scalar(xpn[t % 4][:, :], xp[:, t, :], mvp[:, t, 0:1], rp[:, t:t + 1],
                                                    ALU.subtract, ALU.mult).then_inc(s_nrm, 1)

                    def norm_embedded(q):
                        for t in (2 * q, 2 * q + 1):
                            dve.wait_ge(s_mm, t + 1)
                            nc.vector.bn_stats(bny[:, t, :], bank[4 + t % 4][:, 0:C]).then_inc(s_ybn, 1)
                        dve.wait_ge(s_ybn, 2 * q + 2)
                        for t in (2 * q, 2 * q + 1):
                            nc.vector.bn_aggr(mvy[:, t, :], bny[:, t, :]).then_inc(s_ymv, 1)
                        dve.wait_ge(s_ymv, 2 * q + 2)
                        nc.vector.tensor_scalar(vy[:, 2 * q:2 * q + 2], mvy[:, 2 * q:2 * q + 2, 1], 1e-6, None, ALU.add
                                                ).then_inc(s_yve, 1)
                        for t in (2 * q, 2 * q + 1):
                            nc.vector.scalar_tensor_tensor(Y[:, t, :], bank[4 + t % 4][:, 0:C], mvy[:, t, 0:1],
                                                           rows[:, LN2G, :], ALU.subtract, ALU.mult).then_inc(s_yg, 1)
                        dve.wait_ge(s_ry, q + 1)
                        for t in (2 * q, 2 * q + 1):
                            dve.wait_ge(s_yg, t + 1)
                            nc.vector.scalar_tensor_tensor(Y[:, t, :], Y[:, t, :], ry[:, t:t + 1], rows[:, LN2B, :],
                                                           ALU.mult, ALU.add).then_inc(s_yo, 1)

                    nc.vector.memset(one1[:, :], 1.0).then_inc(s_one, 1)
                    dve.wait_ge(s_w, 16)
                    for k in range(PK):
                        nc.vector.tensor_scalar(tokws[:, k, :], tokw[:, k, :], vecs[:, V_LN1G + k:V_LN1G + k + 1],
                                                None, ALU.mult).then_inc(s_fm, 1)
                    stats(0)
                    for q in range(1, PAIRS):
                        stats(q)
                        norm(q - 1)
                    norm_embedded(0)
                    norm(PAIRS - 1)
                    for q in range(1, PAIRS):
                        norm_embedded(q)

                @block.gpsimd
                def _(pool):
                    def patches(q):
                        pool.wait_ge(s_ve, q + 1)
                        nc.gpsimd.tensor_tensor(rp[:, 2 * q:2 * q + 2], ve[:, 2 * q:2 * q + 2], nhalf[:, 0:2], ALU.pow
                                                ).then_inc(s_rp, 1)

                    def embedded(q):
                        pool.wait_ge(s_yve, q + 1)
                        nc.gpsimd.tensor_tensor(ry[:, 2 * q:2 * q + 2], vy[:, 2 * q:2 * q + 2], nhalf[:, 0:2], ALU.pow
                                                ).then_inc(s_ry, 1)

                    for q in range(PAIRS):
                        patches(q)
                    for q in range(PAIRS):
                        embedded(q)

                @block.tensor
                def _(pe):
                    def transpose(t):
                        pe.wait_ge(s_nrm, t + 1)
                        if t >= 2:
                            pe.wait_ge(s_ev, 2 * t - 2)
                        for j in range(PK):
                            tr = nc.tensor.transpose(bank[2 * (t % 2) + j // 4][:, (j % 4) * P:(j % 4 + 1) * P],
                                                     xpn[t % 4][:, j * P:(j + 1) * P], ident[:, :])
                        tr.then_inc(s_tr, 1)

                    def embed(t):
                        pe.wait_ge(s_ev, 2 * t + 2)
                        if t >= 4:
                            pe.wait_ge(s_yg, t - 3)
                        for j in range(PK):
                            nc.tensor.matmul(bank[4 + t % 4][:, 0:C], xpt[t % 2][:, j, :], tokws[:, j, :],
                                             start=(j == 0), stop=False)
                        nc.tensor.matmul(bank[4 + t % 4][:, 0:C], one1[:, :], brow[:, :], start=False,
                                         stop=True).then_inc(s_mm, 1)

                    pe.wait_ge(s_w, 16)
                    for k in range(PK):
                        mm = nc.tensor.matmul(bank[7][0:1, 0:C], vecs[:, V_LN1B + k:V_LN1B + k + 1], tokw[:, k, :],
                                              start=(k == 0), stop=(k == PK - 1))
                    mm.then_inc(s_bd, 1)
                    pe.wait_ge(s_fm, PK)
                    pe.wait_ge(s_bc, 1)
                    pe.wait_ge(s_one, 1)
                    transpose(0)
                    for t in range(PT_TILES):
                        if t + 1 < PT_TILES:
                            transpose(t + 1)
                        embed(t)

                @block.scalar
                def _(act):
                    act.wait_ge(s_bd, 1)
                    nc.scalar.copy(brow[:, :], bank[7][0:1, 0:C]).then_inc(s_bc, 1)
                    for t in range(PT_TILES):
                        act.wait_ge(s_tr, t + 1)
                        if t >= 2:
                            act.wait_ge(s_mm, t - 1)
                        nc.scalar.copy(xpt[t % 2][:, 0:4, :], bank[2 * (t % 2)][:, 0:512]).then_inc(s_ev, 1)
                        nc.scalar.copy(xpt[t % 2][:, 4:6, :], bank[2 * (t % 2) + 1][:, 0:256]).then_inc(s_ev, 1)

        end_phase()
        if stop == 0:
            return H

        NG = 6

        def residual_norm(src, finish, save, twice, affine, beside=None):
            beside = beside or {}
            (s_t, s_r, s_bn, s_x, s_ps, s_pw, s_n, s_tr, s_e) = phase_sem([
                "back_transposed", "residual_added", "norm_stats", "norm_step", "pow_step", "norm_pow", "normed",
                "norm_transposed", "norm_evacuated"])
            STEPS = 7
            with ExitStack() as ph:
                xn = [ph.enter_context(nc.sbuf_tensor(f"xn{i}_{ph_n[0]}", [P, C], F32)) for i in range(NG)]
                with nc.Block() as block:
                    @block.sync
                    def _(sp):
                        if "sync" in beside:
                            beside["sync"](sp)

                    @block.vector
                    def _(dve):
                        if "vector" in beside:
                            beside["vector"](dve)
                        with dve.Fori(0, TILES // NG) as g:
                            for j in range(0, NG, 2):
                                if finish:
                                    for k in (j, j + 1):
                                        dve.wait_ge(s_t, g * NG + (k + 1))
                                        finish(g * NG + k, bank[k][:, 0:C], dve, s_r)
                                for k in (j, j + 1):
                                    if finish:
                                        dve.wait_ge(s_r, g * NG + (k + 1))
                                    nc.vector.bn_stats(stats[:, ds(g * NG + k, 1), :], src[:, ds(g * NG + k, 1), :]
                                                       ).then_inc(s_bn, 1)
                            dve.wait_ge(s_bn, g * NG + NG)
                            n = [0]

                            def step(ins):
                                n[0] += 1
                                ins.then_inc(s_x, 1)
                                if n[0] < STEPS:
                                    dve.wait_ge(s_x, g * STEPS + n[0])

                            st = stats[:, ds(g * NG, NG), :]
                            ta, tb, tc, tm = (x[:, ds(g * NG, NG)] for x in (tmpa, tmpb, tmpc, mean))
                            step(nc.vector.tensor_tensor(ta, st[:, :, 1], st[:, :, 4], ALU.add))
                            step(nc.vector.tensor_scalar(tm, ta, 0.5, None, ALU.mult))
                            step(nc.vector.tensor_tensor(ta, st[:, :, 1], st[:, :, 4], ALU.subtract))
                            step(nc.vector.scalar_tensor_tensor(tb, ta, 0.25, ta, ALU.mult, ALU.mult))
                            step(nc.vector.tensor_tensor(ta, st[:, :, 2], st[:, :, 5], ALU.add))
                            step(nc.vector.scalar_tensor_tensor(ta, ta, 1.0 / C, tb, ALU.mult, ALU.add))
                            step(nc.vector.tensor_scalar(tc, ta, 1e-5, None, ALU.add))
                        r = rstd2 if twice else rstd
                        with dve.Fori(0, TILES // NG) as g:
                            dve.wait_ge(s_pw, g + 1)
                            for k in range(NG):
                                i = g * NG + k
                                t = src[:, ds(i, 1), :].rearrange("p t n -> p (t n)")
                                if save:
                                    nc.vector.tensor_scalar(XN[:, ds(i, 1), :].rearrange("p t n -> p (t n)"), t,
                                                            mean[:, ds(i, 1)], rstd[:, ds(i, 1)],
                                                            ALU.subtract, ALU.mult)
                                dve.wait_ge(s_e, g * NG + (k + 1))
                                nc.vector.tensor_scalar(xn[k][:, :], t, mean[:, ds(i, 1)], r[:, ds(i, 1)],
                                                        ALU.subtract, ALU.mult).then_inc(s_n, 1)

                    @block.gpsimd
                    def _(pool):
                        n = [0]

                        def step(ins):
                            n[0] += 1
                            ins.then_inc(s_ps, 1)
                            pool.wait_ge(s_ps, n[0])

                        for g in range(TILES // NG):
                            r, r2, v, ve, t, ex = (x[:, g * NG:(g + 1) * NG]
                                                   for x in (rstd, rstd2, tmpa, tmpc, tmpb, nhalf))
                            pool.wait_ge(s_x, STEPS * (g + 1))
                            ins = nc.gpsimd.tensor_tensor(r, ve, ex, ALU.pow)
                            if twice:
                                step(ins)
                                step(nc.gpsimd.tensor_tensor(t, v, r, ALU.mult))
                                step(nc.gpsimd.tensor_tensor(t, t, r, ALU.mult))
                                step(nc.gpsimd.tensor_scalar(t, t, 1e-5, None, ALU.add))
                                step(nc.gpsimd.tensor_tensor(t, t, ex, ALU.pow))
                                ins = nc.gpsimd.tensor_tensor(r2, t, r, ALU.mult)
                            ins.then_inc(s_pw, 1)
                        if "gpsimd_after" in beside:
                            beside["gpsimd_after"](pool)

                    @block.tensor
                    def _(pe):
                        if "tensor" in beside:
                            beside["tensor"](pe)
                        if finish:
                            for i in range(TILES):
                                if i >= NG:
                                    pe.wait_ge(s_r, i - NG + 1)
                                nc.tensor.transpose(bank[i % NG][:, 0:P], AT[:, 0, i * P:(i + 1) * P], ident[:, :])
                                nc.tensor.transpose(bank[i % NG][:, P:C], AT[0:C1, 1, i * P:(i + 1) * P],
                                                    ident[0:C1, 0:C1]).then_inc(s_t, 1)
                        with pe.Fori(0, TILES // NG) as g:
                            for k in range(NG):
                                pe.wait_ge(s_n, g * NG + (k + 1))
                                nc.tensor.transpose(bank[k][:, 0:P], xn[k][:, 0:P], ident[:, :])
                                nc.tensor.transpose(bank[k][0:C1, P:2 * P], xn[k][:, P:C], ident[:, :]
                                                    ).then_inc(s_tr, 1)

                    @block.scalar
                    def _(act):
                        if "scalar" in beside:
                            beside["scalar"](act)
                        act.sem_inc(s_e, NG)
                        for i in range(TILES):
                            act.wait_ge(s_tr, i + 1)
                            for c, n in CH:
                                src_ps = bank[i % NG][0:n, c * P:(c + 1) * P]
                                dst = XT[0:n, c, i * P:(i + 1) * P]
                                if affine:
                                    v = affine[i // HALF] + c
                                    ins = nc.scalar.activation(dst, src_ps, ACT.Identity, scale=vecs[0:n, v:v + 1],
                                                               bias=vecs[0:n, v + 2:v + 3])
                                else:
                                    ins = nc.scalar.copy(dst, src_ps)
                            ins.then_inc(s_e, 1)
            end_phase()

        def load_samples(sp, s_xb, s_used, first, count):
            sp.dma_start(XB[:, :, :], XT[:, :, first * SLOT:first * SLOT + SEQ]).then_inc(s_xb, 16)
            with sp.Fori(0, count - 1) as n:
                sp.wait_ge(s_used, n + 1)
                sp.dma_start(XB[:, :, :], XT[:, :, ds((n + 1 + first) * SLOT, SEQ)]).then_inc(s_xb, 16)

        residual_norm(H, None, False, False, None)
        with ExitStack() as ph:
            def psb(name, shape, dt=F32):
                return ph.enter_context(nc.sbuf_tensor(name, shape, dt))

            wqkv, wproj, wgp = a_wqkv, a_wproj, a_wgp
            QK = psb("a0_QK", [P, 2, 2, SEQ])
            V = psb("a0_V", [P, 2, C])
            gneg, gsum, gr, smax, sneg, ssum, sr = (psb(f"a0_{x}", [P, 2]) for x in
                                                    ("gneg", "gsum", "gr", "smax", "sneg", "ssum", "sr"))
            EG = psb("a0_EG", [P, 2, GP])
            GW = psb("a0_GW", [P, 2, P])
            GT = psb("a0_GT", [GP, SEQ])
            ES = psb("a0_ES", [P, 2, SEQ])
            TT = psb("a0_TT", [P, 2, SEQ])
            WW = psb("a0_WW", [P, 2, SEQ])
            WT = psb("a0_WT", [P, 2, SEQ])
            OT = psb("a0_OT", [P, 2, SEQ])
            scale = float(C) ** -0.5
            (s_xb, s_qkp, s_qkv, s_qk, s_v, s_lg, s_s, s_gm, s_sm0, s_sm, s_eg, s_es, s_rg, s_gw, s_rs, s_gt, s_gte,
             s_g, s_t, s_ww, s_wt, s_wte, s_o, s_ot, s_pr, s_at) = phase_sem([
                "sample_loaded", "qk_projected", "projected", "qk_evacuated", "v_evacuated", "group_logits", "scores",
                "group_max", "score_max", "score_shift", "group_exp", "score_exp", "group_recip", "group_weights",
                "score_recip", "group_transposed", "group_evacuated", "group_product", "mix", "weighted",
                "weights_transposed", "weights_evacuated", "attended", "attended_evacuated", "out_projected",
                "out_evacuated"])
            with nc.Block() as block:
                @block.sync
                def _(sp):
                    load_samples(sp, s_xb, s_qkv, 0, B)

                @block.tensor
                def _(pe):
                    def project_qk(n):
                        pe.wait_ge(s_xb, 16 * n + 16)
                        for w in range(2):
                            for m, rows_m in CH:
                                for c, rows_c in CH:
                                    mm = nc.tensor.matmul(bank[w][0:rows_m, m * SEQ:(m + 1) * SEQ],
                                                          wqkv[0:rows_c, c, w * C + m * P:w * C + m * P + rows_m],
                                                          XB[0:rows_c, c, :], start=(m == 0 and c == 0), stop=(c == 1),
                                                          skip_group_check=True)
                        mm.then_inc(s_qkp, 1)

                    def project_v(n):
                        for i, (t0, nt) in enumerate(QA_SEGS):
                            for c, rows_c in CH:
                                mm = nc.tensor.matmul(bank[2][0:nt, i * C:(i + 1) * C], XB[0:rows_c, c, t0:t0 + nt],
                                                      wqkv[0:rows_c, c, 2 * C:3 * C], start=(i == 0 and c == 0),
                                                      stop=(c == 1), skip_group_check=True)
                        mm.then_inc(s_qkv, 1)

                    def scores(n):
                        pe.wait_ge(s_qk, 4 * n + 4)
                        for i, (t0, nt) in enumerate(QA_SEGS):
                            for c, rows_c in CH:
                                mm = nc.tensor.matmul(bank[3][0:nt, i * GP:(i + 1) * GP],
                                                      QK[0:rows_c, 0, c, t0:t0 + nt], wgp[0:rows_c, c, :],
                                                      start=(i == 0 and c == 0), stop=(c == 1), skip_group_check=True)
                        mm.then_inc(s_lg, 1)
                        for i, (t0, nt) in enumerate(QA_SEGS):
                            for c, rows_c in CH:
                                mm = nc.tensor.matmul(bank[4][0:nt, i * SEQ:(i + 1) * SEQ],
                                                      QK[0:rows_c, 0, c, t0:t0 + nt], QK[0:rows_c, 1, c, :],
                                                      start=(i == 0 and c == 0), stop=(c == 1), skip_group_check=True)
                        mm.then_inc(s_s, 1)

                    def out_project(n):
                        pe.wait_ge(s_ot, 2 * n + 2)
                        for m, rows_m in CH:
                            for c, rows_c in CH:
                                mm = nc.tensor.matmul(bank[6][0:rows_m, m * SEQ:(m + 1) * SEQ],
                                                      wproj[0:rows_c, c, m * P:m * P + rows_m], OT[0:rows_c, c, :],
                                                      start=(m == 0 and c == 0), stop=(c == 1), skip_group_check=True)
                        mm.then_inc(s_pr, 1)

                    def sample(n, first, last):
                        pe.wait_ge(s_gw, 2 * n + 2)
                        for i, (t0, nt) in enumerate(QA_SEGS):
                            tr = nc.tensor.transpose(bank[7][:, 2 * SEQ + t0:2 * SEQ + t0 + nt], GW[0:nt, i, :],
                                                     ident[0:nt, 0:nt])
                        tr.then_inc(s_gt, 1)
                        if not first:
                            out_project(n - 1)
                        if not last:
                            project_qk(n + 1)
                        pe.wait_ge(s_gte, n + 1)
                        if not first:
                            pe.wait_ge(s_at, 2 * n)
                        for i, (t0, nt) in enumerate(QA_SEGS):
                            mm = nc.tensor.matmul(bank[6][0:nt, i * SEQ:(i + 1) * SEQ], GT[:, t0:t0 + nt], GT[:, :],
                                                  start=(i == 0), stop=True, skip_group_check=True)
                        mm.then_inc(s_g, 1)
                        if not last:
                            pe.wait_ge(s_v, 2 * n + 2)
                            project_v(n + 1)
                        pe.wait_ge(s_ww, 2 * n + 2)
                        for i, (q0, nq) in enumerate(QA_SEGS):
                            for j, (k0, nk) in enumerate(QA_SEGS):
                                tr = nc.tensor.transpose(bank[7][0:nk, j * SEQ + q0:j * SEQ + q0 + nq],
                                                         WW[0:nq, i, k0:k0 + nk], ident[0:nq, 0:nq])
                        tr.then_inc(s_wt, 1)
                        if not last:
                            scores(n + 1)
                        pe.wait_ge(s_wte, 2 * n + 2)
                        pe.wait_ge(s_v, 2 * n + 2)
                        for m, rows_m in CH:
                            for j, (k0, nk) in enumerate(QA_SEGS):
                                mm = nc.tensor.matmul(bank[5][0:rows_m, m * SEQ:(m + 1) * SEQ],
                                                      V[0:nk, j, m * P:m * P + rows_m], WT[0:nk, j, :],
                                                      start=(m == 0 and j == 0), stop=(j == 1), skip_group_check=True)
                        mm.then_inc(s_o, 1)

                    pe.wait_ge(w_early, 7 * 16)
                    project_qk(0)
                    project_v(0)
                    scores(0)
                    sample(0, True, False)
                    with pe.Fori(0, B - 2) as i:
                        sample(i + 1, False, False)
                    sample(B - 1, False, True)
                    out_project(B - 1)

                @block.scalar
                def _(act):
                    def evacuate_qk(n):
                        act.wait_ge(s_qkp, n + 1)
                        for w, vb in ((0, V_BQ), (1, V_BK)):
                            for c, rows_c in CH:
                                nc.scalar.activation(QK[0:rows_c, w, c, :], bank[w][0:rows_c, c * SEQ:(c + 1) * SEQ],
                                                     ACT.Identity, bias=vecs[0:rows_c, vb + c:vb + c + 1]
                                                     ).then_inc(s_qk, 1)

                    def exponentials(n):
                        act.wait_ge(s_gm, 2 * n + 2)
                        for i, (t0, nt) in enumerate(QA_SEGS):
                            nc.scalar.activation(EG[0:nt, i, :], bank[3][0:nt, i * GP:(i + 1) * GP], ACT.Exp,
                                                 bias=gneg[0:nt, i:i + 1], accum_out=gsum[0:nt, i:i + 1]
                                                 ).then_inc(s_eg, 1)
                        act.wait_ge(s_sm, 2 * n + 2)
                        for i, (t0, nt) in enumerate(QA_SEGS):
                            nc.scalar.activation(ES[0:nt, i, :], bank[4][0:nt, i * SEQ:(i + 1) * SEQ], ACT.Exp,
                                                 bias=sneg[0:nt, i:i + 1], scale=scale, accum_out=ssum[0:nt, i:i + 1]
                                                 ).then_inc(s_es, 1)

                    def sample(n, last):
                        act.wait_ge(s_gt, n + 1)
                        nc.scalar.copy(GT[:, :], bank[7][0:GP, 2 * SEQ:3 * SEQ]).then_inc(s_gte, 1)
                        if not last:
                            evacuate_qk(n + 1)
                        act.wait_ge(s_wt, n + 1)
                        for j, (k0, nk) in enumerate(QA_SEGS):
                            nc.scalar.copy(WT[0:nk, j, :], bank[7][0:nk, j * SEQ:(j + 1) * SEQ]).then_inc(s_wte, 1)
                        if not last:
                            exponentials(n + 1)
                        act.wait_ge(s_o, n + 1)
                        for c, rows_c in CH:
                            nc.scalar.copy(OT[0:rows_c, c, :], bank[5][0:rows_c, c * SEQ:(c + 1) * SEQ]
                                           ).then_inc(s_ot, 1)

                    evacuate_qk(0)
                    exponentials(0)
                    with act.Fori(0, B - 1) as n:
                        sample(n, False)
                    sample(B - 1, True)

                @block.vector
                def _(dve):
                    def evacuate_v(n):
                        dve.wait_ge(s_qkv, n + 1)
                        for i, (t0, nt) in enumerate(QA_SEGS):
                            nc.vector.tensor_tensor(V[0:nt, i, :], bank[2][0:nt, i * C:(i + 1) * C],
                                                    rows[0:nt, BV0, :], ALU.add).then_inc(s_v, 1)

                    def softmax(n):
                        dve.wait_ge(s_lg, n + 1)
                        for i, (t0, nt) in enumerate(QA_SEGS):
                            nc.vector.tensor_reduce(gneg[0:nt, i:i + 1], bank[3][0:nt, i * GP:(i + 1) * GP], AX.X,
                                                    ALU.max, negate=True).then_inc(s_gm, 1)
                        dve.wait_ge(s_s, n + 1)
                        for i, (t0, nt) in enumerate(QA_SEGS):
                            nc.vector.tensor_reduce(smax[0:nt, i:i + 1], bank[4][0:nt, i * SEQ:(i + 1) * SEQ], AX.X,
                                                    ALU.max).then_inc(s_sm0, 1)
                        dve.wait_ge(s_sm0, 2 * n + 2)
                        for i, (t0, nt) in enumerate(QA_SEGS):
                            nc.vector.tensor_scalar(sneg[0:nt, i:i + 1], smax[0:nt, i:i + 1], -scale, None, ALU.mult
                                                    ).then_inc(s_sm, 1)
                        dve.wait_ge(s_eg, 2 * n + 2)
                        for i, (t0, nt) in enumerate(QA_SEGS):
                            nc.vector.reciprocal(gr[0:nt, i:i + 1], gsum[0:nt, i:i + 1]).then_inc(s_rg, 1)
                        dve.wait_ge(s_rg, 2 * n + 2)
                        for i, (t0, nt) in enumerate(QA_SEGS):
                            nc.vector.tensor_scalar(GW[0:nt, i, 0:GP], EG[0:nt, i, :], gr[0:nt, i:i + 1], None, ALU.mult
                                                    ).then_inc(s_gw, 1)
                        dve.wait_ge(s_es, 2 * n + 2)
                        for i, (t0, nt) in enumerate(QA_SEGS):
                            nc.vector.reciprocal(sr[0:nt, i:i + 1], ssum[0:nt, i:i + 1]).then_inc(s_rs, 1)

                    def finish(n):
                        dve.wait_ge(s_pr, n + 1)
                        for c, rows_c in CH:
                            nc.vector.tensor_scalar(AT[0:rows_c, c, ds(n * SLOT, SEQ)],
                                                    bank[6][0:rows_c, c * SEQ:(c + 1) * SEQ],
                                                    vecs[0:rows_c, V_BP0 + c:V_BP0 + c + 1], None, ALU.add
                                                    ).then_inc(s_at, 1)

                    def sample(n, first, last):
                        if not first:
                            finish(n - 1)
                        dve.wait_ge(s_g, n + 1)
                        for i, (t0, nt) in enumerate(QA_SEGS):
                            nc.vector.tensor_scalar(TT[0:nt, i, :], bank[6][0:nt, i * SEQ:(i + 1) * SEQ],
                                                    alo[0:nt, 3:4], alo[0:nt, 2:3], ALU.mult, ALU.add
                                                    ).then_inc(s_t, 1)
                        dve.wait_ge(s_rs, 2 * n + 2)
                        dve.wait_ge(s_t, 2 * n + 2)
                        for i, (t0, nt) in enumerate(QA_SEGS):
                            nc.vector.scalar_tensor_tensor(WW[0:nt, i, :], ES[0:nt, i, :], sr[0:nt, i:i + 1],
                                                           TT[0:nt, i, :], ALU.mult, ALU.mult).then_inc(s_ww, 1)
                        if not last:
                            softmax(n + 1)
                            dve.wait_ge(s_o, n + 1)
                            evacuate_v(n + 1)

                    nc.vector.memset(AT[:, :, :], 0.0)
                    nc.vector.memset(GW[:, :, :], 0.0)
                    evacuate_v(0)
                    softmax(0)
                    sample(0, True, False)
                    with dve.Fori(0, B - 2) as i:
                        sample(i + 1, False, False)
                    sample(B - 1, False, True)
                    finish(B - 1)

        end_phase()

        def add_to_h(i, psum, dve, s):
            h = H[:, ds(i, 1), :]
            nc.vector.tensor_tensor(h, psum, h, ALU.add).then_inc(s, 1)

        residual_norm(H, add_to_h, True, True, (V_N1L, V_N1S))
        if stop == 2:
            return H

        def heads_attention(ph, cfg):
            def psb(name, shape, dt=F32):
                return ph.enter_context(nc.sbuf_tensor(f"{cfg['name']}_{name}", shape, dt))

            keys, kv, parts = cfg["keys"], cfg["kv"], cfg["parts"]
            ns, nt = UNITS, sum(len(parts[u]) for u in range(UNITS))
            t_of = [[(sum(len(parts[x]) for x in range(u)) + i, *p) for i, p in enumerate(parts[u])]
                    for u in range(UNITS)]
            width = UH * max(n for k, n in keys)
            s_ring = (2, 4, 5, 3)
            Q = psb("Q", [HC, 2, SEQ])
            KH = psb("KH", [HC, NR, 2, SEQ])
            V = psb("V", [P, 2, NH, HP])
            W = psb("W", [P, ns, width])
            MX, SM, RS = (psb(x, [P, ns, UH]) for x in ("MX", "SM", "RS"))
            PT = psb("PT", [P, cfg["pt_rows"], NH, SEQ])
            O = psb("O", [P, HB, SEQ])
            scale = float(HD) ** -0.5
            N, RUNS, masks = cfg["count"], cfg["runs"], cfg.get("masks")
            ng, nqk = cfg["finish_ops"], 1 + NR
            (s_set, s_xb, s_qkp, s_vp, s_qk, s_v, s_sc, s_mx, s_sub, s_ex, s_sm, s_rc, s_nrm, s_tr, s_pt,
             s_pv, s_os, s_out, s_fin) = phase_sem([
                "buffers_set", "sample_loaded", "qk_projected", "v_projected",
                "qk_evacuated", "v_evacuated", "scores", "maxima", "shifted", "exponentials", "sums", "reciprocals",
                "normalised", "weights_transposed", "weights_evacuated", "attended", "attended_evacuated",
                "out_projected", "out_finished"])

            def unit(x, u):
                return x[:, 0:UH * keys[u][1]].rearrange("p (r k) -> p r k", r=UH)

            def per_query(x, u):
                return x[:, u, :].unsqueeze(2).broadcast_to([P, UH, keys[u][1]])

            def pipelined(eng, sample):
                for run in range(RUNS):
                    sample(run * N, run - 1 if run else None, run, run)
                    with eng.Fori(0, N - 2) as j:
                        sample(j + (run * N + 1), run, run, run)
                    sample(run * N + (N - 1), run, run, run + 1 if run + 1 < RUNS else None)

            LAST = RUNS * N - 1
            with nc.Block() as block:
                @block.sync
                def _(sp):
                    if "sync" in cfg:
                        cfg["sync"](sp)
                    sp.sem_inc(s_vp, 1)
                    for run in range(RUNS):
                        with sp.Fori(0, N) as n:
                            sp.wait_ge(s_vp, n + (run * N + 1))
                            sp.dma_start(XB[:, :, :], XT[:, :, ds((n + cfg["first"](run)) * SLOT, SEQ)]
                                         ).then_inc(s_xb, 16)

                @block.tensor
                def _(pe):
                    def project_qk(g, run):
                        pe.wait_ge(s_xb, g * 16 + 16)
                        for w in range(2):
                            for m in range(2):
                                for c, n in CH:
                                    mm = nc.tensor.matmul(bank[4 + w][0:HC, m * SEQ:(m + 1) * SEQ],
                                                          cfg["w"][run][w][0:n, c, m * HC:(m + 1) * HC], XB[0:n, c, :],
                                                          start=(m == 0 and c == 0), stop=(c == 1),
                                                          skip_group_check=True)
                        mm.then_inc(s_qkp, 1)

                    def project_v(run):
                        order = sorted(range(2), key=lambda i: -kv[i][1])
                        for x, i in enumerate(order):
                            t0, n_t = kv[i]
                            for c, n in CH:
                                mm = nc.tensor.matmul(bank[6][0:n_t, i * C:(i + 1) * C], XB[0:n, c, t0:t0 + n_t],
                                                      cfg["w"][run][2][0:n, c, :], start=(x == 0 and c == 0),
                                                      stop=(c == 1), skip_group_check=True)
                        mm.then_inc(s_vp, 1)

                    def weights_of(run):
                        cfg["ready"](pe, run)

                    def transpose(g, u):
                        for i, w0, nk, row in t_of[u]:
                            if i >= 2:
                                pe.wait_ge(s_pt, g * nt + (i - 1))
                            pe.wait_ge(s_nrm, g * ns + (u + 1))
                            for x in range(UH):
                                k0 = x * keys[u][1] + w0
                                tr = nc.tensor.transpose(bank[i % 2][0:nk, x * P:(x + 1) * P], W[:, u, k0:k0 + nk],
                                                         ident[:, :])
                            tr.then_inc(s_tr, 1)

                    def scores(g, u):
                        k0, nk = keys[u]
                        if u >= 4:
                            pe.wait_ge(s_sub, g * ns + (u - 3))
                        dst = bank[s_ring[u % 4]]
                        if masks:
                            nc.tensor.matmul(dst[:, 0:UH * nk], identb[:, :],
                                             masks[u][:, 0:nk].unsqueeze(1).broadcast_to([P, UH, nk]),
                                             start=True, stop=False, skip_group_check=True)
                        if u < UNITS - 1:
                            c, r0 = UH * u // NR, UH * u % NR
                            mm = nc.tensor.matmul(dst[:, 0:UH * nk], Q[:, c, 0:P], KH[:, r0:r0 + UH, c, k0:k0 + nk],
                                                  start=not masks, stop=True, skip_group_check=True)
                        else:
                            for h in range(NH):
                                x, r = h // 4, h % 4
                                mm = nc.tensor.matmul(dst[HP * r:HP * r + HP, x * nk:(x + 1) * nk],
                                                      Q[:, h // NR, TAIL:SEQ], KH[:, h % NR, h // NR, k0:k0 + nk],
                                                      start=(x == 0 and not masks), stop=True,
                                                      tile_position=(0, HP * r), skip_group_check=True)
                        mm.then_inc(s_sc, 1)

                    def attend(g):
                        pe.wait_ge(s_pt, (g + 1) * nt)
                        pe.wait_ge(s_v, g * 2 + 2)
                        pe.wait_ge(s_fin, (g + 1) * ng)
                        for b in range(HB):
                            for y, (k0, nk, q0, nq, row) in enumerate(cfg["ksegs"]):
                                for r in range(4):
                                    mm = nc.tensor.matmul(
                                        bank[7][HP * r:HP * r + HP, b * SEQ + q0:b * SEQ + q0 + nq],
                                        V[0:nk, kv.index((k0, nk)), 4 * b + r, :], PT[0:nk, row, 4 * b + r, q0:q0 + nq],
                                        start=(b == 0 and y == 0), stop=(y == len(cfg["ksegs"]) - 1),
                                        tile_position=(0, HP * r), skip_group_check=True)
                        mm.then_inc(s_pv, 1)

                    def out_project(g, run):
                        pe.wait_ge(s_os, g + 1)
                        for x, (col, m0, rows_m) in enumerate(cfg["out_tiles"]):
                            for b in range(HB):
                                mm = nc.tensor.matmul(bank[7][0:rows_m, col:col + SEQ],
                                                      cfg["w"][run][3][:, b, m0:m0 + rows_m], O[:, b, :],
                                                      start=(x == 0 and b == 0), stop=(b == HB - 1),
                                                      skip_group_check=True)
                        mm.then_inc(s_out, 1)

                    def sample(g, prev, k, following):
                        pe.wait_ge(s_qk, g * nqk + nqk)
                        if prev is not None:
                            pe.wait_ge(s_sub, g * ns)
                        for u in range(UNITS):
                            if prev is not None:
                                transpose(g - 1, u)
                            scores(g, u)
                        if prev is not None:
                            attend(g - 1)
                        if following is not None:
                            if following != k:
                                weights_of(following)
                            pe.wait_ge(s_sub, g * ns + (ns - 2))
                            project_qk(g + 1, following)
                            pe.wait_ge(s_v, g * 2 + 2)
                            project_v(following)
                        if prev is not None:
                            out_project(g - 1, prev)

                    pe.wait_ge(s_set, 2)
                    weights_of(0)
                    project_qk(0, 0)
                    project_v(0)
                    pipelined(pe, sample)
                    for u in range(UNITS):
                        transpose(LAST, u)
                    attend(LAST)
                    out_project(LAST, RUNS - 1)

                @block.scalar
                def _(act):
                    def evacuate_qk(g):
                        act.wait_ge(s_qkp, g + 1)
                        nc.scalar.copy(Q[:, :, :], bank[4][0:HC, 0:2 * SEQ]).then_inc(s_qk, 1)
                        for r in range(NR):
                            nc.scalar.activation(KH[:, r, :, :], bank[5][0:HC, 0:2 * SEQ], ACT.Identity,
                                                 scale=vecs[0:HC, V_HEAD + r:V_HEAD + r + 1]).then_inc(s_qk, 1)

                    def evacuate_v(g):
                        act.wait_ge(s_vp, g + 2)
                        for i, (t0, n_t) in enumerate(kv):
                            nc.scalar.copy(V[0:n_t, i, :, 0:HD],
                                           bank[6][0:n_t, i * C:(i + 1) * C].rearrange("p (h d) -> p h d", h=NH)
                                           ).then_inc(s_v, 1)

                    def evacuate_weights(g, u):
                        for i, w0, nk, row in t_of[u]:
                            act.wait_ge(s_tr, g * nt + (i + 1))
                            if u < UNITS - 1:
                                dst = PT[0:nk, row, UH * u:UH * (u + 1), 0:P]
                                src = bank[i % 2][0:nk, 0:UH * P].rearrange("p (r q) -> p r q", r=UH)
                            else:
                                dst = PT[0:nk, row, :, P:SEQ]
                                src = bank[i % 2][0:nk, 0:NH * HP].rearrange("p (r q) -> p r q", r=NH)[:, :, P - TAIL:HP]
                            nc.scalar.copy(dst, src).then_inc(s_pt, 1)

                    def evacuate_attended(g):
                        act.wait_ge(s_pv, g + 1)
                        nc.scalar.copy(O[:, :, :], bank[7][:, 0:HB * SEQ]).then_inc(s_os, 1)

                    def sample(g, prev, k, following):
                        for u in range(UNITS + 1):
                            if prev is not None and u < UNITS:
                                evacuate_weights(g - 1, u)
                            if u == UNITS - 1:
                                if prev is not None:
                                    evacuate_attended(g - 1)
                                evacuate_v(g)
                            if u:
                                act.wait_ge(s_sub, g * ns + u)
                                x = unit(W[:, u - 1, :], u - 1)
                                nc.scalar.activation(x, x, ACT.Exp, scale=scale).then_inc(s_ex, 1)
                        if following is not None:
                            evacuate_qk(g + 1)

                    act.wait_ge(s_set, 2)
                    evacuate_qk(0)
                    pipelined(act, sample)
                    for u in range(UNITS):
                        evacuate_weights(LAST, u)
                    evacuate_attended(LAST)

                @block.vector
                def _(dve):
                    nc.vector.memset(V[:, :, :, :], 0.0).then_inc(s_set, 1)
                    dve.wait_ge(s_set, 1)
                    dve.sem_inc(s_set, 1)
                    dve.sem_inc(s_fin, ng)

                    def sample(g, prev, k, following):
                        def shift(u):
                            dve.wait_ge(s_mx, g * ns + (u + 1))
                            nc.vector.tensor_tensor(unit(W[:, u, :], u), unit(bank[s_ring[u % 4]], u), per_query(MX, u),
                                                    ALU.subtract).then_inc(s_sub, 1)

                        def reciprocal(u):
                            dve.wait_ge(s_sm, g * ns + (u + 1))
                            nc.vector.reciprocal(RS[:, u, :], SM[:, u, :]).then_inc(s_rc, 1)

                        for u in range(ns):
                            dve.wait_ge(s_sc, g * ns + (u + 1))
                            nc.vector.tensor_reduce(MX[:, u, :], unit(bank[s_ring[u % 4]], u), AX.X, ALU.max
                                                    ).then_inc(s_mx, 1)
                            shift(u)
                        for u in range(ns):
                            dve.wait_ge(s_ex, g * ns + (u + 1))
                            nc.vector.tensor_reduce(SM[:, u, :], unit(W[:, u, :], u), AX.X, ALU.add
                                                    ).then_inc(s_sm, 1)
                            reciprocal(u)
                        if prev is not None:
                            dve.wait_ge(s_out, g)
                            cfg["finish"](g - 1, prev, bank[7], s_fin)

                    pipelined(dve, sample)
                    dve.wait_ge(s_out, LAST + 1)
                    cfg["finish"](LAST, RUNS - 1, bank[7], s_fin)

                @block.gpsimd
                def _(pool):
                    def sample(g, prev, k, following):
                        for u in range(ns):
                            pool.wait_ge(s_rc, g * ns + (u + 1))
                            x = unit(W[:, u, :], u)
                            nc.gpsimd.tensor_tensor(x, x, per_query(RS, u), ALU.mult).then_inc(s_nrm, 1)

                    if "gpsimd" in cfg:
                        cfg["gpsimd"](pool)
                    pipelined(pool, sample)

        with ExitStack() as ph:
            def psb(name, shape, dt=F32):
                return ph.enter_context(nc.sbuf_tensor(name, shape, dt))

            fq, fk, fv, fp = f_wq, f_wk, f_wv, f_wp
            fps = psb("f_wps", [P, HB, C])
            s_fs, = phase_sem(["elastic_weights"])
            FPS_PARTS = ((0, 0, P, ((0, 64, 2), (64, 96, 1), (96, C, 0))), (1, 0, 64, ((0, 96, 1), (96, C, 0))),
                         (1, 64, P, ((0, C, 0),)), (2, 0, P, ((0, C, 0),)))

            def scale_f(pool):
                n = 0
                for b, lo, hi, parts in FPS_PARTS:
                    for c0, c1, k in parts:
                        n += 1
                        nc.gpsimd.tensor_scalar(fps[lo:hi, b, c0:c1], fp[lo:hi, b, c0:c1], gs[lo:hi, k:k + 1], None,
                                                ALU.mult).then_inc(s_fs, 1)
                        pool.wait_ge(s_fs, n)

            def ready_f(pe, run):
                if run == 0:
                    pe.wait_ge(w_early, 7 * 16)
                else:
                    pe.wait_ge(s_fs, sum(len(x[3]) for x in FPS_PARTS))

            def finish_f(g, run, psum, s_fin):
                for c, rows_c in CH:
                    bias = vecs[0:rows_c, V_BPL + c:V_BPL + c + 1] if run == 0 else bps[0:rows_c, c:c + 1]
                    nc.vector.tensor_scalar(AT[0:rows_c, c, ds(g * SLOT, SEQ)],
                                            psum[0:rows_c, c * SEQ:(c + 1) * SEQ], bias, None, ALU.add
                                            ).then_inc(s_fin, 1)

            heads_attention(ph, {
                "name": "f", "runs": 2, "count": B // 2, "w": [(fq, fk, fv, fp), (fq, fk, fv, fps)],
                "gpsimd": scale_f, "ready": ready_f, "first": lambda run: run * (B // 2),
                "finish": finish_f, "finish_ops": 2, "out_tiles": ((0, 0, P), (SEQ, P, C1)),
                "kv": list(QA_SEGS), "pt_rows": 2, "keys": [(0, SEQ)] * UNITS,
                "parts": [[(k0, nk, row) for row, (k0, nk) in enumerate(QA_SEGS)]] * UNITS,
                "ksegs": [(k0, nk, 0, SEQ, s) for s, (k0, nk) in enumerate(QA_SEGS)],
            })

        end_phase()

        early.close()

        def add_to_xn(i, psum, dve, s):
            x = XN[:, ds(i, 1), :]
            nc.vector.tensor_tensor(x, psum, x, ALU.add).then_inc(s, 1)

        late = ctx.enter_context(ExitStack())

        def lsb(stack, name, shape):
            return stack.enter_context(nc.sbuf_tensor(name, shape, F32))

        gu_w = lsb(late, "e_guw", [P, EXPERTS, HB, 2 * C])
        ew = [tuple(lsb(late, f"e_w{x}{e}", [P, 2, C]) for x in "qkv") for e in range(EXPERTS)]
        fold = ctx.enter_context(ExitStack())
        eo = lsb(fold, "e_o", [P, EXPERTS, 2 * HB * P])
        eg = lsb(fold, "e_g", [P, EXPERTS, 2 * 2 * C])
        mlp = ctx.enter_context(ExitStack())
        m_w1, m_w2 = lsb(mlp, "m_w1", [P, 2, HID]), lsb(mlp, "m_w2", [P, HM, C])
        m_w2a, m_w2b, m_w2c = (lsb(mlp, f"m_w2{x}", [P, HM, n]) for x, n in (("a", C), ("b", 96), ("c", 64)))
        s_wm = sem("elastic_mlp_weights")

        def load_late(sp):
            sp.dma_start(m_w1[:, :, :], d["f_w1"]).then_inc(w_ffn, 16)
            sp.dma_start(m_w2[:, :, :], d["f_w2"]).then_inc(w_ffn, 16)
            sp.dma_start(eo[:, :, :], d["e_o"].rearrange("e p c n -> p e (c n)")).then_inc(w_fold, 16)
            sp.dma_start(eg[:, :, :], d["e_gu"].rearrange("e p c n -> p e (c n)")).then_inc(w_fold, 16)
            for e in range(EXPERTS):
                for dst, src in zip(ew[e], ("e_q", "e_k", "e_v")):
                    sp.dma_start(dst[:, :, :], d[src][e]).then_inc(w_exp, 16)

        def scale_mlp(pool):
            pool.wait_ge(w_ffn, 32)
            for k, (w, n) in enumerate(((m_w2a, C), (m_w2b, 96), (m_w2c, 64))):
                nc.gpsimd.tensor_scalar(w[:, :, :], m_w2[:, :, 0:n], vecs[:, V_GUM + k:V_GUM + k + 1], None, ALU.mult
                                        ).then_inc(s_wm, 1)

        residual_norm(XN, add_to_xn, False, False, (V_N2L, V_N2S), {"sync": load_late, "gpsimd_after": scale_mlp})
        if stop == 3:
            return H

        GT_ = 3 * P

        def feed_forward(tag, w1, w2s, hid, ready, b1, groups, k_rows, finish, store=None):
            nv = len(k_rows)
            units = nv * HM
            g0, g1 = groups
            (s_up, s_gl, s_dn, s_fn, s_x, s_store) = phase_sem([
                f"{tag}_hidden", f"{tag}_gelu", f"{tag}_down", f"{tag}_finished", f"{tag}_partial", f"{tag}_stored"])
            with nc.Block() as block:
                @block.tensor
                def _(pe):
                    for s_w, n_w in ready:
                        pe.wait_ge(s_w, n_w)
                    with pe.Fori(0, g1 - g0) as g:
                        for m in range(HM):
                            for v, rows_k in enumerate(k_rows):
                                u = m * nv + v
                                if v == 0:
                                    pe.wait_ge(s_gl, g * units + u + nv)
                                chunks = [(c, min(P, rows_k - c * P)) for c in range(2) if rows_k > c * P]
                                for x, (c, n) in enumerate(chunks):
                                    mm = nc.tensor.matmul(bank[u % 6][:, 0:GT_], w1[0:n, c, m * P:(m + 1) * P],
                                                          XT[0:n, c, ds((g + g0) * GT_, GT_)], start=(x == 0),
                                                          stop=(x == len(chunks) - 1))
                                mm.then_inc(s_up, 1)
                        pe.wait_ge(s_gl, (g + 1) * units + 6)
                        for j in range(3):
                            pe.wait_ge(s_fn, g * 3 + (1 if j < 2 else 2))
                            for m in range(HM):
                                for v, w in enumerate(w2s):
                                    n = w.shape[2]
                                    mm = nc.tensor.matmul(bank[6 + j % 2][:, 0:n], hid[:, m * nv + v, j * P:(j + 1) * P],
                                                          w[:, m, :], start=(m == 0 and v == 0),
                                                          stop=(m == HM - 1), skip_group_check=True)
                            mm.then_inc(s_dn, 1)

                @block.scalar
                def _(act):
                    act.sem_inc(s_gl, 6)
                    with act.Fori(0, g1 - g0) as g:
                        for m in range(HM):
                            for v in range(nv):
                                u = m * nv + v
                                act.wait_ge(s_up, g * units + u + 1)
                                nc.scalar.activation(hid[:, u, :], bank[u % 6][:, 0:GT_], ACT.Gelu,
                                                     bias=vecs[:, b1 + m:b1 + m + 1]).then_inc(s_gl, 1)

                @block.vector
                def _(dve):
                    dve.sem_inc(s_fn, 1)
                    with dve.Fori(0, g1 - g0) as g:
                        for j in range(3):
                            dve.wait_ge(s_dn, g * 3 + j + 1)
                            finish(dve, (g + g0) * 3 + j, g * 3 + j, bank[6 + j % 2][:, 0:C], s_x, s_fn)

                if store:
                    @block.sync
                    def _(sp):
                        with sp.Fori(0, g1 - g0) as g:
                            sp.wait_ge(s_fn, g * 3 + 4)
                            sp.dma_start(out.rearrange("(t p) n -> p t n", p=P)[:, ds((g + g0) * 3, 3), :],
                                         H[:, ds((g + g0) * 3, 3), :]).then_inc(s_store, 16)
                        sp.wait_ge(s_store, 16 * (g1 - g0))

        with ExitStack() as ph:
            def psb(name, shape, dt=F32):
                return ph.enter_context(nc.sbuf_tensor(name, shape, dt))

            hid = psb("m_hid", [P, 3 * HM, GT_])
            part = psb("m_part", [P, C])

            def finish_m(row):
                def finish(dve, tile, count, psum, s_x, s_fn):
                    h = H[:, ds(tile, 1), :].rearrange("p t n -> p (t n)")
                    x = XN[:, ds(tile, 1), :].rearrange("p t n -> p (t n)")
                    nc.vector.tensor_tensor(part[:, :], psum, x, ALU.add).then_inc(s_x, 1)
                    dve.wait_ge(s_x, count * 3 + 1)
                    nc.vector.tensor_tensor(part[:, :], part[:, :], rows[:, row, :], ALU.add).then_inc(s_x, 1)
                    dve.wait_ge(s_x, count * 3 + 2)
                    nc.vector.tensor_tensor(h, part[:, :], h, ALU.add).then_inc(s_x, 1)
                    dve.wait_ge(s_x, count * 3 + 3)
                    dve.sem_inc(s_fn, 1)
                return finish

            feed_forward("wide", m_w1, (m_w2,), hid, ((w_ffn, 32),), V_B1, (0, 3), (C,), finish_m(B2L))
            feed_forward("elastic", m_w1, (m_w2a, m_w2b, m_w2c), hid, ((s_wm, 3),), V_B1, (3, 6), (C, 96, 64),
                         finish_m(B2S))

        end_phase()
        mlp.close()

        s_f, s_c = phase_sem(["folded", "fold_evacuated"])

        def fold_products(pe):
            pe.wait_ge(w_fold, 32)
            for e in range(EXPERTS):
                for b in range(HB):
                    u = e * HB + b
                    if u >= 2:
                        pe.wait_ge(s_c, u - 1)
                    for c, n in CH:
                        mm = nc.tensor.matmul(bank[6 + u % 2][:, 0:2 * C],
                                              eo[0:n, e, c * HB * P + b * P:c * HB * P + (b + 1) * P],
                                              eg[0:n, e, c * 2 * C:(c + 1) * 2 * C],
                                              start=(c == 0), stop=(c == 1))
                    mm.then_inc(s_f, 1)

        def fold_evacuate(act):
            for u in range(EXPERTS * HB):
                act.wait_ge(s_f, u + 1)
                nc.scalar.copy(gu_w[:, u // HB, u % HB, :], bank[6 + u % 2][:, 0:2 * C]).then_inc(s_c, 1)

        residual_norm(H, None, False, False, None, {"tensor": fold_products, "scalar": fold_evacuate})
        fold.close()
        if stop == 4:
            return H

        g_w1, g_w2 = lsb(late, "l_w1", [P, 2, HID]), lsb(late, "l_w2", [P, HM, C])
        with ExitStack() as ph:
            def psb(name, shape, dt=F32):
                return ph.enter_context(nc.sbuf_tensor(name, shape, dt))

            GU = psb("e_GU", [P, HB, NTOK])
            KT, NKT = P - (WIN - 1), SEQ - P + WIN - 1
            mka, mkb = psb("e_mka", [P, P], BF16), psb("e_mkb", [P, NKT], BF16)
            s_m, = phase_sem(["masks"])
            with nc.Block() as block:
                @block.vector
                def _(dve):
                    nc.vector.memset(GU[:, :, :], 0.0)

                @block.gpsimd
                def _(pool):
                    n = 0
                    for mk, nf, spans in ((mka, P, [(0, P, 0)]),
                                          (mkb, NKT, [(HP * r, HP * (r + 1), TAIL - KT) for r in range(4)])):
                        n += 1
                        nc.gpsimd.memset(mk[:, :], 0.0).then_inc(s_m, 1)
                        for lo, hi, base in spans:
                            for b_, c_ in ((base, 1), (WIN - 1 - base, -1)):
                                pool.wait_ge(s_m, n)
                                n += 1
                                nc.gpsimd.affine_select(out=mk[lo:hi, :], in_=mk[lo:hi, :], compare_op=ALU.is_ge,
                                                        fill=NEG, base=b_, pattern=[[-c_, nf]], channel_multiplier=c_
                                                        ).then_inc(s_m, 1)
                        pool.wait_ge(s_m, n)

            def load_last(sp):
                sp.dma_start(g_w1[:, :, :], d["g_w1"]).then_inc(w_last, 16)
                sp.dma_start(g_w2[:, :, :], d["g_w2"]).then_inc(w_last, 16)

            def finish_e(g, run, psum, s_fin):
                gu = GU[:, :, ds((g - run * B) * SLOT, SEQ)]
                nc.vector.tensor_tensor(gu, psum[:, 0:HB * SEQ].rearrange("p (b q) -> p b q", b=HB), gu, ALU.add
                                        ).then_inc(s_fin, 1)

            heads_attention(ph, {
                "name": "e", "runs": EXPERTS, "count": B, "w": [(*ew[e], gu_w[:, e, :, :]) for e in range(EXPERTS)],
                "sync": load_last, "ready": lambda pe, run: pe.wait_ge(w_exp, 3 * 16 * EXPERTS),
                "first": lambda run: 0,
                "finish": finish_e, "finish_ops": 1, "out_tiles": tuple((b * SEQ, b * P, P) for b in range(HB)),
                "kv": [(0, P), (KT, NKT)], "pt_rows": 1, "masks": [mka] * (UNITS - 1) + [mkb],
                "keys": [(0, P)] * (UNITS - 1) + [(KT, NKT)], "parts": [[(0, P, 0)]] * (UNITS - 1) + [[(0, NKT, 0)]],
                "ksegs": [(0, P, 0, P, 0), (KT, NKT, P, SEQ - P, 0)],
            })

            PARTS = 3
            part_n = NTOK // PARTS
            s_sl, = phase_sem(["silu"])
            with nc.Block() as block:
                @block.scalar
                def _(act):
                    for g in range(PARTS):
                        cols = slice(g * part_n, (g + 1) * part_n)
                        nc.scalar.activation(AT[:, 0, cols], GU[:, 0, cols], ACT.Silu).then_inc(s_sl, 1)
                        nc.scalar.activation(AT[C1:P, 1, cols], GU[0:C1, 1, cols], ACT.Silu).then_inc(s_sl, 1)

                @block.vector
                def _(dve):
                    for g in range(PARTS):
                        cols = slice(g * part_n, (g + 1) * part_n)
                        dve.wait_ge(s_sl, g * 2 + 1)
                        nc.vector.tensor_tensor(AT[:, 0, cols], AT[:, 0, cols], GU[:, 2, cols], ALU.mult)
                        dve.wait_ge(s_sl, g * 2 + 2)
                        nc.vector.tensor_tensor(AT[0:C1, 1, cols], AT[C1:P, 1, cols], GU[C1:P, 1, cols], ALU.mult)

        end_phase()
        residual_norm(H, add_to_h, False, False, None)
        if stop == 5:
            return H

        with ExitStack() as ph:
            def psb(name, shape, dt=F32):
                return ph.enter_context(nc.sbuf_tensor(name, shape, dt))

            hid = psb("l_hid", [P, HM, GT_])

            def finish_l(dve, tile, count, psum, s_x, s_fn):
                h = H[:, ds(tile, 1), :].rearrange("p t n -> p (t n)")
                nc.vector.tensor_tensor(h, psum, h, ALU.add).then_inc(s_fn, 1)

            feed_forward("last", g_w1, (g_w2,), hid, ((w_last, 32),), V_FB, (0, 6), (C,), finish_l, store=True)
        end_phase()
        return H


def kernel(**inputs):
    import numpy as np
    import concourse.bacc as bacc
    from concourse.bass_utils import run_bass_kernel_spmd

    arrays = lay_out(**inputs)
    nc = bacc.Bacc("TRN2", target_bir_lowering=False, num_devices=1)
    d = {n: nc.dram_tensor(f"in_{n}_dram", a.shape, mybir.dt.from_np(a.dtype), kind="ExternalInput").ap()
         for n, a in arrays.items()}
    out = nc.dram_tensor("out_0_dram", (NTOK, C), F32, kind="ExternalOutput").ap()
    fusion_kernel(nc, d, out)
    r = run_bass_kernel_spmd(nc, [{f"in_{n}_dram": a for n, a in arrays.items()}], core_ids=[0])
    got = np.asarray(r.results[0]["out_0_dram"])
    return np.ascontiguousarray(got.reshape(B, SLOT, C)[:, :SEQ])


def lay_out(**inputs):
    import numpy as np

    a = {k: np.asarray(v) for k, v in inputs.items()}

    def chunks(w):
        o = np.zeros((2, P, w.shape[1]), np.float32)
        o[0], o[1, :C1] = w[:P], w[P:]
        return np.ascontiguousarray(o.transpose(1, 0, 2))

    def heads_out(w):
        o = np.zeros((w.shape[0], NH, HP), np.float32)
        o[:, :, :HD] = w.reshape(-1, NH, HD)
        return o.reshape(-1, NH * HP)

    def heads_in(w):
        return np.ascontiguousarray(heads_out(w.T).T.reshape(HB, P, -1).transpose(1, 0, 2))

    def blocks(w):
        return np.ascontiguousarray(w.reshape(-1, P, w.shape[1]).transpose(1, 0, 2))

    def cols(v):
        o = np.zeros(-(-v.size // P) * P, np.float32)
        o[:v.size] = v.ravel()
        return o.reshape(-1, P).T

    x = a["x"].reshape(B, 3, 8, 16, 8, 16).transpose(0, 2, 4, 3, 5, 1).reshape(B * NPATCH, PD)
    h0 = np.zeros((B, SLOT, C), np.float32)
    h0[:, NPATCH:SEQ] = a["txt"]
    bqkv = a["L0_attn_b_qkv"]
    head = (np.arange(P)[:, None] // HD == np.arange(NR)).astype(np.float32)
    f = "L0_ffn_"
    vecs = [cols(a["L0_tok_ln1_g"]), cols(a["L0_tok_ln1_b"]), cols(bqkv[:C]), cols(bqkv[C:2 * C]),
            cols(a["L0_attn_b_proj"])]
    for n in ("n1l", "n1s", "n2l", "n2s"):
        vecs += [cols(a[f + n + "_g"]), cols(a[f + n + "_b"])]
    vecs += [cols(a[f + "b_proj"]), cols(a[f + "b_fc1"]), cols(a["L1_ffn_in_bias"]),
             np.repeat(a[f + "gumbel_weights"][None], P, 0), np.repeat(a["L0_attn_alpha"][None], P, 0),
             head]
    vecs = np.concatenate(vecs, 1)
    vecs = np.concatenate([vecs, np.zeros((P, 64 - vecs.shape[1]), np.float32)], 1)
    rows = np.stack([a["L0_tok_ln2_g"], a["L0_tok_ln2_b"], bqkv[2 * C:], a[f + "b_fc2"], a[f + "b_fc2"]])
    r = {
        "patches": x, "h0": h0.reshape(NTOK, C), "tok_w": a["L0_tok_W_proj"], "vecs": vecs,
        "rows": np.repeat(rows[None], P, 0),
        "a0_qkv": chunks(a["L0_attn_W_qkv"]), "a0_proj": chunks(a["L0_attn_W_proj"]), "a0_gp": chunks(a["L0_attn_W_gp"]),
        "f_q": chunks(a[f + "w_qkv"][:, :C]), "f_k": chunks(a[f + "w_qkv"][:, C:2 * C]),
        "f_v": chunks(a[f + "w_qkv"][:, 2 * C:]), "f_proj": heads_in(a[f + "w_proj"]),
        "f_w1": chunks(a[f + "w_fc1"]), "f_w2": blocks(a[f + "w_fc2"]),
        "g_w1": chunks(a["L1_ffn_in_weight"].T), "g_w2": blocks(a["L1_ffn_out_weight"]),
        "e_q": np.stack([chunks(w.T) for w in a["L1_attn_wq"]]),
        "e_k": np.stack([chunks(w.T) for w in a["L1_attn_wk"]]),
        "e_v": np.stack([chunks(w.T) for w in a["L1_attn_wv"]]),
        "e_o": np.stack([chunks(heads_out(w)) for w in a["L1_attn_wo"]]),
        "e_gu": np.stack([chunks(np.concatenate([a["L1_attn_w_gate"][:, cols_e], a["L1_attn_w_up"][P:, cols_e],
                                                 a["L1_attn_w_up"][:P, cols_e]], 0).T)
                          for cols_e in (slice(e * C, (e + 1) * C) for e in range(EXPERTS))]),
    }
    return {k: np.ascontiguousarray(v) for k, v in r.items()}
```
